# Optimizing a Trainium2 kernel written in Bass

```python
import numpy as np
import jax
import jax.numpy as jnp

def _softmax(x, axis=-1):
    return jax.nn.softmax(x, axis=axis)

def _gelu(x):
    return jax.nn.gelu(x, approximate=True)

def _silu(x):
    return jax.nn.silu(x)

def _sigmoid(x):
    return jax.nn.sigmoid(x)

def _layernorm(x, axis=-1, eps=1e-05):
    m = jnp.mean(x, axis=axis, keepdims=True)
    v = jnp.var(x, axis=axis, keepdims=True)
    return (x - m) / jnp.sqrt(v + eps)

def _scatter_add(tgt, idx, src, axis=0):
    return tgt.at[idx].add(src)

def _segment_sum(src, seg, n):
    return jax.ops.segment_sum(src, seg, n)
kernel_name = 'mk_decoder_preln_d1_seqx_r8_916a0b'

def setup_inputs(seed: int=0):
    np.random.seed(seed)
    _w = jnp.asarray

    def _rec_inputs():
        import jax
        import jax.numpy as jnp
        _rk = jax.random.key(seed)
        x = 0.5 + 0.2887 * jax.random.normal(jax.random.fold_in(_rk, 1), (4, 256, 256), jnp.float32)
        _lenS = 256 - jax.random.randint(jax.random.fold_in(_rk, 7), (4,), 0, max(1, 256 // 4) + 1, jnp.int32)
        _lenS2 = 256 - jax.random.randint(jax.random.fold_in(_rk, 8), (4,), 0, max(1, 256 // 4) + 1, jnp.int32)
        _ctx_512P = jax.random.normal(jax.random.fold_in(_rk, 11), (4, 16, 64), jnp.float32)
        _ctx_512c = jax.random.dirichlet(jax.random.fold_in(_rk, 511), 0.3 * jnp.ones((16,), jnp.float32), (4, 256))
        _ctx_512t = jnp.einsum('bsk,bkd->bsd', _ctx_512c, _ctx_512P)
        _ctx_512t = _ctx_512t * jax.lax.rsqrt(jnp.mean(jnp.square(_ctx_512t)) + 1e-12) * 0.953939
        ctx_512 = 7.22013e-05 + 1.00017 * (_ctx_512t + 0.3 * jax.random.normal(jax.random.fold_in(_rk, 611), (4, 256, 64), jnp.float32))
        return (x, ctx_512)
    x, ctx_512 = _rec_inputs()

    def _L0_attn_setup():
        import jax, jax.numpy as jnp
        import numpy as np
        D_MODEL = 256
        D_INNER = 256
        N_QK = 32
        N_V = 32
        D_STATE = 64
        D_CONV = 4
        CHUNK = 128
        CONV_DIM = D_INNER + 2 * N_QK * D_STATE
        IN_OUT = 2 * D_INNER + 2 * N_QK * D_STATE + N_V

        def causal_depthwise_conv(x, w, b):
            B, L, C = x.shape
            K = w.shape[1]
            xp = jnp.pad(x, ((0, 0), (K - 1, 0), (0, 0)))
            y = b[None, None, :]
            for k in range(K):
                y = y + xp[:, k:k + L, :] * w[None, None, :, k]
            return y

        def ssd_chunk_scan(x, dt, B, C, chunk):
            b, l, h, p = x.shape
            n = B.shape[-1]
            nc = l // chunk
            x = x.reshape(b, nc, chunk, h, p)
            dt = dt.reshape(b, nc, chunk, h)
            B = B.reshape(b, nc, chunk, h, n)
            C = C.reshape(b, nc, chunk, h, n)
            a = -dt
            cum = jnp.cumsum(a, axis=2)
            xdt = x * dt[..., None]
            CB = jnp.einsum('bcqhn,bckhn->bchqk', C, B)
            cumT = jnp.swapaxes(cum, 2, 3)
            diff = cumT[..., :, None] - cumT[..., None, :]
            mask = jnp.tril(jnp.ones((chunk, chunk), dtype=bool))
            decay = jnp.exp(jnp.where(mask, diff, -jnp.inf))
            y_intra = jnp.einsum('bchqk,bckhp->bcqhp', CB * decay, xdt)
            state_decay = jnp.exp(cum[:, :, -1:, :] - cum)
            states = jnp.einsum('bckhn,bckhp->bchpn', B * state_decay[..., None], xdt)
            chunk_decay = jnp.exp(cum[:, :, -1, :])

            def step(carry, inp):
                st, cd = inp
                new = carry * cd[:, :, None, None] + st
                return (new, carry)
            init = jnp.zeros((b, h, p, n), dtype=x.dtype)
            _, prev = jax.lax.scan(step, init, (jnp.moveaxis(states, 1, 0), jnp.moveaxis(chunk_decay, 1, 0)))
            prev = jnp.moveaxis(prev, 0, 1)
            y_inter = jnp.einsum('bcqhn,bchpn->bcqhp', C * jnp.exp(cum)[..., None], prev)
            return (y_intra + y_inter).reshape(b, l, h, p)
        key = jax.random.key(seed)
        ks = jax.random.split(key, 6)
        u = jax.random.normal(ks[0], (2, 512, D_MODEL), dtype=jnp.float32)
        W_in = jax.random.normal(ks[1], (IN_OUT, D_MODEL), dtype=jnp.float32) * 0.02
        conv_w = jax.random.normal(ks[2], (CONV_DIM, D_CONV), dtype=jnp.float32) * 0.2
        conv_b = jax.random.normal(ks[3], (CONV_DIM,), dtype=jnp.float32) * 0.02
        D = jnp.ones((N_V,), dtype=jnp.float32)
        z_bias = jnp.zeros((D_INNER,), dtype=jnp.float32)
        W_out = jax.random.normal(ks[4], (D_MODEL, D_INNER), dtype=jnp.float32) * 0.02
        return {'u': u, 'W_in': W_in, 'conv_w': conv_w, 'conv_b': conv_b, 'D': D, 'z_bias': z_bias, 'W_out': W_out}
    _L0_attn_all = _L0_attn_setup()
    _L0_attn_in = {k: v for k, v in _L0_attn_all.items() if k in ('W_in', 'conv_w', 'conv_b', 'D', 'z_bias', 'W_out')}
    del _L0_attn_all

    def _L0_xattn_setup():
        import jax, jax.numpy as jnp
        import numpy as np
        P_ASEM = 0.6
        key = jax.random.key(seed)
        k1, k2, k3 = jax.random.split(key, 3)
        B, N, D = (8, 256, 64)
        x = jax.random.normal(k1, (B, N, D), dtype=jnp.float32)
        adj = jax.random.uniform(k2, (B, N, N), dtype=jnp.float32)
        bound = 1.0 / np.sqrt(2 * D)
        W = jax.random.uniform(k3, (1, 2 * D), dtype=jnp.float32, minval=-bound, maxval=bound)
        b = jnp.zeros((1,), dtype=jnp.float32)
        return {'x': x, 'adj': adj, 'W': W, 'b': b}
    _L0_xattn_all = _L0_xattn_setup()
    _L0_xattn_in = {k: v for k, v in _L0_xattn_all.items() if k in ('W', 'b')}
    del _L0_xattn_all

    def _L0_ffn_setup():
        import jax, jax.numpy as jnp
        import numpy as np
        H = 256
        I = 256
        E_ROUTED = 7
        NS = 1
        TOPK = 2
        TEMP = 1.0

        def _moe_forward(x, Wr, br, gate_bias, Wup, bup, Wgate, bgate, Wdown, bdown, Wsu, bsu, Wsg, bsg, Wsd, bsd):
            B, S, _ = x.shape
            xt = x.reshape(-1, H)
            N = xt.shape[0]
            gate = (xt @ Wr + br) / TEMP
            bias_gate = gate + gate_bias
            _, ids = jax.lax.top_k(bias_gate, TOPK)
            sel_logits = jnp.take_along_axis(gate, ids, axis=-1)
            masked = jnp.full_like(gate, -jnp.inf)
            masked = masked.at[jnp.arange(N)[:, None], ids].set(sel_logits)
            probs = jax.nn.softmax(masked, axis=-1)
            u = jnp.einsum('nh,ehi->eni', xt, Wup) + bup[:, None, :]
            g = jax.nn.silu(jnp.einsum('eni,eij->enj', u, Wgate) + bgate[:, None, :]) * u
            eo = jnp.einsum('enj,ejh->enh', g, Wdown) + bdown[:, None, :]
            out = jnp.einsum('ne,enh->nh', probs, eo)
            su = (xt @ Wsu + bsu).reshape(N, NS, I)
            sg = jax.nn.silu(su @ Wsg + bsg) * su
            so = (sg @ Wsd + bsd).sum(axis=1)
            out = out + so
            return out.reshape(B, S, H)
        key = jax.random.key(seed)
        ks = jax.random.split(key, 20)
        s = lambda fan_in: 1.0 / np.sqrt(fan_in)
        inp = {'x': jax.random.normal(ks[0], (4, 128, H), dtype=jnp.float32), 'Wr': jax.random.normal(ks[1], (H, E_ROUTED), jnp.float32) * s(H), 'br': jax.random.normal(ks[2], (E_ROUTED,), jnp.float32) * s(H), 'gate_bias': jnp.zeros((E_ROUTED,), jnp.float32), 'Wup': jax.random.normal(ks[3], (E_ROUTED, H, I), jnp.float32) * s(H), 'bup': jax.random.normal(ks[4], (E_ROUTED, I), jnp.float32) * s(H), 'Wgate': jax.random.normal(ks[5], (E_ROUTED, I, I), jnp.float32) * s(I), 'bgate': jax.random.normal(ks[6], (E_ROUTED, I), jnp.float32) * s(I), 'Wdown': jax.random.normal(ks[7], (E_ROUTED, I, H), jnp.float32) * s(I), 'bdown': jax.random.normal(ks[8], (E_ROUTED, H), jnp.float32) * s(I), 'Wsu': jax.random.normal(ks[9], (H, NS * I), jnp.float32) * s(H), 'bsu': jax.random.normal(ks[10], (NS * I,), jnp.float32) * s(H), 'Wsg': jax.random.normal(ks[11], (I, I), jnp.float32) * s(I), 'bsg': jax.random.normal(ks[12], (I,), jnp.float32) * s(I), 'Wsd': jax.random.normal(ks[13], (I, H), jnp.float32) * s(I), 'bsd': jax.random.normal(ks[14], (H,), jnp.float32) * s(I)}
        return inp
    _L0_ffn_all = _L0_ffn_setup()
    _L0_ffn_in = {k: v for k, v in _L0_ffn_all.items() if k in ('Wr', 'br', 'gate_bias', 'Wup', 'bup', 'Wgate', 'bgate', 'Wdown', 'bdown', 'Wsu', 'bsu', 'Wsg', 'bsg', 'Wsd', 'bsd')}
    del _L0_ffn_all
    return {'x': x, 'ctx_512': ctx_512, 'L0_attn_W_in': _L0_attn_in['W_in'], 'L0_attn_conv_w': _L0_attn_in['conv_w'], 'L0_attn_conv_b': _L0_attn_in['conv_b'], 'L0_attn_D': _L0_attn_in['D'], 'L0_attn_z_bias': _L0_attn_in['z_bias'], 'L0_attn_W_out': _L0_attn_in['W_out'], 'L0_xattn_W': _L0_xattn_in['W'], 'L0_xattn_b': _L0_xattn_in['b'], 'L0_ffn_Wr': _L0_ffn_in['Wr'], 'L0_ffn_br': _L0_ffn_in['br'], 'L0_ffn_gate_bias': _L0_ffn_in['gate_bias'], 'L0_ffn_Wup': _L0_ffn_in['Wup'], 'L0_ffn_bup': _L0_ffn_in['bup'], 'L0_ffn_Wgate': _L0_ffn_in['Wgate'], 'L0_ffn_bgate': _L0_ffn_in['bgate'], 'L0_ffn_Wdown': _L0_ffn_in['Wdown'], 'L0_ffn_bdown': _L0_ffn_in['bdown'], 'L0_ffn_Wsu': _L0_ffn_in['Wsu'], 'L0_ffn_bsu': _L0_ffn_in['bsu'], 'L0_ffn_Wsg': _L0_ffn_in['Wsg'], 'L0_ffn_bsg': _L0_ffn_in['bsg'], 'L0_ffn_Wsd': _L0_ffn_in['Wsd'], 'L0_ffn_bsd': _L0_ffn_in['bsd']}

def reference(x, ctx_512, L0_attn_W_in, L0_attn_conv_w, L0_attn_conv_b, L0_attn_D, L0_attn_z_bias, L0_attn_W_out, L0_xattn_W, L0_xattn_b, L0_ffn_Wr, L0_ffn_br, L0_ffn_gate_bias, L0_ffn_Wup, L0_ffn_bup, L0_ffn_Wgate, L0_ffn_bgate, L0_ffn_Wdown, L0_ffn_bdown, L0_ffn_Wsu, L0_ffn_bsu, L0_ffn_Wsg, L0_ffn_bsg, L0_ffn_Wsd, L0_ffn_bsd):
    import jax
    import jax.numpy as jnp

    def _L0_attn_ref(u, W_in, conv_w, conv_b, D, z_bias, W_out):
        import jax, jax.numpy as jnp
        import numpy as np
        D_MODEL = 256
        D_INNER = 256
        N_QK = 32
        N_V = 32
        D_STATE = 64
        D_CONV = 4
        CHUNK = 128
        CONV_DIM = D_INNER + 2 * N_QK * D_STATE
        IN_OUT = 2 * D_INNER + 2 * N_QK * D_STATE + N_V

        def causal_depthwise_conv(x, w, b):
            B, L, C = x.shape
            K = w.shape[1]
            xp = jnp.pad(x, ((0, 0), (K - 1, 0), (0, 0)))
            y = b[None, None, :]
            for k in range(K):
                y = y + xp[:, k:k + L, :] * w[None, None, :, k]
            return y

        def ssd_chunk_scan(x, dt, B, C, chunk):
            b, l, h, p = x.shape
            n = B.shape[-1]
            nc = l // chunk
            x = x.reshape(b, nc, chunk, h, p)
            dt = dt.reshape(b, nc, chunk, h)
            B = B.reshape(b, nc, chunk, h, n)
            C = C.reshape(b, nc, chunk, h, n)
            a = -dt
            cum = jnp.cumsum(a, axis=2)
            xdt = x * dt[..., None]
            CB = jnp.einsum('bcqhn,bckhn->bchqk', C, B)
            cumT = jnp.swapaxes(cum, 2, 3)
            diff = cumT[..., :, None] - cumT[..., None, :]
            mask = jnp.tril(jnp.ones((chunk, chunk), dtype=bool))
            decay = jnp.exp(jnp.where(mask, diff, -jnp.inf))
            y_intra = jnp.einsum('bchqk,bckhp->bcqhp', CB * decay, xdt)
            state_decay = jnp.exp(cum[:, :, -1:, :] - cum)
            states = jnp.einsum('bckhn,bckhp->bchpn', B * state_decay[..., None], xdt)
            chunk_decay = jnp.exp(cum[:, :, -1, :])

            def step(carry, inp):
                st, cd = inp
                new = carry * cd[:, :, None, None] + st
                return (new, carry)
            init = jnp.zeros((b, h, p, n), dtype=x.dtype)
            _, prev = jax.lax.scan(step, init, (jnp.moveaxis(states, 1, 0), jnp.moveaxis(chunk_decay, 1, 0)))
            prev = jnp.moveaxis(prev, 0, 1)
            y_inter = jnp.einsum('bcqhn,bchpn->bcqhp', C * jnp.exp(cum)[..., None], prev)
            return (y_intra + y_inter).reshape(b, l, h, p)
        b, l, _ = u.shape
        xBCzA = jnp.einsum('bld,od->blo', u, W_in)
        xBC = xBCzA[..., :CONV_DIM]
        z = xBCzA[..., CONV_DIM:CONV_DIM + D_INNER]
        A_log = xBCzA[..., CONV_DIM + D_INNER:]
        xBC = causal_depthwise_conv(xBC, conv_w, conv_b)
        x = xBC[..., :D_INNER]
        Bm = xBC[..., D_INNER:D_INNER + N_QK * D_STATE]
        Cm = xBC[..., D_INNER + N_QK * D_STATE:]
        x = x.reshape(b, l, N_V, D_INNER // N_V)
        Bm = Bm.reshape(b, l, N_QK, D_STATE)
        Cm = Cm.reshape(b, l, N_QK, D_STATE)
        dt = jax.nn.softplus(A_log)
        x_scan = x / dt[..., None]
        y = ssd_chunk_scan(x_scan, dt, Bm, Cm, CHUNK)
        y = y + D[None, None, :, None] * x
        y = y.reshape(b, l, D_INNER)
        out = jnp.einsum('bli,oi->blo', y * jax.nn.silu(z + z_bias), W_out)
        return out

    def _L0_xattn_ref(x, adj, W, b):
        import jax, jax.numpy as jnp
        import numpy as np
        P_ASEM = 0.6
        D = x.shape[-1]
        Wi = W[:, :D]
        Wj = W[:, D:]
        si = jnp.einsum('bnd,d->bn', x, Wi[0])
        sj = jnp.einsum('bnd,d->bn', x, Wj[0])
        xij = jax.nn.sigmoid(si[:, :, None] + sj[:, None, :] + b[0])
        return P_ASEM * xij + (1.0 - P_ASEM) * adj

    def _L0_ffn_ref(x, Wr, br, gate_bias, Wup, bup, Wgate, bgate, Wdown, bdown, Wsu, bsu, Wsg, bsg, Wsd, bsd):
        import jax, jax.numpy as jnp
        import numpy as np
        H = 256
        I = 256
        E_ROUTED = 7
        NS = 1
        TOPK = 2
        TEMP = 1.0

        def _moe_forward(x, Wr, br, gate_bias, Wup, bup, Wgate, bgate, Wdown, bdown, Wsu, bsu, Wsg, bsg, Wsd, bsd):
            B, S, _ = x.shape
            xt = x.reshape(-1, H)
            N = xt.shape[0]
            gate = (xt @ Wr + br) / TEMP
            bias_gate = gate + gate_bias
            _, ids = jax.lax.top_k(bias_gate, TOPK)
            sel_logits = jnp.take_along_axis(gate, ids, axis=-1)
            masked = jnp.full_like(gate, -jnp.inf)
            masked = masked.at[jnp.arange(N)[:, None], ids].set(sel_logits)
            probs = jax.nn.softmax(masked, axis=-1)
            u = jnp.einsum('nh,ehi->eni', xt, Wup) + bup[:, None, :]
            g = jax.nn.silu(jnp.einsum('eni,eij->enj', u, Wgate) + bgate[:, None, :]) * u
            eo = jnp.einsum('enj,ejh->enh', g, Wdown) + bdown[:, None, :]
            out = jnp.einsum('ne,enh->nh', probs, eo)
            su = (xt @ Wsu + bsu).reshape(N, NS, I)
            sg = jax.nn.silu(su @ Wsg + bsg) * su
            so = (sg @ Wsd + bsd).sum(axis=1)
            out = out + so
            return out.reshape(B, S, H)
        return _moe_forward(x, Wr, br, gate_bias, Wup, bup, Wgate, bgate, Wdown, bdown, Wsu, bsu, Wsg, bsg, Wsd, bsd)
    x = x + _L0_attn_ref(_layernorm(x, axis=-1), L0_attn_W_in, L0_attn_conv_w, L0_attn_conv_b, L0_attn_D, L0_attn_z_bias, L0_attn_W_out)
    x = x + _L0_xattn_ref(ctx_512, _layernorm(x, axis=-1), L0_xattn_W, L0_xattn_b)
    x = x + _L0_ffn_ref(_layernorm(x, axis=-1), L0_ffn_Wr, L0_ffn_br, L0_ffn_gate_bias, L0_ffn_Wup, L0_ffn_bup, L0_ffn_Wgate, L0_ffn_bgate, L0_ffn_Wdown, L0_ffn_bdown, L0_ffn_Wsu, L0_ffn_bsu, L0_ffn_Wsg, L0_ffn_bsg, L0_ffn_Wsd, L0_ffn_bsd)
    return x

_drawn_inputs = setup_inputs


def setup_inputs(seed=0):
    import zlib

    import numpy as np

    out = dict(_drawn_inputs(seed))
    spreads = {'L0_attn_D': (1.0, 0.6), 'L0_attn_z_bias': (0.0, 0.395), 'L0_ffn_gate_bias': (0.0, 0.1)}
    factors = {'L0_attn_conv_b': 4.81}
    for name, (base, spread) in spreads.items():
        noise = np.random.default_rng([zlib.crc32(name.encode()), seed]).standard_normal(out[name].shape)
        drawn = base * np.exp(spread * noise) if base else spread * noise
        out[name] = jnp.asarray(drawn.astype(out[name].dtype))
    for name, factor in factors.items():
        out[name] = (out[name] * factor).astype(out[name].dtype)
    return out
```

```python
from contextlib import ExitStack

import concourse.bass as bass
from concourse import mybir

P = 128
F32 = mybir.dt.float32
F32R = mybir.dt.float32r
BF16 = mybir.dt.bfloat16
ALU = mybir.AluOpType
ACT = mybir.ActivationFunctionType
AX = mybir.AxisListType

NSEQ, SEQ, DM = 4, 256, 256
T = NSEQ * SEQ // P
HALF = 512
KD = DM // P
NH, HD, NS = 32, 8, 64
PAIRS = NH // 2
TAPS = 4
C_X, C_B = 0, DM
C_C = C_B + NH * NS
C_Z = C_C + NH * NS
C_A = C_Z + DM
ZA = DM + NH
NE = 8
NR = 7
TOPK = 2
EPS = 1e-5
P_SEM = 0.6
NEG = -1e30
CTX = 64


def decoder_layer(nc, x, ctx_in, W_in, conv_w, conv_b, D, z_bias, W_out, xw, xb, Wr, br, gate_bias,
                  Wup, bup, Wgate, bgate, Wdown, bdown, Wsu, bsu, Wsg, bsg, Wsd, bsd, out):
    x_v = x.rearrange("b (c p) d -> p (b c) d", p=P)
    out_v = out.rearrange("b (c p) d -> p (b c) d", p=P)
    ctx_v = ctx_in.rearrange("b (c p) d -> p (b c) d", p=P)
    cum_dram = nc.dram_tensor("cum_dram", (3, NH * T, P), BF16, kind="Internal").ap()

    with ExitStack() as stack:
        def sb(name, shape, dt=F32):
            return stack.enter_context(nc.sbuf_tensor(name, shape, dt))

        def sem(name):
            return stack.enter_context(nc.semaphore(name))

        bank = [stack.enter_context(nc.psum_tensor(f"bank{i}", [P, HALF], F32)) for i in range(8)]

        ident = sb("ident", [P, P])
        ident_bf = sb("ident_bf", [P, P], BF16)
        neg_tri = sb("neg_tri", [P, P])
        neg_ones = sb("neg_ones", [P, P])
        mask = sb("mask", [P, 4, P], BF16)
        earlier = sb("earlier", [P, NR, NR])
        xres = sb("xres", [P, T, DM])
        stats = sb("stats", [P, T, 6])
        mv = sb("mv", [P, T, 2])
        var = sb("var", [P, T])
        lnv = sb("lnv", [P, T])
        rstd = sb("rstd", [P, T])
        nt0 = sb("nt0", [P, T])
        nt1 = sb("nt1", [P, T])
        uth = sb("uth", [P, KD, T * P], F32R)
        utl = sb("utl", [P, KD, T * P], F32R)
        xtok = sb("xtok", [P, T, DM])
        xsd = sb("xsd", [P, NSEQ, DM])
        y = sb("y", [P, T, DM])
        z = sb("z", [P, T, DM])
        sig = sb("sig", [P, T, DM])
        a_log = sb("a_log", [P, T, NH])
        neg_abs = sb("neg_abs", [P, T, NH])
        dts = sb("dts", [P, T, NH])
        cum = sb("cum", [P, T, NH])
        rem = sb("rem", [P, T, NH])
        cparts = sb("cparts", [P, 3, NH, T], BF16)
        cpartsT = sb("cpartsT", [P, 3, 2, P], BF16)
        ecum = sb("ecum", [P, NSEQ, NH])
        sdec = sb("sdec", [P, NSEQ, NH])
        w_raw = [sb(f"w_raw{i}", [P, 2, DM]) for i in range(2)]
        parts = sb("parts", [P, 8, HALF], F32R)
        wth = [parts[:, i, :].rearrange("p (a k c) -> p a k c", a=2, k=KD) for i in range(2)]
        wtl = [parts[:, 2 + i, :].rearrange("p (a k c) -> p a k c", a=2, k=KD) for i in range(2)]
        conv = [sb(f"conv{i}", [P, 2, T * P]) for i in range(2)]
        taps = [sb(f"taps{i}", [P, 2, TAPS]) for i in range(2)]
        tap_b = [sb(f"tap_b{i}", [P, 2]) for i in range(2)]
        cl = [sb(f"cl{i}", [27, 2, P], BF16) for i in range(2)]
        cr = [sb(f"cr{i}", [27, 2, T, P], BF16) for i in range(2)]
        dec = [sb(f"dec{i}", [P, HALF]) for i in range(2)]
        g = [sb(f"g{i}", [P, HALF]) for i in range(2)]
        gh = [parts[:, 4 + i, :] for i in range(2)]
        gl = [parts[:, 6 + i, :] for i in range(2)]
        xp = [sb(f"xp{i}", [P, T, 2, 2, HD], F32R) for i in range(2)]
        xs = [sb(f"xs{i}", [P, NSEQ, 2 * HD]) for i in range(2)]
        xpair = [sb(f"xpair{i}", [P, T, 2 * HD]) for i in range(2)]
        btok = sb("btok", [P, NSEQ, P])
        state = sb("state", [P, NSEQ, 2, HD])
        ysum = sb("ysum", [P, T, 2, HD])
        yint = sb("yint", [P, NSEQ, 2, HD])
        wzh = sb("wzh", [P, KD, ZA], F32R)
        wzl = sb("wzl", [P, KD, ZA], F32R)
        zb = sb("zb", [P, DM])
        db = sb("db", [P, NH])
        woT = sb("woT", [P, KD, DM])
        yzT = [sb(f"yzT{i}", [P, DM]) for i in range(2)]
        wi_wj = sb("wi_wj", [CTX, 2])
        wj_rep = sb("wj_rep", [CTX, P])
        xbb = sb("xbb", [P, 1])
        si = sb("si", [P, T])
        ew_raw = [sb(f"ew_raw{i}", [P, 3, KD * DM]) for i in range(2)]
        ewh = [sb(f"ewh{i}", [P, 3, KD, DM], F32R) for i in range(2)]
        ewl = [sb(f"ewl{i}", [P, 3, KD, DM], F32R) for i in range(2)]
        uh = sb("uh", [P, 4, HALF], F32R)
        ul = sb("ul", [P, 4, HALF], F32R)
        eh = parts[:, 0:4, :]
        el = parts[:, 4:8, :]
        b_rows = sb("b_rows", [2 * NE, DM])
        b_cols = sb("b_cols", [P, NE, 2, KD])
        eb = [sb(f"eb{i}", [P, 2, KD]) for i in range(2)]
        bd = sb("bd", [NE, DM])
        wr_raw = sb("wr_raw", [P, KD, 8])
        wrh = sb("wrh", [P, KD, 8], F32R)
        wrl = sb("wrl", [P, KD, 8], F32R)
        brb = sb("brb", [P, 2, NR])
        lg = sb("lg", [P, T, NR])
        bg = sb("bg", [P, T, NR])
        gt = sb("gt", [P, T, NR, NR])
        ge = sb("ge", [P, T, NR, NR])
        sel = sb("sel", [P, T, NR])
        mx = sb("mx", [P, T])
        prob = sb("prob", [P, T, NE])
        probT = sb("probT", [NE, T * P])
        u32 = conv[0][:].rearrange("p a (b n) -> p (a b) n", n=HALF)
        e32 = conv[1][:].rearrange("p a (b n) -> p (a b) n", n=HALF)
        xn = y
        wz_rawz = ew_raw[0][:, 0, :].rearrange("p (a d) -> p a d", a=2)
        wz_rawa = ew_raw[0][0:NH, 1, 0:DM]
        wo_raw = ew_raw[0][:, 2, :].rearrange("p (a d) -> p a d", a=2)
        ctx_raw = ew_raw[1][:, 0, :].rearrange("p (t d) -> p t d", t=T)
        ctxT = ew_raw[1][0:CTX, 1:3, :].rearrange("p a n -> p (a n)")

        def f32(ap):
            return ap.bitcast(F32)

        x_in = [sem(f"x_in{i}") for i in range(2)]
        w_in = [sem(f"w_in{i}") for i in range(2)]
        taps_in = [sem(f"taps_in{i}") for i in range(2)]
        cum_in = [sem(f"cum_in{i}") for i in range(2)]
        ew_in = [sem(f"ew_in{i}") for i in range(2)]
        wz_in, wo_in, ctx_sm_in = sem("wz_in"), sem("wo_in"), sem("ctx_sm_in")
        small_in = sem("small_in")
        cum_out, y_out = sem("cum_out"), sem("y_out")
        const_chain, const_done = sem("const_chain"), sem("const_done")
        dve_chain, act_chain = sem("dve_chain"), sem("act_chain")
        var_done, rstd_done, xn_done = sem("var_done"), sem("rstd_done"), sem("xn_done")
        ut_turned, uth_done, utl_done = sem("ut_turned"), sem("uth_done"), sem("utl_done")
        w_turned, wth_done, wtl_done = sem("w_turned"), sem("wth_done"), sem("wtl_done")
        wz_turned, wzh_done, wzl_done = sem("wz_turned"), sem("wzh_done"), sem("wzl_done")
        za_done, za_read = sem("za_done"), sem("za_read")
        nabs_done, sp_done, dt_done = sem("nabs_done"), sem("sp_done"), sem("dt_done")
        cum_done, cum_read, cexp_done = sem("cum_done"), sem("cum_read"), sem("cexp_done")
        cpart_done, cpart_turned, cpart_read = sem("cpart_done"), sem("cpart_turned"), sem("cpart_read")
        x_turned, x_read, xtok_ready = sem("x_turned"), sem("x_read"), sem("xtok_ready")
        misc_turned, misc_read, wj_done = sem("misc_turned"), sem("misc_read"), sem("wj_done")
        pair_done, pair_read = sem("pair_done"), sem("pair_read")
        proj_done, acc_first, tap_done = sem("proj_done"), sem("acc_first"), sem("tap_done")
        expo_done, exp_done, cb_done = sem("expo_done"), sem("exp_done"), sem("cb_done")
        g_done, gh_done, gl_done, y_done = sem("g_done"), sem("gh_done"), sem("gl_done"), sem("y_done")
        b_turned, b_read, st_done, st_read = sem("b_turned"), sem("b_read"), sem("st_done"), sem("st_read")
        inter_done, y_step = sem("inter_done"), sem("y_step")
        eb_done = sem("eb_done")
        xp_hi, xp_lo, xs_done = sem("xp_hi"), sem("xp_lo"), sem("xs_done")
        sig_done, silu_done = sem("sig_done"), sem("silu_done")
        yz_done, yz_turned, yz_read = sem("yz_done"), sem("yz_turned"), sem("yz_read")
        o_done, o_read = sem("o_done"), sem("o_read")
        wr_done, gate_done, pexp_in, pexp_done = sem("wr_done"), sem("gate_done"), sem("pexp_in"), sem("pexp_done")
        prob_done, prob_turned, prob_read = sem("prob_done"), sem("prob_turned"), sem("prob_read")
        bdn_done, bdn_read = sem("bdn_done"), sem("bdn_read")
        ewh_done, ewl_done = sem("ewh_done"), sem("ewl_done")
        up_done, up_read, uh_done, ul_done = sem("up_done"), sem("up_read"), sem("uh_done"), sem("ul_done")
        gate2_done, silu2_done, e_done = sem("gate2_done"), sem("silu2_done"), sem("e_done")
        eh_done, el_done, down_done, acc_done = sem("eh_done"), sem("el_done"), sem("down_done"), sem("acc_done")

        def at_least(eng, s, n):
            if not isinstance(n, int) or n > 0:
                eng.wait_ge(s, n)

        def over_pairs(eng, body):
            body(1, 0, 1)
            with eng.Fori(1, PAIRS // 2 - 1) as k:
                body(2 * k, k, 0)
                body(2 * k + 1, k, 1)
            for n in range(PAIRS - 2, PAIRS + 1):
                body(n, n // 2, n % 2)

        def last(n, ahead):
            return isinstance(n, int) and n + ahead > PAIRS

        def over_experts(eng, body):
            for e in range(2):
                body(e, e // 2, e % 2)
            with eng.Fori(1, NE // 2 - 1) as k:
                body(2 * k, k, 0)
                body(2 * k + 1, k, 1)
            for e in range(NE - 2, NE):
                body(e, e // 2, e % 2)

        block = stack.enter_context(nc.Block())

        @block.sync
        def _(sp):
            def load_w(m, k, q):
                at_least(sp, w_turned, m - 1)
                b0 = 0 if isinstance(m, int) and m == 0 else C_B + P * (m - 1)
                c0 = P if isinstance(m, int) and m == 0 else C_C + P * (m - 1)
                sp.dma_start(w_raw[q][:, 0, :], W_in[bass.ds(b0, P), :]).then_inc(w_in[q], 16)
                sp.dma_start(w_raw[q][:, 1, :], W_in[bass.ds(c0, P), :]).then_inc(w_in[q], 16)

            def load_taps(m, q):
                at_least(sp, tap_done, 12 * (m - 1))
                b0 = 0 if isinstance(m, int) and m == 0 else C_B + P * (m - 1)
                c0 = P if isinstance(m, int) and m == 0 else C_C + P * (m - 1)
                for j, r0 in enumerate((b0, c0)):
                    sp.dma_start(taps[q][:, j, :], conv_w[bass.ds(r0, P), :]).then_inc(taps_in[q], 16)
                    sp.dma_start(tap_b[q][:, j:j + 1],
                                 conv_b[bass.ds(r0, P)].unsqueeze(1)).then_inc(taps_in[q], 16)

            def load_cum(m, q):
                at_least(sp, expo_done, 4 * (m - 2))
                for s in range(3):
                    sp.dma_start(cl[q][T * s:T * s + T, :, :],
                                 cum_dram[s, bass.ds(2 * T * (m - 1), 2 * T), :]
                                 .rearrange("(j t) k -> t j k", j=2)).then_inc(cum_in[q], 16)
                sp.dma_start(cr[q][24:27, :, :, :].rearrange("s j t k -> s (j t k)"),
                             cum_dram[:, bass.ds(2 * T * (m - 1), 2 * T), :]
                             .rearrange("s r k -> s (r k)")).then_inc(cum_in[q], 16)

            for i in range(2):
                sp.dma_start(xres[:, 4 * i:4 * i + 4, :], x_v[:, 4 * i:4 * i + 4, :]).then_inc(x_in[i], 16)
            load_w(0, 0, 0)
            load_w(1, 0, 1)
            load_taps(0, 0)
            load_taps(1, 1)
            load_w(2, 1, 0)
            load_w(3, 1, 1)
            load_taps(2, 0)
            sp.wait_ge(cpart_read, 1)
            sp.dma_start(cum_dram.rearrange("s (c p) k -> p s c k", p=P), cpartsT[:]).then_inc(cum_out, 16)
            sp.wait_ge(cum_out, 16)
            sp.wait_ge(const_done, 1)
            load_cum(1, 1)

            def body(n, k, q):
                if not last(n, 1):
                    load_cum(n + 1, 1 - q)
                if not last(n, 3):
                    load_w(n + 3, None, 1 - q)
                if not last(n, 2) and not (isinstance(n, int) and n == 0):
                    load_taps(n + 2, q)

            over_pairs(sp, body)

            def load_expert(e, q):
                at_least(sp, ewl_done, 3 * (e - 1))
                for j, w in enumerate((Wup, Wgate, Wdown)):
                    sp.dma_start(ew_raw[q][:, j, :].rearrange("p (k d) -> p k d", k=KD),
                                 w[bass.ds(e, 1), :, :].rearrange("e (k p) d -> p (e k) d", p=P)).then_inc(ew_in[q], 16)

            load_expert(0, 0)
            load_expert(1, 1)
            with sp.Fori(1, 3) as k:
                load_expert(2 * k, 0)
                load_expert(2 * k + 1, 1)
            load_expert(6, 0)
            at_least(sp, ewl_done, 3 * (NE - 2))
            for j, w in enumerate((Wsu, Wsg, Wsd)):
                sp.dma_start(ew_raw[1][:, j, :].rearrange("p (k d) -> p k d", k=KD),
                             w.rearrange("(k p) d -> p k d", p=P)).then_inc(ew_in[1], 16)
            for i in range(4):
                sp.wait_ge(acc_done, T * (NE - 1) + 2 * i + 2)
                sp.dma_start(out_v[:, 2 * i:2 * i + 2, :], xres[:, 2 * i:2 * i + 2, :]).then_inc(y_out, 16)
            sp.wait_ge(y_out, 64)

        @block.gpsimd
        def _(pool):
            steps = [0]

            def link(ins):
                steps[0] += 1
                ins.then_inc(const_chain, 1)
                pool.wait_ge(const_chain, steps[0])

            link(pool.memset(ident[:], 0.0))
            link(pool.affine_select(out=ident[:], in_=ident[:], compare_op=ALU.not_equal, fill=1.0,
                                    base=0, pattern=[[-1, P]], channel_multiplier=1))
            pool.tensor_copy(ident_bf[:], ident[:]).then_inc(const_done, 1)
            link(pool.memset(neg_ones[:], -1.0))
            link(pool.affine_select(out=neg_tri[:], in_=neg_ones[:], compare_op=ALU.is_ge, fill=0.0,
                                    base=0, pattern=[[1, P]], channel_multiplier=-1))
            link(pool.memset(mask[:], 0.0))
            link(pool.affine_select(out=mask[:], in_=mask[:], compare_op=ALU.is_ge, fill=NEG,
                                    base=0, pattern=[[0, 4], [1, P]], channel_multiplier=-1))
            link(pool.memset(earlier[:], 1.0))
            link(pool.affine_select(out=earlier[:], in_=earlier[:], compare_op=ALU.is_gt, fill=0.0,
                                    base=0, pattern=[[1, NR], [-1, NR]], channel_multiplier=0))
            link(pool.memset(state[:], 0.0))
            for q in range(2):
                link(pool.memset(cl[q][:], 1.0))
                link(pool.memset(cr[q][:], 0.0))
                for s in range(3):
                    link(pool.affine_select(out=cr[q][:].rearrange("p j t k -> p j t k"), in_=cr[q][:],
                                            compare_op=ALU.not_equal, fill=-1.0, base=-T * s,
                                            pattern=[[0, 2], [-1, T], [0, P]], channel_multiplier=1))
            pool.memset(prob[:], 1.0).then_inc(const_done, 1)

            def prepare(m, q):
                c0 = 2 * HD * (m - 1)
                src = xtok[:, :, bass.ds(c0, 2 * HD)]
                pool.tensor_copy(xp[q][:, :, :, 0, :], src.rearrange("p t (j d) -> p t j d", j=2)).then_inc(xp_hi, 1)
                pool.tensor_copy(xpair[q][:], src).then_inc(xp_hi, 1)
                pool.tensor_copy(xs[q][:], xsd[:, :, bass.ds(c0, 2 * HD)]).then_inc(xs_done, 1)
                pool.wait_ge(xp_hi, 2 * m)
                pool.tensor_tensor(xp[q][:, :, :, 1, :], xpair[q][:].rearrange("p t (j d) -> p t j d", j=2),
                                   f32(xp[q][:, :, :, 0, :]), ALU.subtract).then_inc(xp_lo, 1)

            pool.wait_ge(xtok_ready, 2)
            prepare(1, 1)

            def body(n, k, q):
                for u in range(4):
                    a = 4 * (n - 1) + u
                    pool.wait_ge(gh_done, a + 1)
                    at_least(pool, y_done, a - 1)
                    pool.tensor_tensor(gl[u % 2], g[u % 2][:], f32(gh[u % 2]),
                                       ALU.subtract).then_inc(gl_done, 1)
                    if u == 1 and not last(n, 1):
                        prepare(n + 1, 1 - q)

            over_pairs(pool, body)

            def expert(e, k, q):
                if isinstance(e, int) and e == 0:
                    pool.wait_ge(misc_read, 2)
                pool.tensor_copy(eb[q][:], b_cols[:, bass.ds(e, 1), :, :].rearrange("p e a k -> p (e a) k")).then_inc(eb_done, 1)
                for v in range(4):
                    pool.wait_ge(uh_done, 4 * e + v + 1)
                    pool.tensor_tensor(ul[:, v, :], u32[:, v, :], f32(uh[:, v, :]),
                                       ALU.subtract).then_inc(ul_done, 1)
                for v in range(4):
                    pool.wait_ge(eh_done, 4 * e + v + 1)
                    pool.tensor_tensor(el[:, v, :], e32[:, v, :], f32(eh[:, v, :]),
                                       ALU.subtract).then_inc(el_done, 1)

            over_experts(pool, expert)

        @block.scalar
        def _(act):
            steps = [0]

            def link(ins):
                steps[0] += 1
                ins.then_inc(act_chain, 1)
                act.wait_ge(act_chain, steps[0])

            act.dma_start(wz_rawz, W_in[C_Z:C_Z + DM, :].rearrange("(a p) d -> p a d", p=P)).then_inc(wz_in, 16)
            act.dma_start(wz_rawa, W_in[C_A:C_A + NH, :]).then_inc(wz_in, 16)
            act.dma_start(zb[:], z_bias.partition_broadcast(P)).then_inc(small_in, 16)
            act.dma_start(db[:], D.partition_broadcast(P)).then_inc(small_in, 16)
            act.dma_start(wo_raw, W_out.rearrange("(a p) d -> p a d", p=P)).then_inc(wo_in, 16)
            act.dma_start(ctx_raw, ctx_v).then_inc(ctx_sm_in, 16)
            with nc.allow_non_contiguous_dma(reason="128 values"):
                act.dma_start(wi_wj[:], xw.rearrange("a (j p) -> p (a j)", j=2)).then_inc(ctx_sm_in, 16)
            act.dma_start(xbb[:], xb.partition_broadcast(P)).then_inc(small_in, 16)
            act.dma_start(brb[:, 0, :], br.partition_broadcast(P)).then_inc(small_in, 16)
            act.dma_start(brb[:, 1, :], gate_bias.partition_broadcast(P)).then_inc(small_in, 16)
            act.dma_start(wr_raw[:, :, 0:NR], Wr.rearrange("(k p) e -> p k e", p=P)).then_inc(small_in, 16)
            for dst, src in ((b_rows[0:NR, :], bup), (b_rows[NR:NE, :], bsu.unsqueeze(0)),
                             (b_rows[NE:NE + NR, :], bgate), (b_rows[NE + NR:2 * NE, :], bsg.unsqueeze(0)),
                             (bd[0:NR, :], bdown), (bd[NR:NE, :], bsd.unsqueeze(0))):
                act.dma_start(dst, src).then_inc(small_in, 16)

            def inverse_root(ev):
                s = slice(4 * (ev % 2), 4 * (ev % 2) + 4)
                act.wait_ge(var_done, ev + 1)
                link(act.activation(lnv[:, s], var[:, s], ACT.Ln))
                act.activation(rstd[:, s], lnv[:, s], ACT.Exp, scale=-0.5).then_inc(rstd_done, 1)

            def split_turned(i, b):
                h, k = i % 4 // 2, i % 2
                act.wait_ge(ut_turned, i + 1)
                act.copy(uth[:, k, HALF * h:HALF * (h + 1)], bank[b][:]).then_inc(uth_done, 1)

            def split_w(m, q):
                act.wait_ge(w_turned, m + 1)
                at_least(act, proj_done, 4 * (m - 1))
                act.copy(parts[:, q, :], bank[6][:]).then_inc(wth_done, 1)

            def first_tap(m, k, q, u):
                act.wait_ge(proj_done, 4 * m + u + 1)
                if u == 0:
                    act.wait_ge(taps_in[q], 64 * (k + 1))
                j, h = u // 2, u % 2
                act.activation(conv[q][:, j, HALF * h:HALF * (h + 1)], bank[u % 2][:], ACT.Identity,
                               bias=tap_b[q][:, j:j + 1], scale=taps[q][:, j, TAPS - 1:TAPS]).then_inc(acc_first, 1)

            inverse_root(0)
            inverse_root(1)
            split_w(0, 0)
            for k in range(KD):
                act.wait_ge(wz_turned, k + 1)
                act.copy(wzh[:, k, :], bank[4 + k][:, 0:ZA]).then_inc(wzh_done, 1)
            for i in range(4):
                split_turned(i, i)
            split_w(1, 1)
            for u in range(4):
                first_tap(0, 0, 0, u)
            act.wait_ge(nabs_done, 1)
            link(act.activation(neg_abs[:], neg_abs[:], ACT.Exp))
            act.activation(neg_abs[:], neg_abs[:], ACT.Ln, bias=1.0).then_inc(sp_done, 1)
            for i in range(4):
                act.wait_ge(x_turned, i + 1)
                act.copy(xtok[:, 2 * i:2 * i + 2, :].rearrange("p t d -> p (t d)"), bank[2 + i % 2][:]).then_inc(x_read, 1)
            for u in range(4):
                first_tap(1, 0, 1, u)
            act.wait_ge(cum_read, 1)
            act.activation(ecum[:], cum[:].rearrange("p (b c) h -> p b c h", c=2)[:, :, 1, :], ACT.Exp).then_inc(cexp_done, 1)
            act.activation(sdec[:], sdec[:], ACT.Exp).then_inc(cexp_done, 1)
            act.wait_ge(cpart_turned, 1)
            act.copy(cpartsT[:].rearrange("p s c k -> p (s c k)"),
                     bank[5][:].bitcast(BF16)[:, 0:6 * P]).then_inc(cpart_read, 1)
            split_w(2, 0)
            act.wait_ge(misc_turned, 1)
            act.copy(woT[:].rearrange("p k d -> p (k d)"), bank[4][:]).then_inc(misc_read, 1)
            act.wait_ge(misc_turned, 2)
            act.copy(b_cols[:].rearrange("p e a k -> p k a e"),
                     bank[5][:, 0:KD * 2 * NE].rearrange("p (k a e) -> p k a e", k=KD, a=2)).then_inc(misc_read, 1)
            for i in range(2):
                act.wait_ge(misc_turned, 3 + i)
                act.copy(ctxT[:, HALF * i:HALF * (i + 1)], bank[2 + i][0:CTX, :]).then_inc(misc_read, 1)
            for i in range(2):
                act.wait_ge(pair_done, i + 1)
                act.copy(sig[:].rearrange("p (b c) d -> p b c d", c=2)[:, 2 * i:2 * i + 2, 0, :],
                         bank[4 + i][:].rearrange("p (b d) -> p b d", b=2)).then_inc(pair_read, 1)
            act.wait_ge(pair_done, 3)
            act.activation(si[:], bank[2][:, 0:T], ACT.Identity, bias=xbb[:, 0:1]).then_inc(pair_read, 1)

            def body(n, k, q):
                for u in range(4):
                    a, b = 4 * (n - 1) + u, u % 2
                    act.wait_ge(expo_done, a + 1)
                    at_least(act, g_done, a - 1)
                    act.activation(dec[b][:], bank[4 + b][:], ACT.Exp).then_inc(exp_done, 1)
                    act.wait_ge(g_done, a + 1)
                    at_least(act, y_done, a - 1)
                    act.copy(gh[b], g[b][:]).then_inc(gh_done, 1)
                    if not last(n, 1):
                        if u == 0:
                            at_least(act, inter_done, n - 1)
                        first_tap(n + 1, k + (q + 1) // 2, 1 - q, u)
                    if u == 0:
                        act.wait_ge(b_turned, n)
                        at_least(act, st_done, n - 1)
                        act.copy(btok[:].rearrange("p b k -> p (b k)"), bank[6][:]).then_inc(b_read, 1)
                    if u == 1:
                        act.wait_ge(st_done, n)
                        at_least(act, inter_done, n - 1)
                        s_v = bank[6][:, 0:NSEQ * 2 * HD].rearrange("p (b j d) -> p b j d", b=NSEQ, j=2)
                        for j in range(2):
                            r = slice(NS * j, NS * (j + 1))
                            act.copy(state[r, :, j, :], s_v[r, :, j, :]).then_inc(st_read, 1)
                    if u == 2 and not last(n, 2):
                        split_w(n + 2, q)
                if isinstance(n, int) and n == 1:
                    act.wait_ge(pair_read, 3)
                    for t in (1, 3, 5, 7, 0, 2, 4, 6):
                        if t == 0:
                            act.wait_ge(sig_done, 4)
                        act.activation(sig[:, t, :], sig[:, t - t % 2, :], ACT.Sigmoid,
                                       bias=si[:, t:t + 1]).then_inc(sig_done, 1)
                    act.wait_ge(za_read, 2 * T)
                    act.activation(z[:], z[:], ACT.Silu).then_inc(silu_done, 1)

            over_pairs(act, body)

            for t in range(T):
                act.wait_ge(yz_turned, t + 1)
                at_least(act, o_done, t - 1)
                act.copy(yzT[t % 2][:], bank[t % 2][:, 0:DM]).then_inc(yz_read, 1)
            for ev in range(2, 6):
                inverse_root(ev)
            for i in range(4, 8):
                split_turned(i, i)
            act.wait_ge(pexp_in, 1)
            act.activation(lg[:], lg[:], ACT.Exp).then_inc(pexp_done, 1)

            def split_expert(e, q):
                for j in range(3):
                    act.copy(ewh[q][:, j, :, :].rearrange("p k d -> p (k d)"), ew_raw[q][:, j, :]).then_inc(ewh_done, 1)

            def expert(e, k, q):
                if isinstance(e, int) and e == 0:
                    act.wait_ge(ew_in[0], 48)
                    split_expert(0, 0)
                act.wait_ge(eb_done, e + 1)
                for v in range(4):
                    act.wait_ge(up_done, 4 * e + v + 1)
                    at_least(act, e_done, 4 * (e - 1) + v + 1)
                    act.activation(u32[:, v, :], bank[v][:], ACT.Identity,
                                   bias=eb[q][:, 0, v % 2:v % 2 + 1]).then_inc(up_read, 1)
                if not (isinstance(e, int) and e == NE - 1):
                    at_least(act, down_done, 4 * e)
                    act.wait_ge(ew_in[1 - q], 48 * (k + q + 1))
                    split_expert(e + 1, 1 - q)

                def round_e(v):
                    act.wait_ge(e_done, 4 * e + v + 1)
                    at_least(act, down_done, 4 * e)
                    act.copy(eh[:, v, :], e32[:, v, :]).then_inc(eh_done, 1)

                for v in range(4):
                    act.wait_ge(gate2_done, 4 * e + v + 1)
                    at_least(act, el_done, 4 * (e - 1) + v + 1)
                    act.activation(e32[:, v, :], bank[v][:], ACT.Silu,
                                   bias=eb[q][:, 1, v % 2:v % 2 + 1]).then_inc(silu2_done, 1)
                    if v:
                        round_e(v - 1)
                round_e(3)

            over_experts(act, expert)

        @block.vector
        def _(dve):
            steps = [0]

            def link(ins):
                steps[0] += 1
                ins.then_inc(dve_chain, 1)
                dve.wait_ge(dve_chain, steps[0])

            def norm_stats(g4, ev):
                s = slice(4 * g4, 4 * g4 + 4)
                for t in range(4 * g4, 4 * g4 + 4):
                    ins = dve.bn_stats(stats[:, t, :], xres[:, t, :])
                link(ins)
                for t in range(4 * g4, 4 * g4 + 4):
                    ins = dve.bn_aggr(mv[:, t, :], stats[:, t, :])
                link(ins)
                dve.tensor_scalar(var[:, s], mv[:, s, 1], EPS, None, ALU.add).then_inc(var_done, 1)
                dve.wait_ge(rstd_done, ev + 1)
                link(dve.tensor_tensor(nt0[:, s], rstd[:, s], rstd[:, s], ALU.mult))
                link(dve.tensor_tensor(nt1[:, s], nt0[:, s], var[:, s], ALU.mult))
                link(dve.tensor_scalar(nt0[:, s], nt1[:, s], -0.5, 1.5, ALU.mult, ALU.add))
                link(dve.tensor_tensor(rstd[:, s], rstd[:, s], nt0[:, s], ALU.mult))

            def normalise(g4):
                for t in range(4 * g4, 4 * g4 + 4):
                    dve.tensor_scalar(xn[:, t, :], xres[:, t, :], mv[:, t, 0:1], rstd[:, t:t + 1],
                                      ALU.subtract, ALU.mult).then_inc(xn_done, 1)

            def rest_turned(i, b):
                h, k = i % 4 // 2, i % 2
                s = slice(HALF * h, HALF * (h + 1))
                dve.wait_ge(uth_done, i + 1)
                dve.tensor_tensor(utl[:, k, s], bank[b][:], f32(uth[:, k, s]), ALU.subtract).then_inc(utl_done, 1)

            def rest_w(m, q):
                dve.wait_ge(wth_done, m + 1)
                dve.tensor_tensor(parts[:, 2 + q, :], bank[6][:],
                                  f32(parts[:, q, :]), ALU.subtract).then_inc(wtl_done, 1)

            def other_taps(m, q, u):
                j, h = u // 2, u % 2
                src = bank[u % 2][:].rearrange("p (b l) -> p b l", b=2)
                dst = conv[q][:, j, HALF * h:HALF * (h + 1)].rearrange("p (b l) -> p b l", b=2)
                dve.wait_ge(acc_first, 4 * m + u + 1)
                for d in range(1, TAPS):
                    if d > 1:
                        dve.wait_ge(tap_done, 3 * (4 * m + u) + d - 1)
                    dve.scalar_tensor_tensor(
                        out=dst[:, :, d:SEQ], in0=src[:, :, 0:SEQ - d], scalar=taps[q][:, j, TAPS - 1 - d:TAPS - d],
                        in1=dst[:, :, d:SEQ], op0=ALU.mult, op1=ALU.add).then_inc(tap_done, 1)

            for i in range(2):
                dve.wait_ge(x_in[i], 16)
                norm_stats(i, i)
                normalise(i)
            rest_w(0, 0)
            for k in range(KD):
                dve.wait_ge(wzh_done, k + 1)
                dve.tensor_tensor(wzl[:, k, :], bank[4 + k][:, 0:ZA], f32(wzh[:, k, :]), ALU.subtract).then_inc(wzl_done, 1)
            for i in range(4):
                rest_turned(i, i)
            rest_w(1, 1)
            for u in range(4):
                other_taps(0, 0, u)
            dve.wait_ge(small_in, 12 * 16)
            for t in range(T):
                dve.wait_ge(za_done, t + 1)
                b = bank[4 + t % 2]
                dve.tensor_tensor(z[:, t, :], b[:, 0:DM], zb[:], ALU.add).then_inc(za_read, 1)
                dve.tensor_copy(a_log[:, t, :], b[:, DM:ZA]).then_inc(za_read, 1)
            dve.wait_ge(za_read, 2 * T)
            dve.scalar_tensor_tensor(out=neg_abs[:], in0=a_log[:], scalar=-1.0, in1=a_log[:],
                                     op0=ALU.mult, op1=ALU.min).then_inc(nabs_done, 1)
            dve.wait_ge(sp_done, 1)
            dve.scalar_tensor_tensor(out=dts[:], in0=a_log[:], scalar=0.0, in1=neg_abs[:],
                                     op0=ALU.max, op1=ALU.add).then_inc(dt_done, 1)
            dve.wait_ge(cum_done, 1)
            cs = bank[7][:, 0:T * NH].rearrange("p (t h) -> p t h", t=T)
            tot = bank[7][:, T * NH:2 * T * NH].rearrange("p (b c h) -> p b c h", c=2, h=NH)
            link(dve.tensor_copy(cum[:], cs))
            cum_v = cum[:].rearrange("p (b c) h -> p b c h", c=2)
            dve.tensor_tensor(sdec[:], tot[:, :, 0, :], cum_v[:, :, 0, :], ALU.subtract).then_inc(cum_read, 1)
            link(dve.tensor_copy(cparts[:, 0, :, :].rearrange("p h t -> p t h"), cum[:]))
            link(dve.tensor_tensor(rem[:], cum[:], cparts[:, 0, :, :].rearrange("p h t -> p t h"), ALU.subtract))
            link(dve.tensor_copy(cparts[:, 1, :, :].rearrange("p h t -> p t h"), rem[:]))
            link(dve.tensor_tensor(rem[:], rem[:], cparts[:, 1, :, :].rearrange("p h t -> p t h"), ALU.subtract))
            dve.tensor_copy(cparts[:, 2, :, :].rearrange("p h t -> p t h"), rem[:]).then_inc(cpart_done, 1)
            for u in range(4):
                other_taps(1, 1, u)
            dve.wait_ge(x_read, 4)
            for t in range(T):
                ins = dve.tensor_tensor(y[:, t, :].rearrange("p (h d) -> p h d", h=NH),
                                        xtok[:, t, :].rearrange("p (h d) -> p h d", h=NH),
                                        db[:].unsqueeze(2).to_broadcast([P, NH, HD]), ALU.mult)
            ins.then_inc(xtok_ready, 1)
            dve.wait_ge(cexp_done, 2)
            for b in range(NSEQ):
                ins = dve.tensor_tensor(xsd[:, b, :].rearrange("p (h d) -> p h d", h=NH),
                                        xtok[:, 2 * b, :].rearrange("p (h d) -> p h d", h=NH),
                                        sdec[:, b, :].unsqueeze(2).to_broadcast([P, NH, HD]), ALU.mult)
            ins.then_inc(xtok_ready, 1)
            rest_w(2, 0)
            dve.memset(f32(wrh[:]), 0.0)
            link(dve.memset(f32(wrl[:]), 0.0))
            link(dve.tensor_copy(wrh[:, :, 0:NR], wr_raw[:, :, 0:NR]))
            dve.tensor_tensor(wrl[:, :, 0:NR], wr_raw[:, :, 0:NR], f32(wrh[:, :, 0:NR]), ALU.subtract).then_inc(wr_done, 1)
            dve.wait_ge(ctx_sm_in, 32)
            dve.tensor_copy(wj_rep[:], wi_wj[:, 1:2].to_broadcast([CTX, P])).then_inc(wj_done, 1)

            def read_y(n):
                dve.wait_ge(y_done, 4 * n)
                dve.wait_ge(inter_done, n)
                dve.tensor_reduce(ysum[:], bank[7][:, 0:4 * T * HD].rearrange("p (t j s d) -> p (t j) d s", t=T, j=2, s=2),
                                  AX.X, ALU.add).then_inc(y_step, 1)
                dve.tensor_tensor(yint[:], bank[7][:, 256:256 + NSEQ * 2 * HD].rearrange("p (b j d) -> p b j d", b=NSEQ, j=2),
                                  ecum[:, :, bass.ds(2 * (n - 1), 2)].unsqueeze(3).to_broadcast([P, NSEQ, 2, HD]),
                                  ALU.mult).then_inc(y_step, 1)
                odd = ysum[:].rearrange("p (b c) j d -> p b c (j d)", c=2)[:, :, 1, :]
                dve.wait_ge(y_step, 4 * (n - 1) + 2)
                dve.tensor_tensor(odd, odd, yint[:].rearrange("p b j d -> p b (j d)"), ALU.add).then_inc(y_step, 1)
                dst = y[:, :, bass.ds(2 * HD * (n - 1), 2 * HD)]
                dve.wait_ge(y_step, 4 * (n - 1) + 3)
                dve.tensor_tensor(dst, dst, ysum[:].rearrange("p t j d -> p t (j d)"), ALU.add).then_inc(y_step, 1)

            def body(n, k, q):
                for u in range(4):
                    a, b = 4 * (n - 1) + u, u % 2
                    dve.wait_ge(exp_done, a + 1)
                    dve.wait_ge(cb_done, a + 1)
                    at_least(dve, gl_done, a - 1)
                    dve.tensor_tensor(g[b][:], bank[2 + b][:], dec[b][:], ALU.mult).then_inc(g_done, 1)
                    if not last(n, 1):
                        other_taps(n + 1, 1 - q, u)
                    if u == 0 and not (isinstance(n, int) and n == 1):
                        read_y(n - 1)
                    if u == 2 and not last(n, 2):
                        rest_w(n + 2, q)

            over_pairs(dve, body)
            read_y(PAIRS)
            dve.wait_ge(y_step, 4 * PAIRS)

            dve.wait_ge(silu_done, 1)
            for t in range(T):
                dve.tensor_tensor(y[:, t, :], y[:, t, :], z[:, t, :], ALU.mult).then_inc(yz_done, 1)
            dve.wait_ge(sig_done, T)
            for i in range(2):
                for t in range(4 * i, 4 * i + 4):
                    dve.wait_ge(o_done, t + 1)
                    dve.tensor_tensor(xres[:, t, :], bank[2 + t % 2][:, 0:DM], xres[:, t, :], ALU.add).then_inc(o_read, 1)
                dve.wait_ge(o_read, 4 * i + 4)
                norm_stats(i, 2 + i)
                s = slice(4 * i, 4 * i + 4)
                link(dve.tensor_scalar(nt0[:, s], rstd[:, s], 1 - P_SEM, 1.0, ALU.mult, ALU.add))
                link(dve.scalar_tensor_tensor(out=nt1[:, s], in0=mv[:, s, 0], scalar=-(1 - P_SEM), in1=rstd[:, s],
                                              op0=ALU.mult, op1=ALU.mult))
                for t in range(4 * i, 4 * i + 4):
                    ins = dve.tensor_scalar(xres[:, t, :], xres[:, t, :], nt0[:, t:t + 1], nt1[:, t:t + 1],
                                            ALU.mult, ALU.add)
                link(ins)
                for t in range(4 * i, 4 * i + 4):
                    ins = dve.scalar_tensor_tensor(out=xres[:, t, :], in0=sig[:, t, :], scalar=P_SEM,
                                                   in1=xres[:, t, :], op0=ALU.mult, op1=ALU.add)
                link(ins)
            for i in range(2):
                norm_stats(i, 4 + i)
                normalise(i)
            for i in range(4, 8):
                rest_turned(i, i)

            def route():
                dve.wait_ge(gate_done, 1)
                dve.wait_ge(const_done, 2)
                link(dve.tensor_tensor(lg[:], bank[4][:, 0:T * 8].rearrange("p (t e) -> p t e", t=T)[:, :, 0:NR],
                                       brb[:, 0:1, :].to_broadcast([P, T, NR]), ALU.add))
                link(dve.tensor_tensor(bg[:], lg[:], brb[:, 1:2, :].to_broadcast([P, T, NR]), ALU.add))
                me = bg[:].unsqueeze(3).to_broadcast([P, T, NR, NR])
                other = bg[:].unsqueeze(2).to_broadcast([P, T, NR, NR])
                dve.tensor_tensor(gt[:], other, me, ALU.is_gt)
                link(dve.tensor_tensor(ge[:], other, me, ALU.is_ge))
                link(dve.tensor_tensor(ge[:].rearrange("p t a b -> p t (a b)"), ge[:].rearrange("p t a b -> p t (a b)"),
                                       earlier[:].rearrange("p a b -> p (a b)").unsqueeze(1).to_broadcast([P, T, NR * NR]),
                                       ALU.mult))
                link(dve.tensor_tensor(gt[:], gt[:], ge[:], ALU.max))
                link(dve.tensor_reduce(sel[:], gt[:], AX.X, ALU.add))
                link(dve.tensor_scalar(sel[:], sel[:], TOPK - 0.5, None, ALU.is_lt))
                link(dve.tensor_scalar(bg[:], sel[:], -NEG, NEG, ALU.mult, ALU.add))
                link(dve.tensor_tensor(lg[:], lg[:], sel[:], ALU.mult))
                link(dve.tensor_tensor(lg[:], lg[:], bg[:], ALU.add))
                link(dve.tensor_reduce(mx[:], lg[:], AX.X, ALU.max))
                dve.tensor_tensor(lg[:], lg[:], mx[:].unsqueeze(2).to_broadcast([P, T, NR]), ALU.subtract).then_inc(pexp_in, 1)
                dve.wait_ge(pexp_done, 1)
                link(dve.tensor_reduce(mx[:], lg[:], AX.X, ALU.add))
                link(dve.reciprocal(mx[:], mx[:]))
                dve.tensor_tensor(prob[:, :, 0:NR], lg[:], mx[:].unsqueeze(2).to_broadcast([P, T, NR]),
                                  ALU.mult).then_inc(prob_done, 1)

            def rest_expert(e, q):
                for j in range(3):
                    dve.wait_ge(ewh_done, 3 * e + j + 1)
                    dve.tensor_tensor(ewl[q][:, j, :, :].rearrange("p k d -> p (k d)"), ew_raw[q][:, j, :],
                                      f32(ewh[q][:, j, :, :].rearrange("p k d -> p (k d)")), ALU.subtract).then_inc(ewl_done, 1)

            def accumulate(e):
                for t in range(T):
                    dve.wait_ge(down_done, 4 * e + t // 2 + 1)
                    dve.scalar_tensor_tensor(out=xres[:, t, :], in0=bank[4 + t // 2][:, DM * (t % 2):DM * (t % 2 + 1)],
                                             scalar=prob[:, t, bass.ds(e, 1)], in1=xres[:, t, :],
                                             op0=ALU.mult, op1=ALU.add).then_inc(acc_done, 1)

            def expert(e, k, q):
                first, final = (isinstance(e, int) and e == i for i in (0, NE - 1))
                if first:
                    route()
                    rest_expert(0, 0)
                for v in range(4):
                    dve.wait_ge(up_read, 4 * e + v + 1)
                    at_least(dve, gate2_done, 4 * e)
                    dve.tensor_copy(uh[:, v, :], u32[:, v, :]).then_inc(uh_done, 1)
                if first:
                    dve.wait_ge(prob_turned, 1)
                    dve.tensor_copy(probT[:, 0:HALF], bank[4][0:NE, :]).then_inc(prob_read, 1)
                    dve.wait_ge(prob_turned, 2)
                    dve.tensor_copy(probT[:, HALF:2 * HALF], bank[5][0:NE, :]).then_inc(prob_read, 1)
                    for i in range(4):
                        dve.wait_ge(bdn_done, i + 1)
                        dve.tensor_tensor(xres[:, 2 * i:2 * i + 2, :].rearrange("p t d -> p (t d)"),
                                          bank[4 + i][:], xres[:, 2 * i:2 * i + 2, :].rearrange("p t d -> p (t d)"),
                                          ALU.add).then_inc(bdn_read, 1)
                    dve.wait_ge(bdn_read, 4)
                else:
                    accumulate(e - 1)
                if not final:
                    rest_expert(e + 1, 1 - q)
                for v in range(4):
                    dve.wait_ge(silu2_done, 4 * e + v + 1)
                    dve.tensor_tensor(e32[:, v, :], e32[:, v, :], u32[:, v, :], ALU.mult).then_inc(e_done, 1)

            over_experts(dve, expert)
            dve.wait_ge(acc_done, T * (NE - 1))
            accumulate(NE - 1)

        @block.tensor
        def _(pe):
            def three(dst, passes, n):
                for k in range(n):
                    for i, (left, right) in enumerate(passes(k)):
                        ins = pe.matmul(dst, left, right, start=(k == 0 and i == 0), stop=(k == n - 1 and i == 2))
                return ins

            def turn_w(m, k, q, waits):
                pe.wait_ge(w_in[q], 32 * (k + 1))
                waits()
                for j in range(2):
                    for d in range(KD):
                        c = (2 * j + d) * P
                        ins = pe.transpose(bank[6][:, c:c + P], w_raw[q][:, j, d * P:(d + 1) * P], ident[:])
                ins.then_inc(w_turned, 1)

            def project(m, q, u):
                j, h = u // 2, u % 2
                s = slice(HALF * h, HALF * (h + 1))
                if u == 0:
                    pe.wait_ge(wtl_done, m + 1)
                at_least(pe, tap_done, 3 * (4 * m + u - 1))
                three(bank[u % 2][:], lambda k: [(wth[q][:, j, k, :], uth[:, k, s]), (wth[q][:, j, k, :], utl[:, k, s]),
                                                 (wtl[q][:, j, k, :], uth[:, k, s])], KD).then_inc(proj_done, 1)

            def turn_tokens(i, b):
                h, k = i % 4 // 2, i % 2
                pe.wait_ge(xn_done, T * (i // 4) + 4 * (h + 1))
                for t in range(4):
                    ins = pe.transpose(bank[b][:, t * P:(t + 1) * P], xn[:, 4 * h + t, k * P:(k + 1) * P], ident[:])
                ins.then_inc(ut_turned, 1)

            pe.wait_ge(const_done, 1)
            turn_w(0, 0, 0, lambda: None)
            pe.wait_ge(wz_in, 32)
            for k in range(KD):
                for j in range(2):
                    pe.transpose(bank[4 + k][:, j * P:(j + 1) * P], wz_rawz[:, j, k * P:(k + 1) * P], ident[:])
                pe.transpose(bank[4 + k][:, DM:ZA], wz_rawa[:, k * P:(k + 1) * P], ident[0:NH, 0:NH]).then_inc(wz_turned, 1)
            for i in range(4):
                turn_tokens(i, i)
            turn_w(1, 0, 1, lambda: pe.wait_ge(wtl_done, 1))
            pe.wait_ge(utl_done, 4)
            for u in range(4):
                project(0, 0, u)
            pe.wait_ge(wzl_done, KD)
            for t in range(T):
                at_least(pe, za_read, 2 * (t - 1))
                s = slice(t * P, (t + 1) * P)
                three(bank[4 + t % 2][:, 0:ZA], lambda k: [(uth[:, k, s], wzh[:, k, :]), (uth[:, k, s], wzl[:, k, :]),
                                                           (utl[:, k, s], wzh[:, k, :])], KD).then_inc(za_done, 1)
            pe.wait_ge(tap_done, 12)
            for i in range(4):
                at_least(pe, x_read, i - 1)
                for t in range(2):
                    for c in range(2):
                        col = (2 * t + c) * P
                        ins = pe.transpose(bank[2 + i % 2][:, col:col + P],
                                           conv[0][:, c, (2 * i + t) * P:(2 * i + t + 1) * P], ident[:])
                ins.then_inc(x_turned, 1)
            pe.wait_ge(dt_done, 1)
            pe.wait_ge(const_done, 2)
            pe.matmul(bank[7][:, 0:T * NH], neg_tri[:], dts[:].rearrange("p t h -> p (t h)"), start=True, stop=True)
            pe.matmul(bank[7][:, T * NH:2 * T * NH], neg_ones[:], dts[:].rearrange("p t h -> p (t h)"),
                      start=True, stop=True).then_inc(cum_done, 1)
            for u in range(4):
                project(1, 1, u)
            turn_w(2, 1, 0, lambda: pe.wait_ge(wtl_done, 2))
            pe.wait_ge(wo_in, 16)
            for k in range(KD):
                for j in range(2):
                    c = (2 * k + j) * P
                    ins = pe.transpose(bank[4][:, c:c + P], wo_raw[:, j, k * P:(k + 1) * P], ident[:])
            ins.then_inc(misc_turned, 1)
            pe.wait_ge(cpart_done, 1)
            rows = bank[5][:].bitcast(BF16)
            for s in range(3):
                for c in range(2):
                    col = (2 * s + c) * P
                    ins = pe.transpose(rows[:, col:col + P], cparts[:, s, 16 * c:16 * c + 16, :].rearrange("p h t -> p (h t)"),
                                       ident_bf[:])
            ins.then_inc(cpart_turned, 1)
            pe.wait_ge(cpart_read, 1)
            pe.wait_ge(small_in, 12 * 16)
            for k in range(KD):
                ins = pe.transpose(bank[5][:, k * 2 * NE:(k + 1) * 2 * NE], b_rows[:, k * P:(k + 1) * P], ident[0:2 * NE, 0:2 * NE])
            ins.then_inc(misc_turned, 1)
            pe.wait_ge(ctx_sm_in, 32)
            pe.wait_ge(x_read, 4)
            for i in range(2):
                for t in range(4):
                    ins = pe.transpose(bank[2 + i][0:CTX, t * P:(t + 1) * P], ctx_raw[:, 4 * i + t, :], ident[:])
                ins.then_inc(misc_turned, 1)
            pe.wait_ge(misc_read, 4)
            pe.wait_ge(wj_done, 1)
            for i in range(2):
                pe.matmul(bank[4 + i][:], wj_rep[:], ctxT[:, HALF * i:HALF * (i + 1)], start=True, stop=True).then_inc(pair_done, 1)
            for t in range(T):
                ins = pe.matmul(bank[2][:, t:t + 1], ctxT[:, t * P:(t + 1) * P], wi_wj[:, 0:1], start=True, stop=True)
            ins.then_inc(pair_done, 1)
            pe.wait_ge(pair_read, 3)

            def weigh(n, q, u):
                a = 4 * (n - 1) + u
                j, h, b = u // 2, u % 2, u % 2
                pe.wait_ge(gl_done, a + 1)
                if u == 0:
                    pe.wait_ge(xp_lo, n)
                    at_least(pe, y_step, 4 * (n - 1) - 2)
                for i in range(4):
                    t = 4 * h + i
                    c = (2 * t + j) * 2 * HD
                    s = slice(i * P, (i + 1) * P)
                    pe.matmul(bank[7][:, c:c + 2 * HD], gh[b][:, s], xp[q][:, t, j, :, :].rearrange("p s d -> p (s d)"),
                              start=True, stop=False)
                    ins = pe.matmul(bank[7][:, c:c + HD], gl[b][:, s], xp[q][:, t, j, 0, :], start=False, stop=True)
                ins.then_inc(y_done, 1)

            def body(n, k, q):
                for u in range(4):
                    a = 4 * (n - 1) + u
                    j, h, b = u // 2, u % 2, u % 2
                    if u == 0:
                        pe.wait_ge(cum_in[q], 64 * (k + q))
                    at_least(pe, exp_done, a - 1)
                    pe.matmul(bank[4 + b][:], ident_bf[:], mask[:].rearrange("p i k -> p (i k)"), start=True, stop=False)
                    pe.matmul(bank[4 + b][:], cl[q][:, j, :], cr[q][:, j, 4 * h:4 * h + 4, :].rearrange("p t k -> p (t k)"),
                              start=False, stop=True).then_inc(expo_done, 1)
                    if u == 0:
                        pe.wait_ge(tap_done, 12 * (n + 1))
                    at_least(pe, g_done, a - 1)
                    r = slice(NS * j, NS * (j + 1))
                    for i in range(4):
                        s = slice((4 * h + i) * P, (4 * h + i + 1) * P)
                        ins = pe.matmul(bank[2 + b][:, i * P:(i + 1) * P], conv[q][r, 0, s], conv[q][r, 1, s],
                                        start=True, stop=True)
                    ins.then_inc(cb_done, 1)
                    if not last(n, 1):
                        project(n + 1, 1 - q, u)
                    if u == 0:
                        if not (isinstance(n, int) and n == 1):
                            weigh(n - 1, 1 - q, 3)
                        pe.wait_ge(wtl_done, min(n + 2, PAIRS + 1) if isinstance(n, int) else n + 2)
                        for i in range(NSEQ):
                            ins = pe.transpose(bank[6][:, i * P:(i + 1) * P], conv[q][:, 0, 2 * i * P:(2 * i + 1) * P], ident[:])
                        ins.then_inc(b_turned, 1)
                    else:
                        weigh(n, q, u - 1)
                    if u == 1:
                        pe.wait_ge(b_read, n)
                        pe.wait_ge(xs_done, n)
                        for i in range(NSEQ):
                            ins = pe.matmul(bank[6][:, i * 2 * HD:(i + 1) * 2 * HD], btok[:, i, :], xs[q][:, i, :],
                                            start=True, stop=True)
                        ins.then_inc(st_done, 1)
                    if u == 2:
                        pe.wait_ge(st_read, 2 * n)
                        if not last(n, 2):
                            turn_w(n + 2, k + 1, q, lambda: None)
                    if u == 3:
                        for i in range(NSEQ):
                            c = 256 + i * 2 * HD
                            ins = pe.matmul(bank[7][:, c:c + 2 * HD], conv[q][:, 1, (2 * i + 1) * P:(2 * i + 2) * P],
                                            state[:, i, :, :].rearrange("p j d -> p (j d)"), start=True, stop=True)
                        ins.then_inc(inter_done, 1)

            over_pairs(pe, body)
            weigh(PAIRS, 0, 3)

            def turn_yz(t):
                pe.wait_ge(yz_done, t + 1)
                at_least(pe, yz_read, t - 1)
                for k in range(KD):
                    ins = pe.transpose(bank[t % 2][:, k * P:(k + 1) * P], y[:, t, k * P:(k + 1) * P], ident[:])
                ins.then_inc(yz_turned, 1)

            turn_yz(0)
            for t in range(T):
                if t + 1 < T:
                    turn_yz(t + 1)
                pe.wait_ge(yz_read, t + 1)
                at_least(pe, o_read, t - 1)
                for k in range(KD):
                    ins = pe.matmul(bank[2 + t % 2][:, 0:DM], yzT[t % 2][:, k * P:(k + 1) * P], woT[:, k, :],
                                    start=(k == 0), stop=(k == KD - 1))
                ins.then_inc(o_done, 1)
            for i in range(4, 8):
                turn_tokens(i, i)
            pe.wait_ge(utl_done, 8)
            pe.wait_ge(wr_done, 1)
            for t in range(T):
                s = slice(t * P, (t + 1) * P)
                ins = three(bank[4][:, t * 8:(t + 1) * 8],
                            lambda k: [(uth[:, k, s], wrh[:, k, :]), (uth[:, k, s], wrl[:, k, :]),
                                       (utl[:, k, s], wrh[:, k, :])], KD)
            ins.then_inc(gate_done, 1)

            def up(e, q):
                pe.wait_ge(ewl_done, 3 * (e + 1))
                for v in range(4):
                    n, m = v // 2, v % 2
                    s = slice(HALF * n, HALF * (n + 1))
                    c = slice(P * m, P * (m + 1))
                    at_least(pe, silu2_done, 4 * (e - 1) + v + 1)
                    three(bank[v][:], lambda k: [(ewh[q][:, 0, k, c], uth[:, k, s]), (ewh[q][:, 0, k, c], utl[:, k, s]),
                                                 (ewl[q][:, 0, k, c], uth[:, k, s])], KD).then_inc(up_done, 1)

            def gate(e, q):
                for v in range(4):
                    n, m = v // 2, v % 2
                    c = slice(P * m, P * (m + 1))
                    pe.wait_ge(up_read, 4 * e + v + 1)
                    if m == 0:
                        pe.wait_ge(ul_done, 4 * e + 2 * n + 2)
                    three(bank[v][:], lambda k: [(ewh[q][:, 1, k, c], uh[:, 2 * n + k, :]),
                                                 (ewh[q][:, 1, k, c], ul[:, 2 * n + k, :]),
                                                 (ewl[q][:, 1, k, c], uh[:, 2 * n + k, :])], KD).then_inc(gate2_done, 1)

            def down(e, q):
                for t in range(T):
                    n = t // 4
                    if t % 4 == 0:
                        pe.wait_ge(el_done, 4 * e + 2 * n + 2)
                    if t % 2 == 0:
                        at_least(pe, acc_done, T * (e - 1) + t + 2)
                    s = slice((t % 4) * P, (t % 4 + 1) * P)
                    ins = three(bank[4 + t // 2][:, DM * (t % 2):DM * (t % 2 + 1)],
                                lambda k: [(eh[:, 2 * n + k, s], ewh[q][:, 2, k, :]), (eh[:, 2 * n + k, s], ewl[q][:, 2, k, :]),
                                           (el[:, 2 * n + k, s], ewh[q][:, 2, k, :])], KD)
                    if t % 2:
                        ins.then_inc(down_done, 1)

            def expert(e, k, q):
                up(e, q)
                if isinstance(e, int) and e == 0:
                    pe.wait_ge(prob_done, 1)
                    for i in range(2):
                        for t in range(4):
                            ins = pe.transpose(bank[4 + i][0:NE, t * P:(t + 1) * P], prob[:, 4 * i + t, :], ident[:])
                        ins.then_inc(prob_turned, 1)
                    pe.wait_ge(prob_read, 2)
                    for i in range(4):
                        for t in range(2):
                            tt = 2 * i + t
                            ins = pe.matmul(bank[4 + i][:, DM * t:DM * (t + 1)], probT[:, tt * P:(tt + 1) * P], bd[:],
                                            start=True, stop=True)
                        ins.then_inc(bdn_done, 1)
                else:
                    pe.wait_ge(bdn_read, 4)
                    down(e - 1, 1 - q)
                gate(e, q)

            over_experts(pe, expert)
            down(NE - 1, 1)


_INS = ['x', 'ctx_512', 'L0_attn_W_in', 'L0_attn_conv_w', 'L0_attn_conv_b', 'L0_attn_D', 'L0_attn_z_bias',
        'L0_attn_W_out', 'L0_xattn_W', 'L0_xattn_b', 'L0_ffn_Wr', 'L0_ffn_br', 'L0_ffn_gate_bias', 'L0_ffn_Wup',
        'L0_ffn_bup', 'L0_ffn_Wgate', 'L0_ffn_bgate', 'L0_ffn_Wdown', 'L0_ffn_bdown', 'L0_ffn_Wsu', 'L0_ffn_bsu',
        'L0_ffn_Wsg', 'L0_ffn_bsg', 'L0_ffn_Wsd', 'L0_ffn_bsd']
_OUTS = [((NSEQ, SEQ, DM), 'float32')]


def kernel(**inputs):
    import numpy as _np
    import concourse.bacc as _bacc
    from concourse import mybir as _mybir
    from concourse.bass_utils import run_bass_kernel_spmd as _run

    nc = _bacc.Bacc("TRN2", target_bir_lowering=False, num_devices=1)
    arrays, args = {}, []
    for name in _INS:
        a = _np.ascontiguousarray(inputs[name])
        arrays[f"in_{name}_dram"] = a
        args.append(nc.dram_tensor(f"in_{name}_dram", a.shape, _mybir.dt.from_np(a.dtype), kind="ExternalInput").ap())
    for i, (shape, dtype) in enumerate(_OUTS):
        dt = _mybir.dt.from_np(_np.dtype(dtype))
        args.append(nc.dram_tensor(f"out_{i}_dram", shape, dt, kind="ExternalOutput").ap())
    decoder_layer(nc, *args)
    r = _run(nc, [arrays], core_ids=[0])
    got = tuple(r.results[0][f"out_{i}_dram"] for i in range(len(_OUTS)))
    return got[0]
```

```python
from contextlib import ExitStack

import concourse.bass as bass
from concourse import mybir

P = 128
F32 = mybir.dt.float32
F32R = mybir.dt.float32r
I32 = mybir.dt.int32
BF16 = mybir.dt.bfloat16
ALU = mybir.AluOpType
ACT = mybir.ActivationFunctionType
AX = mybir.AxisListType

NSEQ, SEQ, DM = 4, 256, 256
T = NSEQ * SEQ // P
HALF = 512
KD = DM // P
NH, HD, NS = 32, 8, 64
PAIRS = NH // 2
TAPS = 4
C_X, C_B = 0, DM
C_C = C_B + NH * NS
C_Z = C_C + NH * NS
C_A = C_Z + DM
ZA = DM + NH
NE = 8
NR = 7
TOPK = 2
EPS = 1e-5
ROOT_GUESS = 0x5F3759DF
P_SEM = 0.6
NEG = -1e30
CTX = 64
BLOCK = 16
STEP0, STEPS = 32, P // BLOCK - 1


def decoder_layer(nc, x, ctx_in, W_in, conv_w, conv_b, D, z_bias, W_out, xw, xb, Wr, br, gate_bias,
                  Wup, bup, Wgate, bgate, Wdown, bdown, Wsu, bsu, Wsg, bsg, Wsd, bsd, out):
    x_v = x.rearrange("b (c p) d -> p (b c) d", p=P)
    out_v = out.rearrange("b (c p) d -> p (b c) d", p=P)
    ctx_v = ctx_in.rearrange("b (c p) d -> p (b c) d", p=P)
    cum_dram = nc.dram_tensor("cum_dram", (3, NH * T, P), BF16, kind="Internal").ap()

    with ExitStack() as stack:
        def sb(name, shape, dt=F32):
            return stack.enter_context(nc.sbuf_tensor(name, shape, dt))

        def sem(name):
            return stack.enter_context(nc.semaphore(name))

        bank = [stack.enter_context(nc.psum_tensor(f"bank{i}", [P, HALF], F32)) for i in range(8)]

        ident = sb("ident", [P, P])
        neg_tri = sb("neg_tri", [P, P])
        neg_ones = sb("neg_ones", [P, P])
        causal = sb("causal", [P, P])
        earlier = sb("earlier", [P, NR, NR])
        xres = sb("xres", [P, T, DM])
        stats = sb("stats", [P, 2 * T, 6])
        mv = sb("mv", [P, 2 * T, 2])
        var = sb("var", [P, 2 * T])
        bits = sb("bits", [P, 2 * T], I32)
        rstd = sb("rstd", [P, 2 * T])
        nt0 = sb("nt0", [P, 2 * T])
        nt1 = sb("nt1", [P, 2 * T])
        shift = sb("shift", [P, T])
        uth = sb("uth", [P, KD, T * P], F32R)
        utl = sb("utl", [P, KD, T * P], F32R)
        xtok = sb("xtok", [P, T, DM])
        xsd = sb("xsd", [P, NSEQ, DM])
        y = sb("y", [P, T, DM])
        z = sb("z", [P, T, DM])
        sig = sb("sig", [P, T, DM])
        a_log = sb("a_log", [P, T, NH])
        neg_abs = sb("neg_abs", [P, T, NH])
        dts = sb("dts", [P, NH, T])
        cum = sb("cum", [P, NH, T])
        cumT = sb("cumT", [P, 2, P])
        cpartsT = sb("cpartsT", [P, 3, 2, P], BF16)
        ecum = sb("ecum", [P, NSEQ, NH])
        sdec = sb("sdec", [P, NSEQ, NH])
        w_raw = [sb(f"w_raw{i}", [P, 2, DM]) for i in range(2)]
        parts = sb("parts", [P, 8, HALF], F32R)
        wth = [parts[:, i, :].rearrange("p (a k c) -> p a k c", a=2, k=KD) for i in range(2)]
        wtl = [parts[:, 2 + i, :].rearrange("p (a k c) -> p a k c", a=2, k=KD) for i in range(2)]
        conv = [sb(f"conv{i}", [P, 2, T * P]) for i in range(2)]
        taps = [sb(f"taps{i}", [P, 2, TAPS]) for i in range(2)]
        tap_b = [sb(f"tap_b{i}", [P, 2]) for i in range(2)]
        cl = [sb(f"cl{i}", [STEP0 + STEPS, 2, P], BF16) for i in range(2)]
        cr = [sb(f"cr{i}", [STEP0 + STEPS, 2, T, P], BF16) for i in range(2)]
        dec = [sb(f"dec{i}", [P, HALF]) for i in range(2)]
        g = [sb(f"g{i}", [P, HALF]) for i in range(2)]
        xp = [sb(f"xp{i}", [P, T, 2, HD]) for i in range(2)]
        xs = [sb(f"xs{i}", [P, NSEQ, 2 * HD]) for i in range(2)]
        btok = sb("btok", [P, NSEQ, P])
        state = sb("state", [P, NSEQ, 2, HD])
        yint = sb("yint", [P, NSEQ, 2, HD])
        wzh = sb("wzh", [P, KD, ZA], F32R)
        wzl = sb("wzl", [P, KD, ZA], F32R)
        zb = sb("zb", [P, DM])
        db = sb("db", [P, NH])
        woT = sb("woT", [P, KD, DM])
        yzT = [sb(f"yzT{i}", [P, DM]) for i in range(2)]
        wi_wj = sb("wi_wj", [CTX, 2])
        wj_rep = sb("wj_rep", [CTX, P])
        xbb = sb("xbb", [P, 1])
        si = sb("si", [P, T])
        ew_raw = [sb(f"ew_raw{i}", [P, 3, KD * DM]) for i in range(2)]
        ewh = [sb(f"ewh{i}", [P, 3, KD, DM], F32R) for i in range(2)]
        ewl = [sb(f"ewl{i}", [P, 3, KD, DM], F32R) for i in range(2)]
        uh = sb("uh", [P, 4, HALF], F32R)
        ul = sb("ul", [P, 4, HALF], F32R)
        eh = parts[:, 0:4, :]
        el = parts[:, 4:8, :]
        b_rows = sb("b_rows", [2 * NE, DM])
        b_cols = sb("b_cols", [P, NE, 2, KD])
        eb = [sb(f"eb{i}", [P, 2, KD]) for i in range(2)]
        bd = sb("bd", [NE, DM])
        wr_raw = sb("wr_raw", [P, KD, 8])
        wrh = sb("wrh", [P, KD, 8], F32R)
        wrl = sb("wrl", [P, KD, 8], F32R)
        brb = sb("brb", [P, 2, NR])
        lg = sb("lg", [P, T, NR])
        bg = sb("bg", [P, T, NR])
        gt = sb("gt", [P, T, NR, NR])
        ge = sb("ge", [P, T, NR, NR])
        sel = sb("sel", [P, T, NR])
        mx = sb("mx", [P, T])
        prob = sb("prob", [P, T, NE])
        probT = sb("probT", [NE, T * P])
        lgT = probT
        u32 = conv[0][:].rearrange("p a (b n) -> p (a b) n", n=HALF)
        e32 = conv[1][:].rearrange("p a (b n) -> p (a b) n", n=HALF)
        xn = y
        wz_rawz = ew_raw[0][:, 0, :].rearrange("p (a d) -> p a d", a=2)
        wz_rawa = ew_raw[0][0:NH, 1, 0:DM]
        wo_raw = ew_raw[0][:, 2, :].rearrange("p (a d) -> p a d", a=2)
        ctx_raw = ew_raw[1][:, 0, :].rearrange("p (t d) -> p t d", t=T)
        ctxT = ew_raw[1][0:CTX, 1:3, :].rearrange("p a n -> p (a n)")

        def f32(ap):
            return ap.bitcast(F32)

        def zgate(t):
            flat = (ew_raw[1], w_raw[1])[t // 6][:].rearrange("p a d -> p (a d)")
            return flat[:, DM * (t % 6):DM * (t % 6 + 1)]

        x_in = [sem(f"x_in{i}") for i in range(2)]
        w_in = [sem(f"w_in{i}") for i in range(2)]
        taps_in = [sem(f"taps_in{i}") for i in range(2)]
        cum_in = [sem(f"cum_in{i}") for i in range(2)]
        ew_in = [sem(f"ew_in{i}") for i in range(2)]
        wz_in, wo_in, ctx_sm_in = sem("wz_in"), sem("wo_in"), sem("ctx_sm_in")
        small_in = sem("small_in")
        cum_out, y_out = sem("cum_out"), sem("y_out")
        const_chain, const_done = sem("const_chain"), sem("const_done")
        dve_chain, act_chain = sem("dve_chain"), sem("act_chain")
        norm_done, xn_done, xn2_done = sem("norm_done"), sem("xn_done"), sem("xn2_done")
        ut_turned, uth_done, utl_done = sem("ut_turned"), sem("uth_done"), sem("utl_done")
        w_turned, wth_done, wtl_done = sem("w_turned"), sem("wth_done"), sem("wtl_done")
        wz_turned, wzh_done, wzl_done = sem("wz_turned"), sem("wzh_done"), sem("wzl_done")
        za_done, za_read = sem("za_done"), sem("za_read")
        nabs_done, sp_done, dt_done = sem("nabs_done"), sem("sp_done"), sem("dt_done")
        cum_done, cum_read, cexp_done = sem("cum_done"), sem("cum_read"), sem("cexp_done")
        cumT_done, cpart_done = sem("cumT_done"), sem("cpart_done")
        x_turned, x_read, y_init, z_ready = sem("x_turned"), sem("x_read"), sem("y_init"), sem("z_ready")
        misc_turned, misc_read, wj_done = sem("misc_turned"), sem("misc_read"), sem("wj_done")
        ctx_turned, ctx_read = sem("ctx_turned"), sem("ctx_read")
        pair_done, pair_read = sem("pair_done"), sem("pair_read")
        proj_done, acc_first, tap_done = sem("proj_done"), sem("acc_first"), sem("tap_done")
        expo_done, exp_done, cb_done = sem("expo_done"), sem("exp_done"), sem("cb_done")
        g_done, masked, y_done = sem("g_done"), sem("masked"), sem("y_done")
        b_turned, b_read, st_done, st_read = sem("b_turned"), sem("b_read"), sem("st_done"), sem("st_read")
        inter_done, y_step = sem("inter_done"), sem("y_step")
        eb_done = sem("eb_done")
        xp_done = sem("xp_done")
        sig_done, sig_scaled = sem("sig_done"), sem("sig_scaled")
        ztanh_done, zgate_done, z_gated = sem("ztanh_done"), sem("zgate_done"), sem("z_gated")
        lg_done, lgT_read = sem("lg_done"), sem("lgT_read")
        yz_done, yz_turned, yz_read = sem("yz_done"), sem("yz_turned"), sem("yz_read")
        o_done, o_read = sem("o_done"), sem("o_read")
        wr_done, gate_done, pexp_in, pexp_done = sem("wr_done"), sem("gate_done"), sem("pexp_in"), sem("pexp_done")
        prob_done, prob_turned, prob_read = sem("prob_done"), sem("prob_turned"), sem("prob_read")
        bdn_done, bdn_read = sem("bdn_done"), sem("bdn_read")
        ewh_done, ewl_done = sem("ewh_done"), sem("ewl_done")
        up_done, up_read, uh_done, ul_done = sem("up_done"), sem("up_read"), sem("uh_done"), sem("ul_done")
        gate2_done, silu2_done, e_done = sem("gate2_done"), sem("silu2_done"), sem("e_done")
        eh_done, el_done, down_done, acc_done = sem("eh_done"), sem("el_done"), sem("down_done"), sem("acc_done")

        def at_least(eng, s, n):
            if not isinstance(n, int) or n > 0:
                eng.wait_ge(s, n)

        def over_pairs(eng, body):
            body(1, 0, 1)
            with eng.Fori(1, PAIRS // 2 - 1) as k:
                body(2 * k, k, 0)
                body(2 * k + 1, k, 1)
            for n in range(PAIRS - 2, PAIRS + 1):
                body(n, n // 2, n % 2)

        def last(n, ahead):
            return isinstance(n, int) and n + ahead > PAIRS

        def over_experts(eng, body):
            for e in range(2):
                body(e, e // 2, e % 2)
            with eng.Fori(1, NE // 2 - 1) as k:
                body(2 * k, k, 0)
                body(2 * k + 1, k, 1)
            for e in range(NE - 2, NE):
                body(e, e // 2, e % 2)

        block = stack.enter_context(nc.Block())

        @block.sync
        def _(sp):
            def rows(w, m):
                if isinstance(m, int) and m == 0:
                    return w[C_X:C_B].rearrange("(j r) ... -> r j ...", j=2)
                return w[C_B:C_Z].rearrange("(j r) ... -> r j ...", j=2)[bass.ds(P * (m - 1), P)]

            def load_w(m, q):
                at_least(sp, w_turned, m - 1)
                sp.dma_start(w_raw[q][:], rows(W_in, m)).then_inc(w_in[q], 16)

            def load_taps(m, q):
                at_least(sp, tap_done, 12 * (m - 1))
                sp.dma_start(taps[q][:], rows(conv_w, m)).then_inc(taps_in[q], 16)
                for j in range(2):
                    sp.dma_start(tap_b[q][:, j:j + 1], rows(conv_b.unsqueeze(1), m)[:, j, :]).then_inc(taps_in[q], 16)

            def load_cum(m, q):
                at_least(sp, expo_done, 4 * (m - 2))
                for s in range(3):
                    sp.dma_start(cl[q][T * s:T * s + T, :, :],
                                 cum_dram[s, bass.ds(2 * T * (m - 1), 2 * T), :]
                                 .rearrange("(j t) k -> t j k", j=2)).then_inc(cum_in[q], 16)
                sp.dma_start(cr[q][24:27, :, :, :].rearrange("s j t k -> s (j t k)"),
                             cum_dram[:, bass.ds(2 * T * (m - 1), 2 * T), :]
                             .rearrange("s r k -> s (r k)")).then_inc(cum_in[q], 16)

            for i in range(2):
                sp.dma_start(xres[:, 4 * i:4 * i + 4, :], x_v[:, 4 * i:4 * i + 4, :]).then_inc(x_in[i], 16)
            load_w(0, 0)
            sp.dma_start(wz_rawz, W_in[C_Z:C_Z + DM, :].rearrange("(a p) d -> p a d", p=P)).then_inc(wz_in, 16)
            sp.dma_start(wz_rawa, W_in[C_A:C_A + NH, :]).then_inc(wz_in, 16)
            load_w(1, 1)
            load_taps(0, 0)
            load_taps(1, 1)
            sp.dma_start(wo_raw, W_out.rearrange("(a p) d -> p a d", p=P)).then_inc(wo_in, 16)
            sp.dma_start(ctx_raw, ctx_v).then_inc(ctx_sm_in, 16)
            with nc.allow_non_contiguous_dma(reason="128 values"):
                sp.dma_start(wi_wj[:], xw.rearrange("a (j p) -> p (a j)", j=2)).then_inc(ctx_sm_in, 16)
            sp.dma_start(db[:], D.partition_broadcast(P)).then_inc(small_in, 16)
            sp.dma_start(zb[:], z_bias.partition_broadcast(P)).then_inc(small_in, 16)
            sp.dma_start(xbb[:], xb.partition_broadcast(P)).then_inc(small_in, 16)
            load_w(2, 0)
            for dst, src in ((b_rows[0:NR, :], bup), (b_rows[NR:NE, :], bsu.unsqueeze(0)),
                             (b_rows[NE:NE + NR, :], bgate), (b_rows[NE + NR:2 * NE, :], bsg.unsqueeze(0)),
                             (bd[0:NR, :], bdown), (bd[NR:NE, :], bsd.unsqueeze(0)),
                             (brb[:, 0, :], br.partition_broadcast(P)), (brb[:, 1, :], gate_bias.partition_broadcast(P)),
                             (wr_raw[:, :, 0:NR], Wr.rearrange("(k p) e -> p k e", p=P))):
                sp.dma_start(dst, src).then_inc(small_in, 16)
            load_w(3, 1)
            load_taps(2, 0)
            sp.wait_ge(cpart_done, 1)
            sp.dma_start(cum_dram.rearrange("s (c p) k -> p s c k", p=P), cpartsT[:]).then_inc(cum_out, 16)
            sp.wait_ge(cum_out, 16)
            sp.wait_ge(const_done, 2)
            load_cum(1, 1)
            sp.wait_ge(const_done, 3)

            def body(n, k, q):
                if not last(n, 1):
                    load_cum(n + 1, 1 - q)
                if not last(n, 3):
                    load_w(n + 3, 1 - q)
                if not last(n, 2):
                    load_taps(n + 2, q)

            over_pairs(sp, body)

            def load_expert(e, q):
                at_least(sp, ewl_done, 3 * (e - 1))
                for j, w in enumerate((Wup, Wgate, Wdown)):
                    sp.dma_start(ew_raw[q][:, j, :].rearrange("p (k d) -> p k d", k=KD),
                                 w[bass.ds(e, 1), :, :].rearrange("e (k p) d -> p (e k) d", p=P)).then_inc(ew_in[q], 16)

            load_expert(0, 0)
            sp.wait_ge(z_gated, T)
            load_expert(1, 1)
            with sp.Fori(1, 3) as k:
                load_expert(2 * k, 0)
                load_expert(2 * k + 1, 1)
            load_expert(6, 0)
            at_least(sp, ewl_done, 3 * (NE - 2))
            for j, w in enumerate((Wsu, Wsg, Wsd)):
                sp.dma_start(ew_raw[1][:, j, :].rearrange("p (k d) -> p k d", k=KD),
                             w.rearrange("(k p) d -> p k d", p=P)).then_inc(ew_in[1], 16)
            for i in range(4):
                sp.wait_ge(acc_done, T * (NE - 1) + 2 * i + 2)
                sp.dma_start(out_v[:, 2 * i:2 * i + 2, :], xres[:, 2 * i:2 * i + 2, :]).then_inc(y_out, 16)
            sp.wait_ge(y_out, 64)

        @block.gpsimd
        def _(pool):
            steps = [0]

            def link(ins):
                steps[0] += 1
                ins.then_inc(const_chain, 1)
                pool.wait_ge(const_chain, steps[0])

            link(pool.memset(ident[:], 0.0))
            pool.affine_select(out=ident[:], in_=ident[:], compare_op=ALU.not_equal, fill=1.0,
                               base=0, pattern=[[-1, P]], channel_multiplier=1).then_inc(const_done, 1)
            link(pool.memset(neg_ones[:], -1.0))
            link(pool.affine_select(out=neg_tri[:], in_=neg_ones[:], compare_op=ALU.is_ge, fill=0.0,
                                    base=0, pattern=[[1, P]], channel_multiplier=-1))
            link(pool.memset(earlier[:], 1.0))
            link(pool.affine_select(out=earlier[:], in_=earlier[:], compare_op=ALU.is_gt, fill=0.0,
                                    base=0, pattern=[[1, NR], [-1, NR]], channel_multiplier=0))
            link(pool.memset(state[:], 0.0))
            link(pool.memset(prob[:], 1.0))
            link(pool.memset(causal[:], 1.0))
            link(pool.affine_select(out=causal[:], in_=causal[:], compare_op=ALU.is_ge, fill=0.0,
                                    base=0, pattern=[[1, P]], channel_multiplier=-1))
            for q in (1, 0):
                link(pool.memset(cl[q][:], 1.0))
                link(pool.memset(cr[q][0:STEP0, :, :, :], 0.0))
                link(pool.memset(cr[q][STEP0:STEP0 + STEPS, :, :, :], NEG))
                link(pool.affine_select(out=cl[q][STEP0:STEP0 + STEPS, :, :], in_=cl[q][STEP0:STEP0 + STEPS, :, :],
                                        compare_op=ALU.is_ge, fill=0.0, base=-BLOCK,
                                        pattern=[[0, 2], [1, P]], channel_multiplier=-BLOCK))
                step = cr[q][STEP0:STEP0 + STEPS, :, :, :]
                link(pool.affine_select(out=step, in_=step, compare_op=ALU.is_ge, fill=0.0, base=0,
                                        pattern=[[0, 2], [0, T], [1, P]], channel_multiplier=-BLOCK))
                link(pool.affine_select(out=step, in_=step, compare_op=ALU.is_ge, fill=0.0, base=BLOCK - 1,
                                        pattern=[[0, 2], [0, T], [-1, P]], channel_multiplier=BLOCK))
                rows = cr[q][0:STEP0, :, :, :]
                for s in range(3):
                    last_one = pool.affine_select(out=rows, in_=rows, compare_op=ALU.not_equal, fill=-1.0, base=-T * s,
                                                  pattern=[[0, 2], [-1, T], [0, P]], channel_multiplier=1)
                    if s < 2:
                        link(last_one)
                last_one.then_inc(const_done, 1)

            def prepare(m, q):
                c0 = 2 * HD * (m - 1)
                pool.tensor_copy(xp[q][:].rearrange("p t j d -> p t (j d)"), xtok[:, :, bass.ds(c0, 2 * HD)])
                pool.tensor_copy(xs[q][:], xsd[:, :, bass.ds(c0, 2 * HD)]).then_inc(xp_done, 1)

            def by_head(ap):
                return ap.rearrange("p (h d) -> p h d", h=NH)

            pool.wait_ge(x_read, 4)
            pool.wait_ge(cexp_done, 2)
            for b in range(NSEQ):
                ins = pool.tensor_tensor(by_head(xsd[:, b, :]), by_head(xtok[:, 2 * b, :]),
                                         sdec[:, b, :].unsqueeze(2).to_broadcast([P, NH, HD]), ALU.mult)
            link(ins)
            prepare(1, 1)
            pool.wait_ge(small_in, 12 * 16)
            for t in range(T):
                ins = pool.tensor_tensor(by_head(y[:, t, :]), by_head(xtok[:, t, :]),
                                         db[:].unsqueeze(2).to_broadcast([P, NH, HD]), ALU.mult)
            ins.then_inc(y_init, 1)
            pool.wait_ge(za_read, 2 * T)
            pool.tensor_tensor(z[:], z[:], zb[:].unsqueeze(1).to_broadcast([P, T, DM]), ALU.add).then_inc(z_ready, 1)

            def body(n, k, q):
                for u in range(4):
                    pool.wait_ge(g_done, 4 * (n - 1) + u + 1)
                    g_v = g[u % 2][:].rearrange("p (i k) -> p i k", k=P)
                    pool.tensor_tensor(g_v, g_v, causal[:].unsqueeze(1).to_broadcast([P, 4, P]),
                                       ALU.mult).then_inc(masked, 1)
                    if isinstance(n, int) and n == PAIRS - 1:
                        for t in (2 * u, 2 * u + 1):
                            pool.wait_ge(zgate_done, t + 1)
                            pool.tensor_tensor(z[:, t, :], z[:, t, :], zgate(t), ALU.mult).then_inc(z_gated, 1)
                    if u == 1 and not last(n, 1):
                        at_least(pool, y_done, 4 * (n - 1))
                        prepare(n + 1, 1 - q)
                if isinstance(n, int) and n == PAIRS:
                    pool.wait_ge(sig_done, T)
                    pool.tensor_scalar(sig[:], sig[:], P_SEM / 2, P_SEM / 2, ALU.mult, ALU.add).then_inc(sig_scaled, 1)

            over_pairs(pool, body)

            def expert(e, k, q):
                if isinstance(e, int) and e == 0:
                    pool.wait_ge(misc_read, 2)
                pool.tensor_copy(eb[q][:], b_cols[:, bass.ds(e, 1), :, :].rearrange("p e a k -> p (e a) k")).then_inc(eb_done, 1)
                for v in range(4):
                    pool.wait_ge(uh_done, 4 * e + v + 1)
                    pool.tensor_tensor(ul[:, v, :], u32[:, v, :], f32(uh[:, v, :]),
                                       ALU.subtract).then_inc(ul_done, 1)
                for v in range(4):
                    pool.wait_ge(eh_done, 4 * e + v + 1)
                    pool.tensor_tensor(el[:, v, :], e32[:, v, :], f32(eh[:, v, :]),
                                       ALU.subtract).then_inc(el_done, 1)

            over_experts(pool, expert)

        @block.scalar
        def _(act):
            steps = [0]

            def link(ins):
                steps[0] += 1
                ins.then_inc(act_chain, 1)
                act.wait_ge(act_chain, steps[0])

            def split_turned(i, b):
                h, k = i % 4 // 2, i % 2
                act.wait_ge(ut_turned, i + 1)
                act.copy(uth[:, k, HALF * h:HALF * (h + 1)], bank[b][:]).then_inc(uth_done, 1)

            def split_w(m, q):
                act.wait_ge(w_turned, m + 1)
                at_least(act, proj_done, 4 * (m - 1))
                act.copy(parts[:, q, :], bank[6][:]).then_inc(wth_done, 1)

            def first_tap(m, k, q, u):
                act.wait_ge(proj_done, 4 * m + u + 1)
                if u == 0:
                    act.wait_ge(taps_in[q], 48 * (k + 1))
                j, h = u // 2, u % 2
                act.activation(conv[q][:, j, HALF * h:HALF * (h + 1)], bank[u % 2][:], ACT.Identity,
                               bias=tap_b[q][:, j:j + 1], scale=taps[q][:, j, TAPS - 1:TAPS]).then_inc(acc_first, 1)

            def normalise(c, tiles, rounds):
                act.wait_ge(norm_done, rounds)
                for i, t in enumerate(tiles):
                    act.activation(xn[:, t, :], xres[:, t, :], ACT.Identity, bias=nt1[:, c + i:c + i + 1],
                                   scale=rstd[:, c + i:c + i + 1]).then_inc(xn2_done, 1)

            def evacuate_za(t):
                act.wait_ge(za_done, t + 1)
                b = bank[2 + t % 4]
                act.copy(a_log[:, t, :], b[:, DM:ZA]).then_inc(za_read, 1)
                act.copy(z[:, t, :], b[:, 0:DM]).then_inc(za_read, 1)

            split_w(0, 0)
            for k in range(KD):
                act.wait_ge(wz_turned, k + 1)
                act.copy(wzh[:, k, :], bank[4 + k][:, 0:ZA]).then_inc(wzh_done, 1)
            normalise(4, range(4, 8), 1)
            for i in range(4):
                split_turned(i, i)
            split_w(1, 1)
            first_tap(0, 0, 0, 0)
            first_tap(0, 0, 0, 1)
            for t in range(4):
                evacuate_za(t)
            first_tap(0, 0, 0, 2)
            for t in range(4, 8):
                evacuate_za(t)
            act.wait_ge(nabs_done, 1)
            link(act.activation(neg_abs[:], neg_abs[:], ACT.Exp))
            first_tap(0, 0, 0, 3)
            act.activation(neg_abs[:], neg_abs[:], ACT.Ln, bias=1.0).then_inc(sp_done, 1)
            for i in range(2):
                act.wait_ge(ctx_turned, i + 1)
                act.copy(ctxT[:, HALF * i:HALF * (i + 1)], bank[(4, 7)[i]][0:CTX, :]).then_inc(ctx_read, 1)
            first_tap(1, 0, 1, 0)
            for i in range(2):
                act.wait_ge(x_turned, i + 1)
                act.copy(xtok[:, 2 * i:2 * i + 2, :].rearrange("p t d -> p (t d)"), bank[2 + i % 2][:]).then_inc(x_read, 1)
            act.wait_ge(misc_turned, 1)
            act.copy(b_cols[:].rearrange("p e a k -> p k a e"),
                     bank[6][:, 0:KD * 2 * NE].rearrange("p (k a e) -> p k a e", k=KD, a=2)).then_inc(misc_read, 1)
            first_tap(1, 0, 1, 1)
            for i in range(2, 4):
                act.wait_ge(x_turned, i + 1)
                act.copy(xtok[:, 2 * i:2 * i + 2, :].rearrange("p t d -> p (t d)"), bank[2 + i % 2][:]).then_inc(x_read, 1)
            first_tap(1, 0, 1, 2)
            act.wait_ge(cum_read, 1)
            act.activation(ecum[:], cum[:].rearrange("p h (b c) -> p b c h", c=2)[:, :, 1, :], ACT.Exp).then_inc(cexp_done, 1)
            act.activation(sdec[:], sdec[:], ACT.Exp).then_inc(cexp_done, 1)
            first_tap(1, 0, 1, 3)
            for i in range(2):
                act.wait_ge(pair_done, i + 1)
                act.copy(sig[:].rearrange("p (b c) d -> p b c d", c=2)[:, 2 * i:2 * i + 2, 0, :],
                         bank[2 + i][:].rearrange("p (b d) -> p b d", b=2)).then_inc(pair_read, 1)
            act.wait_ge(pair_done, 3)
            link(act.activation(si[:], bank[6][:, 0:T], ACT.Identity, bias=xbb[:, 0:1]))
            act.activation(si[:], si[:], ACT.Identity, scale=0.5).then_inc(pair_read, 1)
            split_w(2, 0)
            act.wait_ge(misc_turned, 2)
            act.copy(woT[:].rearrange("p k d -> p (k d)"), bank[5][:]).then_inc(misc_read, 1)

            def gate_of_z(u):
                act.wait_ge(z_ready, 1)
                for t in (2 * u, 2 * u + 1):
                    act.activation(zgate(t), z[:, t, :], ACT.Tanh, scale=0.5).then_inc(ztanh_done, 1)
                for t in (2 * u, 2 * u + 1):
                    act.wait_ge(ztanh_done, t + 1)
                    act.activation(zgate(t), zgate(t), ACT.Copy, bias=0.5, scale=0.5).then_inc(zgate_done, 1)

            def pairwise(u):
                act.wait_ge(pair_read, 3)
                for t in ((1, 3), (5, 7), (0, 2), (4, 6))[u]:
                    if t == 0:
                        act.wait_ge(sig_done, 4)
                    act.activation(sig[:, t, :], sig[:, t - t % 2, :], ACT.Tanh, scale=0.5,
                                   bias=si[:, t:t + 1]).then_inc(sig_done, 1)

            def body(n, k, q):
                for u in range(4):
                    a, b = 4 * (n - 1) + u, u % 2
                    act.wait_ge(expo_done, a + 1)
                    at_least(act, g_done, a - 1)
                    act.activation(dec[b][:], bank[4 + b][:], ACT.Exp).then_inc(exp_done, 1)
                    if not last(n, 1):
                        if u == 0:
                            at_least(act, inter_done, n - 1)
                        first_tap(n + 1, k + (q + 1) // 2, 1 - q, u)
                    if u == 0:
                        act.wait_ge(b_turned, n)
                        at_least(act, st_done, n - 1)
                        act.copy(btok[:].rearrange("p b k -> p (b k)"), bank[6][:]).then_inc(b_read, 1)
                    if u == 1:
                        act.wait_ge(st_done, n)
                        at_least(act, inter_done, n - 1)
                        s_v = bank[6][:, 0:NSEQ * 2 * HD].rearrange("p (b j d) -> p b j d", b=NSEQ, j=2)
                        for j in range(2):
                            r = slice(NS * j, NS * (j + 1))
                            act.copy(state[r, :, j, :], s_v[r, :, j, :]).then_inc(st_read, 1)
                    if u == 2 and not last(n, 2):
                        split_w(n + 2, q)
                    if isinstance(n, int) and n == PAIRS - 2:
                        gate_of_z(u)
                    if isinstance(n, int) and n == PAIRS - 1:
                        pairwise(u)

            def split_expert(e, q):
                for j in range(3):
                    act.copy(ewh[q][:, j, :, :].rearrange("p k d -> p (k d)"), ew_raw[q][:, j, :]).then_inc(ewh_done, 1)

            over_pairs(act, body)
            act.wait_ge(ew_in[0], 48)
            split_expert(0, 0)

            for t in range(T):
                act.wait_ge(yz_turned, t + 1)
                at_least(act, o_done, (t - 2) // 2 + 1 if t > 1 else 0)
                act.copy(yzT[t % 2][:], bank[4 + t % 3][:, 0:DM]).then_inc(yz_read, 1)
            normalise(T, range(4), 3)
            split_turned(4, 4)
            split_turned(5, 5)

            def copy_logits(i):
                act.wait_ge(lg_done, i + 1)
                act.copy(lgT[:, HALF * i:HALF * (i + 1)], bank[4 + i][0:NE, :]).then_inc(lgT_read, 1)

            def expert(e, k, q):
                first = isinstance(e, int) and e == 0
                act.wait_ge(eb_done, e + 1)
                for v in range(4):
                    if first and v == 2:
                        split_turned(6, 6)
                        split_turned(7, 7)
                    if first and v % 2 == 0:
                        copy_logits(v // 2)
                    act.wait_ge(up_done, 4 * e + v + 1)
                    at_least(act, e_done, 4 * (e - 1) + v + 1)
                    act.activation(u32[:, v, :], bank[v][:], ACT.Identity,
                                   bias=eb[q][:, 0, v % 2:v % 2 + 1]).then_inc(up_read, 1)
                    if first:
                        act.wait_ge(up_read, v + 1)
                        act.copy(uh[:, v, :], u32[:, v, :]).then_inc(uh_done, 1)
                if first:
                    act.wait_ge(pexp_in, 1)
                    act.activation(lg[:], lg[:], ACT.Exp).then_inc(pexp_done, 1)
                if not (isinstance(e, int) and e == NE - 1):
                    at_least(act, down_done, 4 * e)
                    act.wait_ge(ew_in[1 - q], 48 * (k + q + 1))
                    split_expert(e + 1, 1 - q)

                def round_e(v):
                    act.wait_ge(e_done, 4 * e + v + 1)
                    at_least(act, down_done, 4 * e)
                    act.copy(eh[:, v, :], e32[:, v, :]).then_inc(eh_done, 1)

                for v in range(4):
                    act.wait_ge(gate2_done, 4 * e + v + 1)
                    at_least(act, el_done, 4 * (e - 1) + v + 1)
                    act.activation(e32[:, v, :], bank[v][:], ACT.Silu,
                                   bias=eb[q][:, 1, v % 2:v % 2 + 1]).then_inc(silu2_done, 1)
                    if v:
                        round_e(v - 1)
                    if first and v == 1:
                        for i in range(2):
                            act.wait_ge(prob_turned, i + 1)
                            act.copy(probT[:, HALF * i:HALF * (i + 1)], bank[4 + i][0:NE, :]).then_inc(prob_read, 1)
                round_e(3)

            over_experts(act, expert)

        @block.vector
        def _(dve):
            steps = [0]

            def link(ins):
                steps[0] += 1
                ins.then_inc(dve_chain, 1)
                dve.wait_ge(dve_chain, steps[0])

            def moments(first, tiles, tile):
                for i, t in enumerate(tiles):
                    ins = dve.bn_stats(stats[:, first + i, :], tile(t))
                link(ins)
                for i in range(len(tiles)):
                    ins = dve.bn_aggr(mv[:, first + i, :], stats[:, first + i, :])
                link(ins)

            def inverse_roots(s):
                link(dve.tensor_scalar(var[:, s], mv[:, s, 1], EPS, None, ALU.add))
                link(dve.tensor_scalar(bits[:, s], var[:, s].bitcast(I32), 1, None, ALU.logical_shift_right))
                link(dve.tensor_scalar(rstd[:, s].bitcast(I32), bits[:, s], -1, ROOT_GUESS, ALU.mult, ALU.add))
                for _ in range(3):
                    link(dve.scalar_tensor_tensor(out=nt0[:, s], in0=rstd[:, s], scalar=-0.5, in1=rstd[:, s],
                                                  op0=ALU.mult, op1=ALU.mult))
                    link(dve.tensor_tensor(nt0[:, s], nt0[:, s], var[:, s], ALU.mult))
                    link(dve.scalar_tensor_tensor(out=rstd[:, s], in0=nt0[:, s], scalar=1.5, in1=rstd[:, s],
                                                  op0=ALU.add, op1=ALU.mult))
                dve.scalar_tensor_tensor(out=nt1[:, s], in0=mv[:, s, 0], scalar=-1.0, in1=rstd[:, s],
                                         op0=ALU.mult, op1=ALU.mult).then_inc(norm_done, 1)

            def normalise(first, tiles):
                for i, t in enumerate(tiles):
                    c = first + i
                    dve.tensor_scalar(xn[:, t, :], xres[:, t, :], mv[:, c, 0:1], rstd[:, c:c + 1],
                                      ALU.subtract, ALU.mult).then_inc(xn_done, 1)

            def rest_turned(i, b):
                h, k = i % 4 // 2, i % 2
                s = slice(HALF * h, HALF * (h + 1))
                dve.wait_ge(uth_done, i + 1)
                dve.tensor_tensor(utl[:, k, s], bank[b][:], f32(uth[:, k, s]), ALU.subtract).then_inc(utl_done, 1)

            def rest_w(m, q):
                dve.wait_ge(wth_done, m + 1)
                dve.tensor_tensor(parts[:, 2 + q, :], bank[6][:],
                                  f32(parts[:, q, :]), ALU.subtract).then_inc(wtl_done, 1)

            def other_taps(m, q, u, ds=range(1, TAPS)):
                j, h = u // 2, u % 2
                src = bank[u % 2][:].rearrange("p (b l) -> p b l", b=2)
                dst = conv[q][:, j, HALF * h:HALF * (h + 1)].rearrange("p (b l) -> p b l", b=2)
                if ds[0] == 1:
                    dve.wait_ge(acc_first, 4 * m + u + 1)
                for d in ds:
                    if d > 1:
                        dve.wait_ge(tap_done, 3 * (4 * m + u) + d - 1)
                    dve.scalar_tensor_tensor(
                        out=dst[:, :, d:SEQ], in0=src[:, :, 0:SEQ - d], scalar=taps[q][:, j, TAPS - 1 - d:TAPS - d],
                        in1=dst[:, :, d:SEQ], op0=ALU.mult, op1=ALU.add).then_inc(tap_done, 1)

            def from_x(t):
                dve.wait_ge(x_in[t // 4], 16)
                return xres[:, t, :]

            moments(0, range(T), from_x)
            inverse_roots(slice(0, T))
            normalise(0, range(4))
            rest_w(0, 0)
            rest_turned(0, 0)
            rest_turned(1, 1)
            for k in range(KD):
                dve.wait_ge(wzh_done, k + 1)
                dve.tensor_tensor(wzl[:, k, :], bank[4 + k][:, 0:ZA], f32(wzh[:, k, :]), ALU.subtract).then_inc(wzl_done, 1)
            rest_turned(2, 2)
            rest_turned(3, 3)
            other_taps(0, 0, 0)
            rest_w(1, 1)
            other_taps(0, 0, 1)
            other_taps(0, 0, 2)
            dve.wait_ge(za_read, 2 * T)
            dve.scalar_tensor_tensor(out=neg_abs[:], in0=a_log[:], scalar=-1.0, in1=a_log[:],
                                     op0=ALU.mult, op1=ALU.min).then_inc(nabs_done, 1)
            other_taps(0, 0, 3)
            dve.wait_ge(sp_done, 1)
            dve.scalar_tensor_tensor(out=dts[:].rearrange("p h t -> p t h"), in0=a_log[:], scalar=0.0, in1=neg_abs[:],
                                     op0=ALU.max, op1=ALU.add).then_inc(dt_done, 1)
            dve.wait_ge(ctx_sm_in, 32)
            dve.tensor_copy(wj_rep[:], wi_wj[:, 1:2].to_broadcast([CTX, P])).then_inc(wj_done, 1)
            other_taps(1, 1, 0)
            dve.wait_ge(cumT_done, 1)
            c_ps = bank[4][:, 0:2 * P].rearrange("p (c k) -> p c k", c=2)
            link(dve.tensor_copy(cpartsT[:, 0, :, :], c_ps))
            link(dve.tensor_tensor(cumT[:], c_ps, cpartsT[:, 0, :, :], ALU.subtract))
            link(dve.tensor_copy(cpartsT[:, 1, :, :], cumT[:]))
            link(dve.tensor_tensor(cumT[:], cumT[:], cpartsT[:, 1, :, :], ALU.subtract))
            dve.tensor_copy(cpartsT[:, 2, :, :], cumT[:]).then_inc(cpart_done, 1)
            other_taps(1, 1, 1)
            dve.wait_ge(cum_done, 1)
            link(dve.tensor_copy(cum[:], bank[7][:, 0:T * NH].rearrange("p (h t) -> p h t", t=T)))
            tot = bank[7][:, T * NH:2 * T * NH].rearrange("p (h b c) -> p b c h", c=2, h=NH)
            dve.tensor_tensor(sdec[:], tot[:, :, 0, :], cum[:].rearrange("p h (b c) -> p b c h", c=2)[:, :, 0, :],
                              ALU.subtract).then_inc(cum_read, 1)
            other_taps(1, 1, 2)
            other_taps(1, 1, 3)
            rest_w(2, 0)

            def read_y(n):
                dve.wait_ge(y_done, 4 * n)
                dve.wait_ge(inter_done, n)
                dve.tensor_tensor(yint[:], bank[7][:, 2 * T * HD:2 * T * HD + NSEQ * 2 * HD].rearrange("p (b j d) -> p b j d", b=NSEQ, j=2),
                                  ecum[:, :, bass.ds(2 * (n - 1), 2)].unsqueeze(3).to_broadcast([P, NSEQ, 2, HD]),
                                  ALU.mult).then_inc(y_step, 1)
                c0 = 2 * HD * (n - 1)
                dst = y[:, :, bass.ds(c0, 2 * HD)]
                dve.tensor_tensor(dst, bank[7][:, 0:2 * T * HD].rearrange("p (t d) -> p t d", t=T), dst,
                                  ALU.add).then_inc(y_step, 1)
                odd = y[:].rearrange("p (b c) d -> p b c d", c=2)[:, :, 1, bass.ds(c0, 2 * HD)]
                dve.wait_ge(y_step, 3 * (n - 1) + 2)
                dve.tensor_tensor(odd, odd, yint[:].rearrange("p b j d -> p b (j d)"), ALU.add).then_inc(y_step, 1)

            def split_router():
                dve.wait_ge(small_in, 12 * 16)
                dve.memset(f32(wrh[:]), 0.0)
                link(dve.memset(f32(wrl[:]), 0.0))
                link(dve.tensor_copy(wrh[:, :, 0:NR], wr_raw[:, :, 0:NR]))
                dve.tensor_tensor(wrl[:, :, 0:NR], wr_raw[:, :, 0:NR], f32(wrh[:, :, 0:NR]),
                                  ALU.subtract).then_inc(wr_done, 1)

            def body(n, k, q):
                for u in range(4):
                    a, b = 4 * (n - 1) + u, u % 2
                    dve.wait_ge(exp_done, a + 1)
                    dve.wait_ge(cb_done, a + 1)
                    at_least(dve, y_done, a - 1)
                    dve.scalar_tensor_tensor(out=g[b][:], in0=dec[b][:], scalar=1.0, in1=bank[2 + b][:],
                                             op0=ALU.min, op1=ALU.mult).then_inc(g_done, 1)
                    if u == 0:
                        if not (isinstance(n, int) and n == 1):
                            other_taps(n, q, 3, (TAPS - 1,))
                            read_y(n - 1)
                    elif not last(n, 1):
                        other_taps(n + 1, 1 - q, u - 1, (TAPS - 1,))
                    if not last(n, 1):
                        other_taps(n + 1, 1 - q, u, range(1, TAPS - 1))
                    if u == 2 and not last(n, 2):
                        rest_w(n + 2, q)
                    if isinstance(n, int) and n == PAIRS and u == 1:
                        split_router()
                if isinstance(n, int) and n == 1:
                    dve.wait_ge(y_init, 1)

            def rest_expert(e, q):
                for j in range(3):
                    dve.wait_ge(ewh_done, 3 * e + j + 1)
                    dve.tensor_tensor(ewl[q][:, j, :, :].rearrange("p k d -> p (k d)"), ew_raw[q][:, j, :],
                                      f32(ewh[q][:, j, :, :].rearrange("p k d -> p (k d)")), ALU.subtract).then_inc(ewl_done, 1)

            over_pairs(dve, body)
            rest_expert(0, 0)
            read_y(PAIRS)
            dve.wait_ge(y_step, 3 * PAIRS)

            dve.wait_ge(z_gated, T)
            for t in range(T):
                dve.tensor_tensor(y[:, t, :], y[:, t, :], z[:, t, :], ALU.mult).then_inc(yz_done, 1)

            def from_projection(t):
                dve.wait_ge(o_done, t // 2 + 1)
                return bank[t // 2][:, DM * (t % 2):DM * (t % 2 + 1)]

            def from_residual(t):
                dve.wait_ge(o_read, t + 1)
                return xres[:, t, :]

            def second_block(tiles):
                s = slice(tiles[0], tiles[-1] + 1)
                dve.wait_ge(norm_done, 2 + tiles[0] // 4)
                link(dve.tensor_scalar(nt0[:, s], rstd[:, s], 1 - P_SEM, 1.0, ALU.mult, ALU.add))
                link(dve.tensor_scalar(shift[:, s], nt1[:, s], 1 - P_SEM, None, ALU.mult))
                for t in tiles:
                    dve.scalar_tensor_tensor(out=xres[:, t, :], in0=from_projection(t), scalar=nt0[:, t:t + 1],
                                             in1=sig[:, t, :], op0=ALU.mult, op1=ALU.add).then_inc(o_read, 1)

            dve.wait_ge(sig_scaled, 1)
            moments(0, range(4), from_projection)
            inverse_roots(slice(0, 4))
            second_block(range(4))
            moments(T, range(4), from_residual)
            moments(4, range(4, 8), from_projection)
            inverse_roots(slice(4, 12))
            second_block(range(4, 8))
            moments(12, range(4, 8), from_residual)
            rest_turned(4, 4)
            rest_turned(5, 5)
            inverse_roots(slice(12, 16))
            normalise(12, range(4, 8))
            rest_turned(6, 6)
            rest_turned(7, 7)

            def route():
                dve.wait_ge(gate_done, 1)
                dve.wait_ge(const_done, 2)
                link(dve.tensor_tensor(lg[:], bank[6][:, 0:T * 8].rearrange("p (t e) -> p t e", t=T)[:, :, 0:NR],
                                       brb[:, 0:1, :].to_broadcast([P, T, NR]), ALU.add))
                link(dve.tensor_tensor(bg[:], lg[:], brb[:, 1:2, :].to_broadcast([P, T, NR]), ALU.add))
                me = bg[:].unsqueeze(3).to_broadcast([P, T, NR, NR])
                other = bg[:].unsqueeze(2).to_broadcast([P, T, NR, NR])
                dve.tensor_tensor(gt[:], other, me, ALU.is_gt)
                link(dve.tensor_tensor(ge[:], other, me, ALU.is_ge))
                link(dve.tensor_tensor(ge[:].rearrange("p t a b -> p t (a b)"), ge[:].rearrange("p t a b -> p t (a b)"),
                                       earlier[:].rearrange("p a b -> p (a b)").unsqueeze(1).to_broadcast([P, T, NR * NR]),
                                       ALU.mult))
                link(dve.tensor_tensor(gt[:], gt[:], ge[:], ALU.max))
                link(dve.tensor_reduce(sel[:], gt[:], AX.X, ALU.add))
                link(dve.tensor_scalar(sel[:], sel[:], TOPK - 0.5, None, ALU.is_lt))
                link(dve.tensor_scalar(bg[:], sel[:], -NEG, NEG, ALU.mult, ALU.add))
                link(dve.tensor_tensor(lg[:], lg[:], sel[:], ALU.mult))
                link(dve.tensor_tensor(lg[:], lg[:], bg[:], ALU.add))
                link(dve.tensor_reduce(mx[:], lg[:], AX.X, ALU.max))
                dve.tensor_tensor(lg[:], lg[:], mx[:].unsqueeze(2).to_broadcast([P, T, NR]), ALU.subtract).then_inc(pexp_in, 1)
                dve.wait_ge(pexp_done, 1)
                link(dve.tensor_reduce(mx[:], lg[:], AX.X, ALU.add))
                link(dve.reciprocal(mx[:], mx[:]))
                dve.tensor_tensor(prob[:, :, 0:NR], lg[:], mx[:].unsqueeze(2).to_broadcast([P, T, NR]),
                                  ALU.mult).then_inc(prob_done, 1)

            def accumulate(e):
                for t in range(T):
                    dve.wait_ge(down_done, 4 * e + t // 2 + 1)
                    dve.scalar_tensor_tensor(out=xres[:, t, :], in0=bank[4 + t // 2][:, DM * (t % 2):DM * (t % 2 + 1)],
                                             scalar=prob[:, t, bass.ds(e, 1)], in1=xres[:, t, :],
                                             op0=ALU.mult, op1=ALU.add).then_inc(acc_done, 1)

            def expert(e, k, q):
                first, second, final = (isinstance(e, int) and e == i for i in (0, 1, NE - 1))
                if second:
                    for t in range(T):
                        dve.wait_ge(bdn_done, t // 2 + 1)
                        dve.scalar_tensor_tensor(out=xres[:, t, :], in0=bank[4 + t // 2][:, DM * (t % 2):DM * (t % 2 + 1)],
                                                 scalar=shift[:, t:t + 1], in1=xres[:, t, :],
                                                 op0=ALU.add, op1=ALU.add).then_inc(bdn_read, 1)
                    dve.wait_ge(bdn_read, T)
                for v in range(4 * (not first)):
                    dve.wait_ge(up_read, 4 * e + v + 1)
                    at_least(dve, gate2_done, 4 * e)
                    dve.tensor_copy(uh[:, v, :], u32[:, v, :]).then_inc(uh_done, 1)
                if first:
                    route()
                else:
                    accumulate(e - 1)
                if not final:
                    rest_expert(e + 1, 1 - q)
                for v in range(4):
                    dve.wait_ge(silu2_done, 4 * e + v + 1)
                    dve.tensor_tensor(e32[:, v, :], e32[:, v, :], u32[:, v, :], ALU.mult).then_inc(e_done, 1)

            over_experts(dve, expert)
            dve.wait_ge(acc_done, T * (NE - 1))
            accumulate(NE - 1)

        @block.tensor
        def _(pe):
            def three(dst, passes, n):
                for k in range(n):
                    for i, (left, right) in enumerate(passes(k)):
                        ins = pe.matmul(dst, left, right, start=(k == 0 and i == 0), stop=(k == n - 1 and i == 2))
                return ins

            def turn_w(m, k, q, waits):
                pe.wait_ge(w_in[q], 16 * (k + 1))
                waits()
                for j in range(2):
                    for d in range(KD):
                        c = (2 * j + d) * P
                        ins = pe.transpose(bank[6][:, c:c + P], w_raw[q][:, j, d * P:(d + 1) * P], ident[:])
                ins.then_inc(w_turned, 1)

            def project_pass(m, q, u, i):
                j, h, k = u // 2, u % 2, i // 3
                if i == 0:
                    if u == 0:
                        pe.wait_ge(wtl_done, m + 1)
                    if isinstance(m, int) and m == 0 and u < 2:
                        pe.wait_ge(utl_done, 2 * u + 2)
                    at_least(pe, tap_done, 3 * (4 * m + u - 1))
                w = (wth, wth, wtl)[i % 3][q][:, j, k, :]
                x_t = (uth, utl, uth)[i % 3][:, k, HALF * h:HALF * (h + 1)]
                ins = pe.matmul(bank[u % 2][:], w, x_t, start=(i == 0), stop=(i == 3 * KD - 1))
                if i == 3 * KD - 1:
                    ins.then_inc(proj_done, 1)

            def project(m, q, u):
                for i in range(3 * KD):
                    project_pass(m, q, u, i)

            def turn_tokens(i, b):
                h, k = i % 4 // 2, i % 2
                if i < 4:
                    pe.wait_ge((xn_done, xn2_done)[h], 4)
                else:
                    pe.wait_ge((xn2_done, xn_done)[h], 8)
                for t in range(4):
                    ins = pe.transpose(bank[b][:, t * P:(t + 1) * P], xn[:, 4 * h + t, k * P:(k + 1) * P], ident[:])
                ins.then_inc(ut_turned, 1)

            pe.wait_ge(const_done, 1)
            turn_w(0, 0, 0, lambda: None)
            pe.wait_ge(wz_in, 32)
            for k in range(KD):
                for j in range(2):
                    pe.transpose(bank[4 + k][:, j * P:(j + 1) * P], wz_rawz[:, j, k * P:(k + 1) * P], ident[:])
                pe.transpose(bank[4 + k][:, DM:ZA], wz_rawa[:, k * P:(k + 1) * P], ident[0:NH, 0:NH]).then_inc(wz_turned, 1)
            for i in range(4):
                turn_tokens(i, i)
            turn_w(1, 0, 1, lambda: pe.wait_ge(wtl_done, 1))
            def project_za(t):
                if t == 0:
                    pe.wait_ge(wzl_done, KD)
                    pe.wait_ge(utl_done, 4)
                at_least(pe, za_read, 2 * (t - 3))
                s = slice(t * P, (t + 1) * P)
                three(bank[2 + t % 4][:, 0:ZA], lambda k: [(uth[:, k, s], wzh[:, k, :]), (uth[:, k, s], wzl[:, k, :]),
                                                           (utl[:, k, s], wzh[:, k, :])], KD).then_inc(za_done, 1)

            project(0, 0, 0)
            project(0, 0, 1)
            for t in range(4):
                project_za(t)
            project(0, 0, 2)
            for t in range(4, 8):
                project_za(t)
            project(0, 0, 3)
            project(1, 1, 0)
            pe.wait_ge(small_in, 12 * 16)
            for k in range(KD):
                ins = pe.transpose(bank[6][:, k * 2 * NE:(k + 1) * 2 * NE], b_rows[:, k * P:(k + 1) * P], ident[0:2 * NE, 0:2 * NE])
            ins.then_inc(misc_turned, 1)
            pe.wait_ge(wo_in, 16)
            pe.wait_ge(za_read, 2 * T)
            for k in range(KD):
                for j in range(2):
                    c = (2 * k + j) * P
                    ins = pe.transpose(bank[5][:, c:c + P], wo_raw[:, j, k * P:(k + 1) * P], ident[:])
            ins.then_inc(misc_turned, 1)
            pe.wait_ge(ctx_sm_in, 32)
            for i in range(2):
                for t in range(4):
                    ins = pe.transpose(bank[(4, 7)[i]][0:CTX, t * P:(t + 1) * P], ctx_raw[:, 4 * i + t, :], ident[:])
                ins.then_inc(ctx_turned, 1)

            def turn_x(i):
                at_least(pe, x_read, i - 1)
                for t in range(2):
                    for c in range(2):
                        col = (2 * t + c) * P
                        ins = pe.transpose(bank[2 + i % 2][:, col:col + P],
                                           conv[0][:, c, (2 * i + t) * P:(2 * i + t + 1) * P], ident[:])
                ins.then_inc(x_turned, 1)

            pe.wait_ge(tap_done, 12)
            turn_x(0)
            turn_x(1)
            pe.wait_ge(dt_done, 1)
            pe.wait_ge(const_done, 2)
            pe.wait_ge(ctx_read, 2)
            for c in range(2):
                ins = pe.matmul(bank[4][:, c * P:(c + 1) * P], dts[:, 16 * c:16 * c + 16, :].rearrange("p h t -> p (h t)"),
                                neg_tri[:], start=True, stop=True)
            ins.then_inc(cumT_done, 1)
            project(1, 1, 1)
            turn_x(2)
            turn_x(3)
            pe.matmul(bank[7][:, 0:T * NH], neg_tri[:], dts[:].rearrange("p h t -> p (h t)"), start=True, stop=True)
            pe.matmul(bank[7][:, T * NH:2 * T * NH], neg_ones[:], dts[:].rearrange("p h t -> p (h t)"),
                      start=True, stop=True).then_inc(cum_done, 1)
            project(1, 1, 2)
            pe.wait_ge(x_read, 4)
            pe.wait_ge(misc_read, 1)
            pe.wait_ge(wj_done, 1)
            for i in range(2):
                pe.matmul(bank[2 + i][:], wj_rep[:], ctxT[:, HALF * i:HALF * (i + 1)], start=True, stop=True).then_inc(pair_done, 1)
            for t in range(T):
                ins = pe.matmul(bank[6][:, t:t + 1], ctxT[:, t * P:(t + 1) * P], wi_wj[:, 0:1], start=True, stop=True)
            ins.then_inc(pair_done, 1)
            project(1, 1, 3)
            turn_w(2, 1, 0, lambda: pe.wait_ge(pair_read, 3))
            pe.wait_ge(cpart_done, 1)
            pe.wait_ge(misc_read, 2)
            pe.wait_ge(cum_read, 1)

            def weigh(n, q, u, i):
                a = 4 * (n - 1) + u
                j, h, b = u // 2, u % 2, u % 2
                if i == 0:
                    pe.wait_ge(masked, a + 1)
                    if u == 0:
                        pe.wait_ge(xp_done, n)
                        at_least(pe, y_step, 3 * (n - 1) - 1)
                t = 4 * h + i
                c = (2 * t + j) * HD
                ins = pe.matmul(bank[7][:, c:c + HD], g[b][:, i * P:(i + 1) * P], xp[q][:, t, j, :],
                                start=True, stop=True)
                if i == 3:
                    ins.then_inc(y_done, 1)

            def new_state(n, q, i):
                if i == 0:
                    pe.wait_ge(b_read, n)
                    pe.wait_ge(xp_done, n)
                ins = pe.matmul(bank[6][:, i * 2 * HD:(i + 1) * 2 * HD], btok[:, i, :], xs[q][:, i, :],
                                start=True, stop=True)
                if i == NSEQ - 1:
                    ins.then_inc(st_done, 1)

            def from_state(n, q, i):
                if i == 0:
                    pe.wait_ge(st_read, 2 * n)
                c = 2 * T * HD + i * 2 * HD
                ins = pe.matmul(bank[7][:, c:c + 2 * HD], conv[q][:, 1, (2 * i + 1) * P:(2 * i + 2) * P],
                                state[:, i, :, :].rearrange("p j d -> p (j d)"), start=True, stop=True)
                if i == NSEQ - 1:
                    ins.then_inc(inter_done, 1)

            def weigh_before(n, q, u, tiles):
                for i in tiles:
                    if u == 2:
                        weigh(n, q, 1, i)
                    elif not (isinstance(n, int) and n == 1):
                        weigh(n - 1, 1 - q, 3, i)

            def body(n, k, q):
                for u in range(4):
                    a = 4 * (n - 1) + u
                    j, h, b = u // 2, u % 2, u % 2
                    if u == 0:
                        pe.wait_ge(cum_in[q], 64 * (k + q))
                    at_least(pe, exp_done, a - 1)
                    pe.matmul(bank[4 + b][:], cl[q][:, j, :], cr[q][:, j, 4 * h:4 * h + 4, :].rearrange("p t k -> p (t k)"),
                              start=True, stop=True).then_inc(expo_done, 1)
                    if u == 1 and not last(n, 1):
                        project_pass(n + 1, 1 - q, u, 0)
                    if u < 2:
                        pe.wait_ge(tap_done, 12 * n + (9, 12)[u])
                    at_least(pe, g_done, a - 1)
                    r = slice(NS * j, NS * (j + 1))
                    for i in range(4):
                        s = slice((4 * h + i) * P, (4 * h + i + 1) * P)
                        ins = pe.matmul(bank[2 + b][:, i * P:(i + 1) * P], conv[q][r, 0, s], conv[q][r, 1, s],
                                        start=True, stop=True)
                    ins.then_inc(cb_done, 1)
                    for i in range(3 * KD):
                        if not last(n, 1):
                            if u % 2 == 0 and i == 0:
                                weigh_before(n, q, u, (0, 1))
                            if not (u == 1 and i == 0):
                                project_pass(n + 1, 1 - q, u, i)
                            if u % 2 == 0 and i == 0:
                                weigh_before(n, q, u, (2, 3))
                        elif u % 2 == 0 and i == 0:
                            weigh_before(n, q, u, range(4))
                        if i < 4 and u % 2:
                            weigh(n, q, u - 1, i)
                            if u == 1:
                                new_state(n, q, i)
                            else:
                                from_state(n, q, i)
                    if u == 0:
                        pe.wait_ge(wtl_done, min(n + 2, PAIRS + 1) if isinstance(n, int) else n + 2)
                        for i in range(NSEQ):
                            ins = pe.transpose(bank[6][:, i * P:(i + 1) * P], conv[q][:, 0, 2 * i * P:(2 * i + 1) * P], ident[:])
                        ins.then_inc(b_turned, 1)
                    if u == 2:
                        pe.wait_ge(st_read, 2 * n)
                        if not last(n, 2):
                            turn_w(n + 2, k + 1, q, lambda: None)

            over_pairs(pe, body)
            for i in range(4):
                weigh(PAIRS, 0, 3, i)

            def turn_yz(t):
                pe.wait_ge(yz_done, t + 1)
                at_least(pe, yz_read, t - 2)
                for k in range(KD):
                    ins = pe.transpose(bank[4 + t % 3][:, k * P:(k + 1) * P], y[:, t, k * P:(k + 1) * P], ident[:])
                ins.then_inc(yz_turned, 1)

            turn_yz(0)
            turn_yz(1)
            for t in range(T):
                o = bank[t // 2][:, DM * (t % 2):DM * (t % 2 + 1)]
                pe.matmul(o, ident[:], xres[:, t, :], start=True, stop=False)
                pe.wait_ge(yz_read, t + 1)
                for k in range(KD):
                    ins = pe.matmul(o, yzT[t % 2][:, k * P:(k + 1) * P], woT[:, k, :], start=False, stop=(k == KD - 1))
                if t % 2:
                    ins.then_inc(o_done, 1)
                if t + 2 < T:
                    turn_yz(t + 2)
            turn_tokens(4, 4)
            turn_tokens(5, 5)

            def up(e, q, tiles=range(4)):
                pe.wait_ge(ewl_done, 3 * (e + 1))
                for v in tiles:
                    n, m = v // 2, v % 2
                    s = slice(HALF * n, HALF * (n + 1))
                    c = slice(P * m, P * (m + 1))
                    at_least(pe, silu2_done, 4 * (e - 1) + v + 1)
                    if isinstance(e, int) and e == 0 and m == 0:
                        pe.wait_ge(utl_done, 6 + 2 * n)
                    three(bank[v][:], lambda k: [(ewh[q][:, 0, k, c], uth[:, k, s]), (ewh[q][:, 0, k, c], utl[:, k, s]),
                                                 (ewl[q][:, 0, k, c], uth[:, k, s])], KD).then_inc(up_done, 1)

            def gate(e, q, tiles=range(4)):
                for v in tiles:
                    n, m = v // 2, v % 2
                    c = slice(P * m, P * (m + 1))
                    pe.wait_ge(up_read, 4 * e + v + 1)
                    if m == 0:
                        pe.wait_ge(ul_done, 4 * e + 2 * n + 2)
                    three(bank[v][:], lambda k: [(ewh[q][:, 1, k, c], uh[:, 2 * n + k, :]),
                                                 (ewh[q][:, 1, k, c], ul[:, 2 * n + k, :]),
                                                 (ewl[q][:, 1, k, c], uh[:, 2 * n + k, :])], KD).then_inc(gate2_done, 1)

            def down(e, q):
                for t in range(T):
                    n = t // 4
                    if t % 4 == 0:
                        pe.wait_ge(el_done, 4 * e + 2 * n + 2)
                    if t % 2 == 0:
                        if isinstance(e, int) and e == 0:
                            pe.wait_ge(bdn_read, t + 2)
                        at_least(pe, acc_done, T * (e - 1) + t + 2)
                    s = slice((t % 4) * P, (t % 4 + 1) * P)
                    ins = three(bank[4 + t // 2][:, DM * (t % 2):DM * (t % 2 + 1)],
                                lambda k: [(eh[:, 2 * n + k, s], ewh[q][:, 2, k, :]), (eh[:, 2 * n + k, s], ewl[q][:, 2, k, :]),
                                           (el[:, 2 * n + k, s], ewh[q][:, 2, k, :])], KD)
                    if t % 2:
                        ins.then_inc(down_done, 1)

            def logits(i):
                pe.wait_ge(wr_done, 1)
                pe.wait_ge(utl_done, 6 + 2 * i)
                s = slice(HALF * i, HALF * (i + 1))
                three(bank[4 + i][0:NE, :], lambda k: [(wrh[:, k, :], uth[:, k, s]), (wrh[:, k, :], utl[:, k, s]),
                                                       (wrl[:, k, :], uth[:, k, s])], KD).then_inc(lg_done, 1)

            def turn_logits():
                pe.wait_ge(lgT_read, 2)
                for t in range(T):
                    ins = pe.transpose(bank[6][:, t * 8:(t + 1) * 8], lgT[:, t * P:(t + 1) * P], ident[0:NE, 0:NE])
                ins.then_inc(gate_done, 1)

            def turn_prob():
                pe.wait_ge(prob_done, 1)
                for i in range(2):
                    for t in range(4):
                        ins = pe.transpose(bank[4 + i][0:NE, t * P:(t + 1) * P], prob[:, 4 * i + t, :], ident[:])
                    ins.then_inc(prob_turned, 1)

            def down_biases():
                pe.wait_ge(prob_read, 2)
                for i in range(4):
                    for t in range(2):
                        tt = 2 * i + t
                        ins = pe.matmul(bank[4 + i][:, DM * t:DM * (t + 1)], probT[:, tt * P:(tt + 1) * P], bd[:],
                                        start=True, stop=True)
                    ins.then_inc(bdn_done, 1)

            def expert(e, k, q):
                if isinstance(e, int) and e == 0:
                    logits(0)
                    up(0, 0, range(2))
                    turn_tokens(6, 6)
                    turn_tokens(7, 7)
                    logits(1)
                    turn_logits()
                    up(0, 0, range(2, 4))
                    gate(0, 0, range(2))
                    turn_prob()
                    gate(0, 0, range(2, 4))
                    down_biases()
                else:
                    up(e, q)
                    down(e - 1, 1 - q)
                    gate(e, q)

            over_experts(pe, expert)
            down(NE - 1, 1)


_INS = ['x', 'ctx_512', 'L0_attn_W_in', 'L0_attn_conv_w', 'L0_attn_conv_b', 'L0_attn_D', 'L0_attn_z_bias',
        'L0_attn_W_out', 'L0_xattn_W', 'L0_xattn_b', 'L0_ffn_Wr', 'L0_ffn_br', 'L0_ffn_gate_bias', 'L0_ffn_Wup',
        'L0_ffn_bup', 'L0_ffn_Wgate', 'L0_ffn_bgate', 'L0_ffn_Wdown', 'L0_ffn_bdown', 'L0_ffn_Wsu', 'L0_ffn_bsu',
        'L0_ffn_Wsg', 'L0_ffn_bsg', 'L0_ffn_Wsd', 'L0_ffn_bsd']
_OUTS = [((NSEQ, SEQ, DM), 'float32')]


def kernel(**inputs):
    import numpy as _np
    import concourse.bacc as _bacc
    from concourse import mybir as _mybir
    from concourse.bass_utils import run_bass_kernel_spmd as _run

    nc = _bacc.Bacc("TRN2", target_bir_lowering=False, num_devices=1)
    arrays, args = {}, []
    for name in _INS:
        a = _np.ascontiguousarray(inputs[name])
        arrays[f"in_{name}_dram"] = a
        args.append(nc.dram_tensor(f"in_{name}_dram", a.shape, _mybir.dt.from_np(a.dtype), kind="ExternalInput").ap())
    for i, (shape, dtype) in enumerate(_OUTS):
        dt = _mybir.dt.from_np(_np.dtype(dtype))
        args.append(nc.dram_tensor(f"out_{i}_dram", shape, dt, kind="ExternalOutput").ap())
    decoder_layer(nc, *args)
    r = _run(nc, [arrays], core_ids=[0])
    got = tuple(r.results[0][f"out_{i}_dram"] for i in range(len(_OUTS)))
    return got[0]
```

```python
from contextlib import ExitStack

import concourse.bass as bass
from concourse import mybir

P = 128
F32 = mybir.dt.float32
F32R = mybir.dt.float32r
I32 = mybir.dt.int32
BF16 = mybir.dt.bfloat16
ALU = mybir.AluOpType
ACT = mybir.ActivationFunctionType
AX = mybir.AxisListType

NSEQ, SEQ, DM = 4, 256, 256
T = NSEQ * SEQ // P
HALF = 512
KD = DM // P
NH, HD, NS = 32, 8, 64
PAIRS = NH // 2
TAPS = 4
C_X, C_B = 0, DM
C_C = C_B + NH * NS
C_Z = C_C + NH * NS
C_A = C_Z + DM
ZA = DM + NH
NE = 8
NR = 7
TOPK = 2
EPS = 1e-5
ROOT_GUESS = 0x5F3759DF - 2**31
P_SEM = 0.6
NEG = -1e30
CTX = 64
BLOCK = 16
STEP0, STEPS = 32, P // BLOCK - 1


def decoder_layer(nc, x, ctx_in, W_in, conv_w, conv_b, D, z_bias, W_out, xw, xb, Wr, br, gate_bias,
                  Wup, bup, Wgate, bgate, Wdown, bdown, Wsu, bsu, Wsg, bsg, Wsd, bsd, out):
    x_v = x.rearrange("b (c p) d -> p (b c) d", p=P)
    out_v = out.rearrange("b (c p) d -> p (b c) d", p=P)
    ctx_v = ctx_in.rearrange("b (c p) d -> p (b c) d", p=P)
    cum_dram = nc.dram_tensor("cum_dram", (3, NH * T, P), BF16, kind="Internal").ap()

    with ExitStack() as stack:
        def sb(name, shape, dt=F32):
            return stack.enter_context(nc.sbuf_tensor(name, shape, dt))

        def sem(name):
            return stack.enter_context(nc.semaphore(name))

        bank = [stack.enter_context(nc.psum_tensor(f"bank{i}", [P, HALF], F32)) for i in range(8)]

        ident = sb("ident", [P, P])
        neg_tri = sb("neg_tri", [P, P])
        neg_ones = sb("neg_ones", [P, P])
        causal = sb("causal", [P, P])
        earlier = sb("earlier", [P, NR, NR])
        xres = sb("xres", [P, T, DM])
        stats = sb("stats", [P, 2 * T, 6])
        mv = sb("mv", [P, 2 * T, 2])
        var = sb("var", [P, 2 * T])
        bits = sb("bits", [P, 2 * T], I32)
        rstd = sb("rstd", [P, 2 * T])
        nt0 = sb("nt0", [P, 2 * T])
        nt1 = sb("nt1", [P, 2 * T])
        shift = sb("shift", [P, T])
        uth = sb("uth", [P, KD, T * P], F32R)
        utl = sb("utl", [P, KD, T * P], F32R)
        xtok = sb("xtok", [P, T, DM])
        xsd = sb("xsd", [P, NSEQ, DM])
        y = sb("y", [P, T, DM])
        z = sb("z", [P, T, DM])
        sig = sb("sig", [P, T, DM])
        a_log = sb("a_log", [P, T, NH])
        neg_abs = sb("neg_abs", [P, T, NH])
        dts = sb("dts", [P, NH, T])
        cum = sb("cum", [P, NH, T])
        cumT = sb("cumT", [P, 2, P])
        cpartsT = sb("cpartsT", [P, 3, 2, P], BF16)
        ecum = sb("ecum", [P, NSEQ, NH])
        sdec = sb("sdec", [P, NSEQ, NH])
        w_raw = [sb(f"w_raw{i}", [P, 2, DM]) for i in range(2)]
        parts = sb("parts", [P, 8, HALF], F32R)
        wth = [parts[:, i, :].rearrange("p (a k c) -> p a k c", a=2, k=KD) for i in range(2)]
        wtl = [parts[:, 2 + i, :].rearrange("p (a k c) -> p a k c", a=2, k=KD) for i in range(2)]
        conv = [sb(f"conv{i}", [P, 2, T * P]) for i in range(2)]
        taps = [sb(f"taps{i}", [P, 2, TAPS]) for i in range(2)]
        tap_b = [sb(f"tap_b{i}", [P, 2]) for i in range(2)]
        cl = [sb(f"cl{i}", [STEP0 + STEPS, 2, P], BF16) for i in range(2)]
        cr = [sb(f"cr{i}", [STEP0 + STEPS, 2, T, P], BF16) for i in range(2)]
        dec = [sb(f"dec{i}", [P, HALF]) for i in range(2)]
        g = [sb(f"g{i}", [P, HALF]) for i in range(2)]
        xp = [sb(f"xp{i}", [P, T, 2, HD]) for i in range(2)]
        xs = [sb(f"xs{i}", [P, NSEQ, 2 * HD]) for i in range(2)]
        btok = sb("btok", [P, NSEQ, P])
        state = sb("state", [P, NSEQ, 2, HD])
        yint = sb("yint", [P, NSEQ, 2, HD])
        wzh = sb("wzh", [P, KD, ZA], F32R)
        wzl = sb("wzl", [P, KD, ZA], F32R)
        zb = sb("zb", [P, DM])
        db = sb("db", [P, NH])
        woT = sb("woT", [P, KD, DM])
        yzT = sb("yzT", [P, KD, T * P])
        wi_wj = sb("wi_wj", [CTX, 2])
        wj_rep = sb("wj_rep", [CTX, P])
        xbb = sb("xbb", [P, 1])
        si = sb("si", [P, T])
        ew_raw = [sb(f"ew_raw{i}", [P, 3, KD * DM]) for i in range(2)]
        ewh = [sb(f"ewh{i}", [P, 3, KD, DM], F32R) for i in range(2)]
        ewl = [sb(f"ewl{i}", [P, 3, KD, DM], F32R) for i in range(2)]
        uh = sb("uh", [P, 4, HALF], F32R)
        ul = sb("ul", [P, 4, HALF], F32R)
        eh = parts[:, 0:4, :]
        el = parts[:, 4:8, :]
        b_rows = sb("b_rows", [2 * NE, DM])
        b_cols = sb("b_cols", [P, NE, 2, KD])
        eb = [sb(f"eb{i}", [P, 2, KD]) for i in range(2)]
        bd = sb("bd", [NE, DM])
        wr_raw = sb("wr_raw", [P, KD, 8])
        wrh = sb("wrh", [P, KD, 8], F32R)
        wrl = sb("wrl", [P, KD, 8], F32R)
        brb = sb("brb", [P, 2, NR])
        lg = sb("lg", [P, T, NR])
        bg = sb("bg", [P, T, NR])
        gt = sb("gt", [P, T, NR, NR])
        ge = sb("ge", [P, T, NR, NR])
        sel = sb("sel", [P, T, NR])
        mx = sb("mx", [P, T])
        prob = sb("prob", [P, T, NE])
        probT = sb("probT", [NE, T * P])
        lgT = probT
        u32 = conv[0][:].rearrange("p a (b n) -> p (a b) n", n=HALF)
        e32 = conv[1][:].rearrange("p a (b n) -> p (a b) n", n=HALF)
        xn = y
        wz_rawz = ew_raw[0][:, 0, :].rearrange("p (a d) -> p a d", a=2)
        wz_rawa = ew_raw[0][0:NH, 1, 0:DM]
        wo_raw = ew_raw[0][:, 2, :].rearrange("p (a d) -> p a d", a=2)
        ctx_raw = ew_raw[1][:, 0, :].rearrange("p (t d) -> p t d", t=T)
        ctxT = ew_raw[1][0:CTX, 1:3, :].rearrange("p a n -> p (a n)")

        def f32(ap):
            return ap.bitcast(F32)

        def zgate(t):
            flat = (ew_raw[1], w_raw[1])[t // 6][:].rearrange("p a d -> p (a d)")
            return flat[:, DM * (t % 6):DM * (t % 6 + 1)]

        x_in = [sem(f"x_in{i}") for i in range(2)]
        w_in = [sem(f"w_in{i}") for i in range(2)]
        taps_in = [sem(f"taps_in{i}") for i in range(2)]
        cum_in = [sem(f"cum_in{i}") for i in range(2)]
        ew_in = [sem(f"ew_in{i}") for i in range(2)]
        wz_in, wo_in, ctx_sm_in = sem("wz_in"), sem("wo_in"), sem("ctx_sm_in")
        small_in = sem("small_in")
        cum_out, y_out = sem("cum_out"), sem("y_out")
        const_chain, const_done = sem("const_chain"), sem("const_done")
        dve_chain, act_chain = sem("dve_chain"), sem("act_chain")
        norm_done, xn_done, xn2_done = sem("norm_done"), sem("xn_done"), sem("xn2_done")
        ut_turned, uth_done, utl_done = sem("ut_turned"), sem("uth_done"), sem("utl_done")
        w_turned, wth_done, wtl_done = sem("w_turned"), sem("wth_done"), sem("wtl_done")
        wz_turned, wzh_done, wzl_done = sem("wz_turned"), sem("wzh_done"), sem("wzl_done")
        za_done, za_read = sem("za_done"), sem("za_read")
        nabs_done, sp_done, dt_done = sem("nabs_done"), sem("sp_done"), sem("dt_done")
        cum_done, cum_read, cexp_done = sem("cum_done"), sem("cum_read"), sem("cexp_done")
        cumT_done, cpart_done = sem("cumT_done"), sem("cpart_done")
        x_turned, x_read, y_init, z_ready = sem("x_turned"), sem("x_read"), sem("y_init"), sem("z_ready")
        misc_turned, misc_read, wj_done = sem("misc_turned"), sem("misc_read"), sem("wj_done")
        ctx_turned, ctx_read = sem("ctx_turned"), sem("ctx_read")
        pair_done, pair_read = sem("pair_done"), sem("pair_read")
        proj_done, acc_first, tap_done = sem("proj_done"), sem("acc_first"), sem("tap_done")
        expo_done, exp_done, cb_done = sem("expo_done"), sem("exp_done"), sem("cb_done")
        g_done, masked, y_done = sem("g_done"), sem("masked"), sem("y_done")
        b_turned, b_read, st_done, st_read = sem("b_turned"), sem("b_read"), sem("st_done"), sem("st_read")
        inter_done, y_step = sem("inter_done"), sem("y_step")
        eb_done = sem("eb_done")
        xp_done = sem("xp_done")
        sig_done, sig_scaled = sem("sig_done"), sem("sig_scaled")
        ztanh_done, zgate_done, z_gated = sem("ztanh_done"), sem("zgate_done"), sem("z_gated")
        lg_done, lgT_read = sem("lg_done"), sem("lgT_read")
        yz_done, yz_turned, yz_read = sem("yz_done"), sem("yz_turned"), sem("yz_read")
        o_done, o_read = sem("o_done"), sem("o_read")
        wr_done, gate_done, pexp_in, pexp_done = sem("wr_done"), sem("gate_done"), sem("pexp_in"), sem("pexp_done")
        prob_done, prob_turned, prob_read = sem("prob_done"), sem("prob_turned"), sem("prob_read")
        bdn_done, bdn_read = sem("bdn_done"), sem("bdn_read")
        ewh_done, ewl_done = sem("ewh_done"), sem("ewl_done")
        up_done, up_read, uh_done, ul_done = sem("up_done"), sem("up_read"), sem("uh_done"), sem("ul_done")
        gate2_done, silu2_done, e_done = sem("gate2_done"), sem("silu2_done"), sem("e_done")
        eh_done, el_done, down_done, acc_done = sem("eh_done"), sem("el_done"), sem("down_done"), sem("acc_done")
        el_last = sem("el_last")

        def at_least(eng, s, n):
            if not isinstance(n, int) or n > 0:
                eng.wait_ge(s, n)

        def over_pairs(eng, body):
            body(1, 0, 1)
            with eng.Fori(1, PAIRS // 2 - 1) as k:
                body(2 * k, k, 0)
                body(2 * k + 1, k, 1)
            for n in range(PAIRS - 2, PAIRS + 1):
                body(n, n // 2, n % 2)

        def last(n, ahead):
            return isinstance(n, int) and n + ahead > PAIRS

        def over_experts(eng, body):
            for e in range(2):
                body(e, e // 2, e % 2)
            with eng.Fori(1, NE // 2 - 1) as k:
                body(2 * k, k, 0)
                body(2 * k + 1, k, 1)
            for e in range(NE - 2, NE):
                body(e, e // 2, e % 2)

        def head_half(n, u):
            return (u % 2, u // 2) if isinstance(n, int) and n == PAIRS else (u // 2, u % 2)

        def y_bank(n, half):
            return bank[6] if isinstance(n, int) and n == PAIRS and half else bank[7]

        block = stack.enter_context(nc.Block())

        @block.sync
        def _(sp):
            def rows(w, m):
                if isinstance(m, int) and m == 0:
                    return w[C_X:C_B].rearrange("(j r) ... -> r j ...", j=2)
                return w[C_B:C_Z].rearrange("(j r) ... -> r j ...", j=2)[bass.ds(P * (m - 1), P)]

            def load_w(m, q):
                at_least(sp, w_turned, m - 1)
                sp.dma_start(w_raw[q][:], rows(W_in, m)).then_inc(w_in[q], 16)

            def load_taps(m, q):
                at_least(sp, tap_done, 12 * (m - 1))
                sp.dma_start(taps[q][:], rows(conv_w, m)).then_inc(taps_in[q], 16)
                for j in range(2):
                    sp.dma_start(tap_b[q][:, j:j + 1], rows(conv_b.unsqueeze(1), m)[:, j, :]).then_inc(taps_in[q], 16)

            def load_cum(m, q):
                at_least(sp, expo_done, 4 * (m - 2))
                for s in range(3):
                    sp.dma_start(cl[q][T * s:T * s + T, :, :],
                                 cum_dram[s, bass.ds(2 * T * (m - 1), 2 * T), :]
                                 .rearrange("(j t) k -> t j k", j=2)).then_inc(cum_in[q], 16)
                sp.dma_start(cr[q][24:27, :, :, :].rearrange("s j t k -> s (j t k)"),
                             cum_dram[:, bass.ds(2 * T * (m - 1), 2 * T), :]
                             .rearrange("s r k -> s (r k)")).then_inc(cum_in[q], 16)

            for i in range(2):
                sp.dma_start(xres[:, 4 * i:4 * i + 4, :], x_v[:, 4 * i:4 * i + 4, :]).then_inc(x_in[i], 16)
            load_w(0, 0)
            sp.dma_start(wz_rawz, W_in[C_Z:C_Z + DM, :].rearrange("(a p) d -> p a d", p=P)).then_inc(wz_in, 16)
            sp.dma_start(wz_rawa, W_in[C_A:C_A + NH, :]).then_inc(wz_in, 16)
            load_w(1, 1)
            load_taps(0, 0)
            load_taps(1, 1)
            sp.dma_start(wo_raw, W_out.rearrange("(a p) d -> p a d", p=P)).then_inc(wo_in, 16)
            sp.dma_start(ctx_raw, ctx_v).then_inc(ctx_sm_in, 16)
            with nc.allow_non_contiguous_dma(reason="128 values"):
                sp.dma_start(wi_wj[:], xw.rearrange("a (j p) -> p (a j)", j=2)).then_inc(ctx_sm_in, 16)
            sp.dma_start(db[:], D.partition_broadcast(P)).then_inc(small_in, 16)
            sp.dma_start(zb[:], z_bias.partition_broadcast(P)).then_inc(small_in, 16)
            sp.dma_start(xbb[:], xb.partition_broadcast(P)).then_inc(small_in, 16)
            load_w(2, 0)
            for dst, src in ((b_rows[0:NR, :], bup), (b_rows[NR:NE, :], bsu.unsqueeze(0)),
                             (b_rows[NE:NE + NR, :], bgate), (b_rows[NE + NR:2 * NE, :], bsg.unsqueeze(0)),
                             (bd[0:NR, :], bdown), (bd[NR:NE, :], bsd.unsqueeze(0)),
                             (brb[:, 0, :], br.partition_broadcast(P)), (brb[:, 1, :], gate_bias.partition_broadcast(P)),
                             (wr_raw[:, :, 0:NR], Wr.rearrange("(k p) e -> p k e", p=P))):
                sp.dma_start(dst, src).then_inc(small_in, 16)
            load_w(3, 1)
            load_taps(2, 0)
            sp.wait_ge(cpart_done, 1)
            sp.dma_start(cum_dram.rearrange("s (c p) k -> p s c k", p=P), cpartsT[:]).then_inc(cum_out, 16)
            sp.wait_ge(cum_out, 16)
            sp.wait_ge(const_done, 2)
            load_cum(1, 1)
            sp.wait_ge(const_done, 3)

            def body(n, k, q):
                if not last(n, 1):
                    load_cum(n + 1, 1 - q)
                if not last(n, 3):
                    load_w(n + 3, 1 - q)
                if not last(n, 2):
                    load_taps(n + 2, q)

            over_pairs(sp, body)

            def load_expert(e, q):
                at_least(sp, ewl_done, 3 * (e - 1))
                for j, w in enumerate((Wup, Wgate, Wdown)):
                    sp.dma_start(ew_raw[q][:, j, :].rearrange("p (k d) -> p k d", k=KD),
                                 w[bass.ds(e, 1), :, :].rearrange("e (k p) d -> p (e k) d", p=P)).then_inc(ew_in[q], 16)

            load_expert(0, 0)
            sp.wait_ge(z_gated, T)
            load_expert(1, 1)
            with sp.Fori(1, 3) as k:
                load_expert(2 * k, 0)
                load_expert(2 * k + 1, 1)
            load_expert(6, 0)
            at_least(sp, ewl_done, 3 * (NE - 2))
            for j, w in enumerate((Wsu, Wsg, Wsd)):
                sp.dma_start(ew_raw[1][:, j, :].rearrange("p (k d) -> p k d", k=KD),
                             w.rearrange("(k p) d -> p k d", p=P)).then_inc(ew_in[1], 16)
            for i in range(4):
                sp.wait_ge(acc_done, T * (NE - 1) + 2 * i + 2)
                sp.dma_start(out_v[:, 2 * i:2 * i + 2, :], xres[:, 2 * i:2 * i + 2, :]).then_inc(y_out, 16)
            sp.wait_ge(y_out, 64)

        @block.gpsimd
        def _(pool):
            steps = [0]

            def link(ins):
                steps[0] += 1
                ins.then_inc(const_chain, 1)
                pool.wait_ge(const_chain, steps[0])

            link(pool.memset(ident[:], 0.0))
            pool.affine_select(out=ident[:], in_=ident[:], compare_op=ALU.not_equal, fill=1.0,
                               base=0, pattern=[[-1, P]], channel_multiplier=1).then_inc(const_done, 1)
            link(pool.memset(neg_ones[:], -1.0))
            link(pool.affine_select(out=neg_tri[:], in_=neg_ones[:], compare_op=ALU.is_ge, fill=0.0,
                                    base=0, pattern=[[1, P]], channel_multiplier=-1))
            link(pool.memset(earlier[:], 1.0))
            link(pool.affine_select(out=earlier[:], in_=earlier[:], compare_op=ALU.is_gt, fill=0.0,
                                    base=0, pattern=[[1, NR], [-1, NR]], channel_multiplier=0))
            link(pool.memset(state[:], 0.0))
            link(pool.memset(prob[:], 1.0))
            link(pool.memset(causal[:], 1.0))
            link(pool.affine_select(out=causal[:], in_=causal[:], compare_op=ALU.is_ge, fill=0.0,
                                    base=0, pattern=[[1, P]], channel_multiplier=-1))
            for q in (1, 0):
                link(pool.memset(cl[q][:], 1.0))
                link(pool.memset(cr[q][0:STEP0, :, :, :], 0.0))
                link(pool.memset(cr[q][STEP0:STEP0 + STEPS, :, :, :], NEG))
                link(pool.affine_select(out=cl[q][STEP0:STEP0 + STEPS, :, :], in_=cl[q][STEP0:STEP0 + STEPS, :, :],
                                        compare_op=ALU.is_ge, fill=0.0, base=-BLOCK,
                                        pattern=[[0, 2], [1, P]], channel_multiplier=-BLOCK))
                step = cr[q][STEP0:STEP0 + STEPS, :, :, :]
                link(pool.affine_select(out=step, in_=step, compare_op=ALU.is_ge, fill=0.0, base=0,
                                        pattern=[[0, 2], [0, T], [1, P]], channel_multiplier=-BLOCK))
                link(pool.affine_select(out=step, in_=step, compare_op=ALU.is_ge, fill=0.0, base=BLOCK - 1,
                                        pattern=[[0, 2], [0, T], [-1, P]], channel_multiplier=BLOCK))
                rows = cr[q][0:STEP0, :, :, :]
                for s in range(3):
                    last_one = pool.affine_select(out=rows, in_=rows, compare_op=ALU.not_equal, fill=-1.0, base=-T * s,
                                                  pattern=[[0, 2], [-1, T], [0, P]], channel_multiplier=1)
                    if s < 2:
                        link(last_one)
                last_one.then_inc(const_done, 1)

            def prepare(m, q):
                c0 = 2 * HD * (m - 1)
                pool.tensor_copy(xp[q][:].rearrange("p t j d -> p t (j d)"), xtok[:, :, bass.ds(c0, 2 * HD)])
                pool.tensor_copy(xs[q][:], xsd[:, :, bass.ds(c0, 2 * HD)]).then_inc(xp_done, 1)

            def by_head(ap):
                return ap.rearrange("p (h d) -> p h d", h=NH)

            pool.wait_ge(x_read, 4)
            pool.wait_ge(cexp_done, 2)
            for b in range(NSEQ):
                ins = pool.tensor_tensor(by_head(xsd[:, b, :]), by_head(xtok[:, 2 * b, :]),
                                         sdec[:, b, :].unsqueeze(2).to_broadcast([P, NH, HD]), ALU.mult)
            link(ins)
            prepare(1, 1)
            pool.wait_ge(small_in, 12 * 16)
            for t in range(T):
                ins = pool.tensor_tensor(by_head(y[:, t, :]), by_head(xtok[:, t, :]),
                                         db[:].unsqueeze(2).to_broadcast([P, NH, HD]), ALU.mult)
            ins.then_inc(y_init, 1)

            def body(n, k, q):
                for u in range(4):
                    pool.wait_ge(g_done, 4 * (n - 1) + u + 1)
                    g_v = g[u % 2][:].rearrange("p (i k) -> p i k", k=P)
                    pool.tensor_tensor(g_v, g_v, causal[:].unsqueeze(1).to_broadcast([P, 4, P]),
                                       ALU.mult).then_inc(masked, 1)
                    if isinstance(n, int) and n == 1:
                        pool.wait_ge(za_read, 2 * T)
                        t = slice(2 * u, 2 * u + 2)
                        pool.tensor_tensor(z[:, t, :], z[:, t, :], zb[:].unsqueeze(1).to_broadcast([P, 2, DM]),
                                           ALU.add).then_inc(z_ready, 1)
                    if isinstance(n, int) and PAIRS - 2 <= n < PAIRS and 1 <= 4 * (n - PAIRS + 2) + u <= 4:
                        v = (u - 1) % 4
                        for t in (2 * v, 2 * v + 1):
                            pool.wait_ge(zgate_done, t + 1)
                            pool.tensor_tensor(z[:, t, :], z[:, t, :], zgate(t), ALU.mult).then_inc(z_gated, 1)
                    if u == 1 and not last(n, 1):
                        at_least(pool, y_done, 4 * (n - 1))
                        prepare(n + 1, 1 - q)
                if isinstance(n, int) and n == PAIRS:
                    pool.wait_ge(sig_done, T)
                    pool.tensor_scalar(sig[:], sig[:], P_SEM / 2, P_SEM / 2, ALU.mult, ALU.add).then_inc(sig_scaled, 1)

            over_pairs(pool, body)

            def expert(e, k, q):
                if isinstance(e, int) and e == 0:
                    pool.wait_ge(misc_read, 2)
                pool.tensor_copy(eb[q][:], b_cols[:, bass.ds(e, 1), :, :].rearrange("p e a k -> p (e a) k")).then_inc(eb_done, 1)
                for v in range(4):
                    pool.wait_ge(uh_done, 4 * e + v + 1)
                    pool.tensor_tensor(ul[:, v, :], u32[:, v, :], f32(uh[:, v, :]),
                                       ALU.subtract).then_inc(ul_done, 1)
                for v in ((0, 2) if isinstance(e, int) and e == NE - 1 else range(4)):
                    pool.wait_ge(eh_done, 4 * e + v + 1)
                    pool.tensor_tensor(el[:, v, :], e32[:, v, :], f32(eh[:, v, :]),
                                       ALU.subtract).then_inc(el_done, 1)

            over_experts(pool, expert)

        @block.scalar
        def _(act):
            steps = [0]

            def link(ins):
                steps[0] += 1
                ins.then_inc(act_chain, 1)
                act.wait_ge(act_chain, steps[0])

            def split_turned(i, b):
                h, k = i % 4 // 2, i % 2
                act.wait_ge(ut_turned, i + 1)
                act.copy(uth[:, k, HALF * h:HALF * (h + 1)], bank[b][:]).then_inc(uth_done, 1)

            def split_w(m, q):
                act.wait_ge(w_turned, m + 1)
                at_least(act, proj_done, 4 * (m - 1))
                act.copy(parts[:, q, :], bank[6][:]).then_inc(wth_done, 1)

            def first_tap(m, k, q, u):
                act.wait_ge(proj_done, 4 * m + u + 1)
                if u == 0:
                    act.wait_ge(taps_in[q], 48 * (k + 1))
                j, h = u // 2, u % 2
                act.activation(conv[q][:, j, HALF * h:HALF * (h + 1)], bank[u % 2][:], ACT.Identity,
                               bias=tap_b[q][:, j:j + 1], scale=taps[q][:, j, TAPS - 1:TAPS]).then_inc(acc_first, 1)

            def normalise(c, tiles, rounds):
                act.wait_ge(norm_done, rounds)
                for i, t in enumerate(tiles):
                    act.activation(xn[:, t, :], xres[:, t, :], ACT.Identity, bias=nt1[:, c + i:c + i + 1],
                                   scale=rstd[:, c + i:c + i + 1]).then_inc(xn2_done, 1)

            def evacuate_za(t):
                act.wait_ge(za_done, t + 1)
                b = bank[2 + t % 4]
                act.copy(a_log[:, t, :], b[:, DM:ZA]).then_inc(za_read, 1)
                act.copy(z[:, t, :], b[:, 0:DM]).then_inc(za_read, 1)

            split_w(0, 0)
            for k in range(KD):
                act.wait_ge(wz_turned, k + 1)
                act.copy(wzh[:, k, :], bank[4 + k][:, 0:ZA]).then_inc(wzh_done, 1)
            normalise(4, range(4, 8), 1)
            for i in range(4):
                split_turned(i, i)
            split_w(1, 1)
            first_tap(0, 0, 0, 0)
            first_tap(0, 0, 0, 1)
            for t in range(4):
                evacuate_za(t)
            first_tap(0, 0, 0, 2)
            for t in range(4, 8):
                evacuate_za(t)
            act.wait_ge(nabs_done, 1)
            link(act.activation(neg_abs[:], neg_abs[:], ACT.Exp))
            first_tap(0, 0, 0, 3)
            act.activation(neg_abs[:], neg_abs[:], ACT.Ln, bias=1.0).then_inc(sp_done, 1)
            for i in range(2):
                act.wait_ge(ctx_turned, i + 1)
                act.copy(ctxT[:, HALF * i:HALF * (i + 1)], bank[(4, 7)[i]][0:CTX, :]).then_inc(ctx_read, 1)
            first_tap(1, 0, 1, 0)
            for i in range(2):
                act.wait_ge(x_turned, i + 1)
                act.copy(xtok[:, 2 * i:2 * i + 2, :].rearrange("p t d -> p (t d)"), bank[2 + i % 2][:]).then_inc(x_read, 1)
            act.wait_ge(misc_turned, 1)
            act.copy(b_cols[:].rearrange("p e a k -> p k a e"),
                     bank[6][:, 0:KD * 2 * NE].rearrange("p (k a e) -> p k a e", k=KD, a=2)).then_inc(misc_read, 1)
            first_tap(1, 0, 1, 1)
            for i in range(2, 4):
                act.wait_ge(x_turned, i + 1)
                act.copy(xtok[:, 2 * i:2 * i + 2, :].rearrange("p t d -> p (t d)"), bank[2 + i % 2][:]).then_inc(x_read, 1)
            first_tap(1, 0, 1, 2)
            act.wait_ge(cum_read, 1)
            act.activation(ecum[:], cum[:].rearrange("p h (b c) -> p b c h", c=2)[:, :, 1, :], ACT.Exp).then_inc(cexp_done, 1)
            act.activation(sdec[:], sdec[:], ACT.Exp).then_inc(cexp_done, 1)
            for i in range(2):
                act.wait_ge(pair_done, i + 1)
                act.copy(sig[:].rearrange("p (b c) d -> p b c d", c=2)[:, 2 * i:2 * i + 2, 0, :],
                         bank[2 + i][:].rearrange("p (b d) -> p b d", b=2)).then_inc(pair_read, 1)
            act.wait_ge(pair_done, 3)
            link(act.activation(si[:], bank[6][:, 0:T], ACT.Identity, bias=xbb[:, 0:1]))
            act.activation(si[:], si[:], ACT.Identity, scale=0.5).then_inc(pair_read, 1)
            first_tap(1, 0, 1, 3)
            split_w(2, 0)
            act.wait_ge(misc_turned, 2)
            act.copy(woT[:].rearrange("p k d -> p (k d)"), bank[5][:]).then_inc(misc_read, 1)

            def gate_of_z(u):
                act.wait_ge(z_ready, 4)
                for t in (2 * u, 2 * u + 1):
                    act.activation(zgate(t), z[:, t, :], ACT.Tanh, scale=0.5).then_inc(ztanh_done, 1)
                for t in (2 * u, 2 * u + 1):
                    act.wait_ge(ztanh_done, t + 1)
                    act.activation(zgate(t), zgate(t), ACT.Copy, bias=0.5, scale=0.5).then_inc(zgate_done, 1)

            def pairwise(u):
                act.wait_ge(pair_read, 3)
                for t in ((1, 3), (5, 7), (0, 2), (4, 6))[u]:
                    if t == 0:
                        act.wait_ge(sig_done, 4)
                    act.activation(sig[:, t, :], sig[:, t - t % 2, :], ACT.Tanh, scale=0.5,
                                   bias=si[:, t:t + 1]).then_inc(sig_done, 1)

            def copy_yz(k, half):
                act.wait_ge(yz_turned, 2 * k + half + 1)
                act.copy(yzT[:, k, HALF * half:HALF * (half + 1)], bank[(1, 7 - half)[k]][:]).then_inc(yz_read, 1)

            def decays(n, u):
                a, b = 4 * (n - 1) + u, u % 2
                act.wait_ge(expo_done, a + 1)
                at_least(act, g_done, a - 1)
                act.activation(dec[b][:], bank[4 + b][:], ACT.Exp).then_inc(exp_done, 1)

            def copy_b(n):
                act.wait_ge(b_turned, n)
                at_least(act, st_done, n - 1)
                act.copy(btok[:].rearrange("p b k -> p (b k)"), bank[6][:]).then_inc(b_read, 1)

            def copy_state(n):
                act.wait_ge(st_done, n)
                at_least(act, inter_done, n - 1)
                s_v = bank[6][:, 0:NSEQ * 2 * HD].rearrange("p (b j d) -> p b j d", b=NSEQ, j=2)
                for j in range(2):
                    r = slice(NS * j, NS * (j + 1))
                    act.copy(state[r, :, j, :], s_v[r, :, j, :]).then_inc(st_read, 1)

            def split_weights(e, q, j):
                act.copy(ewh[q][:, j, :, :].rearrange("p k d -> p (k d)"), ew_raw[q][:, j, :]).then_inc(ewh_done, 1)

            def body(n, k, q):
                if isinstance(n, int) and n == PAIRS:
                    last_pair(n)
                    return
                for u in range(4):
                    decays(n, u)
                    if u == 0:
                        at_least(act, inter_done, n - 1)
                    first_tap(n + 1, k + (q + 1) // 2, 1 - q, u)
                    if u == 0:
                        copy_b(n)
                    if u == 1:
                        copy_state(n)
                    if u == 2 and not last(n, 2):
                        split_w(n + 2, q)
                    if isinstance(n, int) and n == PAIRS - 2:
                        gate_of_z(u)
                    if isinstance(n, int) and n == PAIRS - 1:
                        pairwise(u)

            def last_pair(n):
                decays(n, 0)
                copy_b(n)
                decays(n, 1)
                copy_yz(0, 0)
                decays(n, 2)
                act.wait_ge(ew_in[0], 48)
                split_weights(0, 0, 0)
                copy_state(n)
                decays(n, 3)
                copy_yz(0, 1)
                split_weights(0, 0, 1)
                split_weights(0, 0, 2)

            over_pairs(act, body)

            copy_yz(1, 0)
            copy_yz(1, 1)
            normalise(T, range(2), 3)
            split_turned(4, 4)
            split_turned(5, 5)
            normalise(12, range(4, 6), 4)

            def copy_logits(i):
                act.wait_ge(lg_done, i + 1)
                act.copy(lgT[:, HALF * i:HALF * (i + 1)], bank[4 + i][0:NE, :]).then_inc(lgT_read, 1)

            def expert(e, k, q):
                first = isinstance(e, int) and e == 0
                act.wait_ge(eb_done, e + 1)
                for v in range(4):
                    if first and v == 2:
                        split_turned(6, 6)
                        split_turned(7, 7)
                    if first and v % 2 == 0:
                        copy_logits(v // 2)
                    act.wait_ge(up_done, 4 * e + v + 1)
                    at_least(act, e_done, 4 * (e - 1) + v + 1)
                    act.activation(u32[:, v, :], bank[v][:], ACT.Identity,
                                   bias=eb[q][:, 0, v % 2:v % 2 + 1]).then_inc(up_read, 1)
                    if first:
                        act.wait_ge(up_read, v + 1)
                        act.copy(uh[:, v, :], u32[:, v, :]).then_inc(uh_done, 1)
                if first:
                    act.wait_ge(pexp_in, 1)
                    act.activation(lg[:], lg[:], ACT.Exp).then_inc(pexp_done, 1)
                if not (isinstance(e, int) and e == NE - 1):
                    at_least(act, down_done, 4 * e)
                    act.wait_ge(ew_in[1 - q], 48 * (k + q + 1))
                    for j in range(3):
                        split_weights(e + 1, 1 - q, j)

                def round_e(v):
                    act.wait_ge(e_done, 4 * e + v + 1)
                    at_least(act, down_done, 4 * e)
                    act.copy(eh[:, v, :], e32[:, v, :]).then_inc(eh_done, 1)

                for v in range(4):
                    act.wait_ge(gate2_done, 4 * e + v + 1)
                    at_least(act, el_done, 4 * (e - 1) + v + 1)
                    act.activation(e32[:, v, :], bank[v][:], ACT.Silu,
                                   bias=eb[q][:, 1, v % 2:v % 2 + 1]).then_inc(silu2_done, 1)
                    if v:
                        round_e(v - 1)
                    if first and v == 0:
                        for i in range(2):
                            act.wait_ge(prob_turned, i + 1)
                            act.copy(probT[:, HALF * i:HALF * (i + 1)], bank[4 + i][0:NE, :]).then_inc(prob_read, 1)
                round_e(3)

            over_experts(act, expert)

        @block.vector
        def _(dve):
            steps = [0]

            def link(ins):
                steps[0] += 1
                ins.then_inc(dve_chain, 1)
                dve.wait_ge(dve_chain, steps[0])

            def moments(first, tiles, tile):
                for i, t in enumerate(tiles):
                    ins = dve.bn_stats(stats[:, first + i, :], tile(t))
                link(ins)
                for i in range(len(tiles)):
                    ins = dve.bn_aggr(mv[:, first + i, :], stats[:, first + i, :])
                link(ins)

            def inverse_roots(s):
                link(dve.tensor_scalar(var[:, s], mv[:, s, 1], EPS, None, ALU.add))
                link(dve.tensor_scalar(bits[:, s], var[:, s].bitcast(I32), 1, None, ALU.logical_shift_right))
                link(dve.tensor_scalar(rstd[:, s].bitcast(I32), bits[:, s], -1, ROOT_GUESS, ALU.mult, ALU.add))
                h, e = nt0, nt1
                link(dve.scalar_tensor_tensor(out=h[:, s], in0=rstd[:, s], scalar=0.5, in1=var[:, s],
                                              op0=ALU.mult, op1=ALU.mult))
                for i in range(3):
                    link(dve.tensor_tensor(e[:, s], h[:, s], rstd[:, s], ALU.mult))
                    if i < 2:
                        dve.scalar_tensor_tensor(out=h[:, s], in0=e[:, s], scalar=1.5, in1=h[:, s],
                                                 op0=ALU.subtract, op1=ALU.mult)
                    link(dve.scalar_tensor_tensor(out=rstd[:, s], in0=e[:, s], scalar=1.5, in1=rstd[:, s],
                                                  op0=ALU.subtract, op1=ALU.mult))
                dve.scalar_tensor_tensor(out=nt1[:, s], in0=mv[:, s, 0], scalar=-1.0, in1=rstd[:, s],
                                         op0=ALU.mult, op1=ALU.mult).then_inc(norm_done, 1)

            def normalise(first, tiles):
                for i, t in enumerate(tiles):
                    c = first + i
                    dve.tensor_scalar(xn[:, t, :], xres[:, t, :], mv[:, c, 0:1], rstd[:, c:c + 1],
                                      ALU.subtract, ALU.mult).then_inc(xn_done, 1)

            def rest_turned(i, b):
                h, k = i % 4 // 2, i % 2
                s = slice(HALF * h, HALF * (h + 1))
                dve.wait_ge(uth_done, i + 1)
                dve.tensor_tensor(utl[:, k, s], bank[b][:], f32(uth[:, k, s]), ALU.subtract).then_inc(utl_done, 1)

            def rest_w(m, q):
                dve.wait_ge(wth_done, m + 1)
                dve.tensor_tensor(parts[:, 2 + q, :], bank[6][:],
                                  f32(parts[:, q, :]), ALU.subtract).then_inc(wtl_done, 1)

            def other_taps(m, q, u, ds=range(1, TAPS)):
                j, h = u // 2, u % 2
                src = bank[u % 2][:].rearrange("p (b l) -> p b l", b=2)
                dst = conv[q][:, j, HALF * h:HALF * (h + 1)].rearrange("p (b l) -> p b l", b=2)
                if ds[0] == 1:
                    dve.wait_ge(acc_first, 4 * m + u + 1)
                for d in ds:
                    if d > 1:
                        dve.wait_ge(tap_done, 3 * (4 * m + u) + d - 1)
                    dve.scalar_tensor_tensor(
                        out=dst[:, :, d:SEQ], in0=src[:, :, 0:SEQ - d], scalar=taps[q][:, j, TAPS - 1 - d:TAPS - d],
                        in1=dst[:, :, d:SEQ], op0=ALU.mult, op1=ALU.add).then_inc(tap_done, 1)

            def from_x(t):
                dve.wait_ge(x_in[t // 4], 16)
                return xres[:, t, :]

            moments(0, range(T), from_x)
            inverse_roots(slice(0, T))
            normalise(0, range(4))
            rest_w(0, 0)
            rest_turned(0, 0)
            rest_turned(1, 1)
            for k in range(KD):
                dve.wait_ge(wzh_done, k + 1)
                dve.tensor_tensor(wzl[:, k, :], bank[4 + k][:, 0:ZA], f32(wzh[:, k, :]), ALU.subtract).then_inc(wzl_done, 1)
            rest_turned(2, 2)
            rest_turned(3, 3)
            other_taps(0, 0, 0)
            rest_w(1, 1)
            other_taps(0, 0, 1)
            other_taps(0, 0, 2)
            dve.wait_ge(za_read, 2 * T)
            dve.scalar_tensor_tensor(out=neg_abs[:], in0=a_log[:], scalar=-1.0, in1=a_log[:],
                                     op0=ALU.mult, op1=ALU.min).then_inc(nabs_done, 1)
            other_taps(0, 0, 3)
            dve.wait_ge(sp_done, 1)
            dve.scalar_tensor_tensor(out=dts[:].rearrange("p h t -> p t h"), in0=a_log[:], scalar=0.0, in1=neg_abs[:],
                                     op0=ALU.max, op1=ALU.add).then_inc(dt_done, 1)
            dve.wait_ge(ctx_sm_in, 32)
            dve.tensor_copy(wj_rep[:], wi_wj[:, 1:2].to_broadcast([CTX, P])).then_inc(wj_done, 1)
            other_taps(1, 1, 0)
            dve.wait_ge(cumT_done, 1)
            c_ps = bank[4][:, 0:2 * P].rearrange("p (c k) -> p c k", c=2)
            link(dve.tensor_copy(cpartsT[:, 0, :, :], c_ps))
            link(dve.tensor_tensor(cumT[:], c_ps, cpartsT[:, 0, :, :], ALU.subtract))
            link(dve.tensor_copy(cpartsT[:, 1, :, :], cumT[:]))
            link(dve.tensor_tensor(cumT[:], cumT[:], cpartsT[:, 1, :, :], ALU.subtract))
            dve.tensor_copy(cpartsT[:, 2, :, :], cumT[:]).then_inc(cpart_done, 1)
            other_taps(1, 1, 1)
            dve.wait_ge(cum_done, 1)
            link(dve.tensor_copy(cum[:], bank[7][:, 0:T * NH].rearrange("p (h t) -> p h t", t=T)))
            tot = bank[7][:, T * NH:2 * T * NH].rearrange("p (h b c) -> p b c h", c=2, h=NH)
            dve.tensor_tensor(sdec[:], tot[:, :, 0, :], cum[:].rearrange("p h (b c) -> p b c h", c=2)[:, :, 0, :],
                              ALU.subtract).then_inc(cum_read, 1)
            other_taps(1, 1, 2)
            other_taps(1, 1, 3)
            rest_w(2, 0)

            def read_y(n, half=None):
                first, b0, nb = 3 * (n - 1), 0, NSEQ
                if half is None:
                    dve.wait_ge(y_done, 4 * n)
                    dve.wait_ge(inter_done, n)
                else:
                    dve.wait_ge(y_done, 4 * (n - 1) + 2 * (half + 1))
                    dve.wait_ge(inter_done, n + half)
                    first, b0, nb = first + 3 * half, 2 * half, NSEQ // 2
                b = slice(b0, b0 + nb)
                src = y_bank(n, half)
                states = src[:, 2 * HD * (T + b0):2 * HD * (T + b0 + nb)]
                dve.tensor_tensor(yint[:, b], states.rearrange("p (b j d) -> p b j d", b=nb, j=2),
                                  ecum[:, b, bass.ds(2 * (n - 1), 2)].unsqueeze(3).to_broadcast([P, nb, 2, HD]),
                                  ALU.mult).then_inc(y_step, 1)
                c0 = 2 * HD * (n - 1)
                dst = y[:, 2 * b0:2 * (b0 + nb), bass.ds(c0, 2 * HD)]
                dve.tensor_tensor(dst, src[:, 4 * b0 * HD:4 * (b0 + nb) * HD].rearrange("p (t d) -> p t d", t=2 * nb), dst,
                                  ALU.add).then_inc(y_step, 1)
                odd = y[:].rearrange("p (b c) d -> p b c d", c=2)[:, b, 1, bass.ds(c0, 2 * HD)]
                dve.wait_ge(y_step, first + 2)
                dve.tensor_tensor(odd, odd, yint[:, b].rearrange("p b j d -> p b (j d)"), ALU.add).then_inc(y_step, 1)

            def gate_y(k, half):
                if half == 0:
                    dve.wait_ge(z_gated, T)
                s, c = slice(4 * half, 4 * half + 4), slice(P * k, P * (k + 1))
                dve.tensor_tensor(y[:, s, c], y[:, s, c], z[:, s, c], ALU.mult).then_inc(yz_done, 1)

            def split_router():
                dve.wait_ge(small_in, 12 * 16)
                dve.memset(f32(wrh[:]), 0.0)
                link(dve.memset(f32(wrl[:]), 0.0))
                link(dve.tensor_copy(wrh[:, :, 0:NR], wr_raw[:, :, 0:NR]))
                dve.tensor_tensor(wrl[:, :, 0:NR], wr_raw[:, :, 0:NR], f32(wrh[:, :, 0:NR]),
                                  ALU.subtract).then_inc(wr_done, 1)

            def rest_weights(e, q, j):
                dve.wait_ge(ewh_done, 3 * e + j + 1)
                dve.tensor_tensor(ewl[q][:, j, :, :].rearrange("p k d -> p (k d)"), ew_raw[q][:, j, :],
                                  f32(ewh[q][:, j, :, :].rearrange("p k d -> p (k d)")), ALU.subtract).then_inc(ewl_done, 1)

            def body(n, k, q):
                for u in range(4):
                    a, b = 4 * (n - 1) + u, u % 2
                    dve.wait_ge(exp_done, a + 1)
                    dve.wait_ge(cb_done, a + 1)
                    at_least(dve, y_done, a - 1)
                    dve.scalar_tensor_tensor(out=g[b][:], in0=dec[b][:], scalar=1.0, in1=bank[2 + b][:],
                                             op0=ALU.min, op1=ALU.mult).then_inc(g_done, 1)
                    if u == 0:
                        if not (isinstance(n, int) and n == 1):
                            other_taps(n, q, 3, (TAPS - 1,))
                            read_y(n - 1)
                    elif not last(n, 1):
                        other_taps(n + 1, 1 - q, u - 1, (TAPS - 1,))
                    if not last(n, 1):
                        other_taps(n + 1, 1 - q, u, range(1, TAPS - 1))
                    if u == 2 and not last(n, 2):
                        rest_w(n + 2, q)
                    if isinstance(n, int) and n == PAIRS - 1 and u == 2:
                        gate_y(0, 0)
                    if isinstance(n, int) and n == PAIRS:
                        if u == 0:
                            gate_y(0, 1)
                        if u == 1:
                            split_router()
                        if u == 2:
                            rest_weights(0, 0, 0)
                            read_y(PAIRS, 0)
                            dve.wait_ge(y_step, 3 * PAIRS)
                            gate_y(1, 0)
                if isinstance(n, int) and n == 1:
                    dve.wait_ge(y_init, 1)

            over_pairs(dve, body)

            def from_projection(t):
                dve.wait_ge(o_done, t // 2 + 1)
                return bank[t // 2][:, DM * (t % 2):DM * (t % 2 + 1)]

            def from_residual(t):
                dve.wait_ge(o_read, t + 1)
                return xres[:, t, :]

            def second_block(tiles):
                s = slice(tiles[0], tiles[-1] + 1)
                dve.wait_ge(norm_done, 2 + tiles[0] // 4)
                link(dve.tensor_scalar(nt0[:, s], rstd[:, s], 1 - P_SEM, 1.0, ALU.mult, ALU.add))
                link(dve.tensor_scalar(shift[:, s], nt1[:, s], 1 - P_SEM, None, ALU.mult))
                for t in tiles:
                    dve.scalar_tensor_tensor(out=xres[:, t, :], in0=from_projection(t), scalar=nt0[:, t:t + 1],
                                             in1=sig[:, t, :], op0=ALU.mult, op1=ALU.add).then_inc(o_read, 1)

            moments(0, range(4), from_projection)
            read_y(PAIRS, 1)
            dve.wait_ge(y_step, 3 * PAIRS + 3)
            gate_y(1, 1)
            inverse_roots(slice(0, 4))
            dve.wait_ge(sig_scaled, 1)
            second_block(range(4))
            moments(T, range(4), from_residual)
            moments(4, range(4, 8), from_projection)
            inverse_roots(slice(4, 12))
            normalise(10, range(2, 4))
            second_block(range(4, 8))
            moments(12, range(4, 8), from_residual)
            rest_turned(4, 4)
            rest_turned(5, 5)
            inverse_roots(slice(12, 16))
            normalise(14, range(6, 8))
            rest_weights(0, 0, 1)
            rest_turned(6, 6)
            rest_turned(7, 7)
            rest_weights(0, 0, 2)

            def route():
                dve.wait_ge(gate_done, 1)
                dve.wait_ge(const_done, 2)
                link(dve.tensor_tensor(lg[:], bank[6][:, 0:T * 8].rearrange("p (t e) -> p t e", t=T)[:, :, 0:NR],
                                       brb[:, 0:1, :].to_broadcast([P, T, NR]), ALU.add))
                link(dve.tensor_tensor(bg[:], lg[:], brb[:, 1:2, :].to_broadcast([P, T, NR]), ALU.add))
                me = bg[:].unsqueeze(3).to_broadcast([P, T, NR, NR])
                other = bg[:].unsqueeze(2).to_broadcast([P, T, NR, NR])
                dve.tensor_tensor(gt[:], other, me, ALU.is_gt)
                link(dve.tensor_tensor(ge[:], other, me, ALU.is_ge))
                link(dve.tensor_tensor(ge[:].rearrange("p t a b -> p t (a b)"), ge[:].rearrange("p t a b -> p t (a b)"),
                                       earlier[:].rearrange("p a b -> p (a b)").unsqueeze(1).to_broadcast([P, T, NR * NR]),
                                       ALU.mult))
                link(dve.tensor_tensor(gt[:], gt[:], ge[:], ALU.max))
                link(dve.tensor_reduce(sel[:], gt[:], AX.X, ALU.add))
                link(dve.tensor_scalar(sel[:], sel[:], TOPK - 0.5, None, ALU.is_lt))
                link(dve.tensor_scalar(bg[:], sel[:], -NEG, NEG, ALU.mult, ALU.add))
                link(dve.tensor_tensor(lg[:], lg[:], sel[:], ALU.mult))
                link(dve.tensor_tensor(lg[:], lg[:], bg[:], ALU.add))
                link(dve.tensor_reduce(mx[:], lg[:], AX.X, ALU.max))
                dve.tensor_tensor(lg[:], lg[:], mx[:].unsqueeze(2).to_broadcast([P, T, NR]), ALU.subtract).then_inc(pexp_in, 1)
                dve.wait_ge(pexp_done, 1)
                link(dve.tensor_reduce(mx[:], lg[:], AX.X, ALU.add))
                link(dve.reciprocal(mx[:], mx[:]))
                dve.tensor_tensor(prob[:, :, 0:NR], lg[:], mx[:].unsqueeze(2).to_broadcast([P, T, NR]),
                                  ALU.mult).then_inc(prob_done, 1)

            def accumulate(e):
                for t in range(T):
                    dve.wait_ge(down_done, 4 * e + t // 2 + 1)
                    dve.scalar_tensor_tensor(out=xres[:, t, :], in0=bank[4 + t // 2][:, DM * (t % 2):DM * (t % 2 + 1)],
                                             scalar=prob[:, t, bass.ds(e, 1)], in1=xres[:, t, :],
                                             op0=ALU.mult, op1=ALU.add).then_inc(acc_done, 1)

            def expert(e, k, q):
                first, second, final = (isinstance(e, int) and e == i for i in (0, 1, NE - 1))
                if second:
                    for t in range(T):
                        dve.wait_ge(bdn_done, t // 2 + 1)
                        dve.scalar_tensor_tensor(out=xres[:, t, :], in0=bank[4 + t // 2][:, DM * (t % 2):DM * (t % 2 + 1)],
                                                 scalar=shift[:, t:t + 1], in1=xres[:, t, :],
                                                 op0=ALU.add, op1=ALU.add).then_inc(bdn_read, 1)
                    dve.wait_ge(bdn_read, T)
                for v in range(4 * (not first)):
                    dve.wait_ge(up_read, 4 * e + v + 1)
                    at_least(dve, gate2_done, 4 * e)
                    dve.tensor_copy(uh[:, v, :], u32[:, v, :]).then_inc(uh_done, 1)
                if first:
                    route()
                else:
                    accumulate(e - 1)
                if not final:
                    for j in range(3):
                        rest_weights(e + 1, 1 - q, j)
                for v in range(4):
                    dve.wait_ge(silu2_done, 4 * e + v + 1)
                    dve.tensor_tensor(e32[:, v, :], e32[:, v, :], u32[:, v, :], ALU.mult).then_inc(e_done, 1)
                    if final and v >= 2:
                        w = 2 * v - 3
                        dve.wait_ge(eh_done, 4 * e + w + 1)
                        dve.tensor_tensor(el[:, w, :], e32[:, w, :], f32(eh[:, w, :]), ALU.subtract).then_inc(el_last, 1)

            over_experts(dve, expert)
            dve.wait_ge(acc_done, T * (NE - 1))
            accumulate(NE - 1)

        @block.tensor
        def _(pe):
            def three(dst, passes, n):
                for k in range(n):
                    for i, (left, right) in enumerate(passes(k)):
                        ins = pe.matmul(dst, left, right, start=(k == 0 and i == 0), stop=(k == n - 1 and i == 2))
                return ins

            def turn_w(m, k, q, waits):
                pe.wait_ge(w_in[q], 16 * (k + 1))
                waits()
                for j in range(2):
                    for d in range(KD):
                        c = (2 * j + d) * P
                        ins = pe.transpose(bank[6][:, c:c + P], w_raw[q][:, j, d * P:(d + 1) * P], ident[:])
                ins.then_inc(w_turned, 1)

            def project_pass(m, q, u, i):
                j, h, k = u // 2, u % 2, i // 3
                if i == 0:
                    if u == 0:
                        pe.wait_ge(wtl_done, m + 1)
                    if isinstance(m, int) and m == 0 and u < 2:
                        pe.wait_ge(utl_done, 2 * u + 2)
                    at_least(pe, tap_done, 3 * (4 * m + u - 1))
                w = (wth, wth, wtl)[i % 3][q][:, j, k, :]
                x_t = (uth, utl, uth)[i % 3][:, k, HALF * h:HALF * (h + 1)]
                ins = pe.matmul(bank[u % 2][:], w, x_t, start=(i == 0), stop=(i == 3 * KD - 1))
                if i == 3 * KD - 1:
                    ins.then_inc(proj_done, 1)

            def project(m, q, u):
                for i in range(3 * KD):
                    project_pass(m, q, u, i)

            def turn_tokens(i, b):
                h, k = i % 4 // 2, i % 2
                if i < 4:
                    pe.wait_ge((xn_done, xn2_done)[h], 4)
                else:
                    pe.wait_ge(xn_done, 6 + 2 * h)
                    pe.wait_ge(xn2_done, 6 + 2 * h)
                for t in range(4):
                    ins = pe.transpose(bank[b][:, t * P:(t + 1) * P], xn[:, 4 * h + t, k * P:(k + 1) * P], ident[:])
                ins.then_inc(ut_turned, 1)

            def keep_warm(b, operand, count):
                for _ in range(count):
                    pe.matmul(bank[b][:, 0:operand.shape[1]], operand[:, 0:P], operand, start=True, stop=True)

            pe.wait_ge(const_done, 1)
            turn_w(0, 0, 0, lambda: None)
            pe.wait_ge(wz_in, 32)
            for k in range(KD):
                for j in range(2):
                    pe.transpose(bank[4 + k][:, j * P:(j + 1) * P], wz_rawz[:, j, k * P:(k + 1) * P], ident[:])
                pe.transpose(bank[4 + k][:, DM:ZA], wz_rawa[:, k * P:(k + 1) * P], ident[0:NH, 0:NH]).then_inc(wz_turned, 1)
            keep_warm(7, ident[:], 6)
            for i in range(4):
                turn_tokens(i, i)
            turn_w(1, 0, 1, lambda: pe.wait_ge(wtl_done, 1))
            def project_za(t):
                if t == 0:
                    pe.wait_ge(wzl_done, KD)
                    pe.wait_ge(utl_done, 4)
                at_least(pe, za_read, 2 * (t - 3))
                s = slice(t * P, (t + 1) * P)
                three(bank[2 + t % 4][:, 0:ZA], lambda k: [(uth[:, k, s], wzh[:, k, :]), (uth[:, k, s], wzl[:, k, :]),
                                                           (utl[:, k, s], wzh[:, k, :])], KD).then_inc(za_done, 1)

            project(0, 0, 0)
            project(0, 0, 1)
            for t in range(4):
                project_za(t)
            project(0, 0, 2)
            for t in range(4, 8):
                project_za(t)
            project(0, 0, 3)
            project(1, 1, 0)
            pe.wait_ge(small_in, 12 * 16)
            for k in range(KD):
                ins = pe.transpose(bank[6][:, k * 2 * NE:(k + 1) * 2 * NE], b_rows[:, k * P:(k + 1) * P], ident[0:2 * NE, 0:2 * NE])
            ins.then_inc(misc_turned, 1)
            pe.wait_ge(wo_in, 16)
            pe.wait_ge(za_read, 2 * T)
            for k in range(KD):
                for j in range(2):
                    c = (2 * k + j) * P
                    ins = pe.transpose(bank[5][:, c:c + P], wo_raw[:, j, k * P:(k + 1) * P], ident[:])
            ins.then_inc(misc_turned, 1)
            pe.wait_ge(ctx_sm_in, 32)
            for i in range(2):
                for t in range(4):
                    ins = pe.transpose(bank[(4, 7)[i]][0:CTX, t * P:(t + 1) * P], ctx_raw[:, 4 * i + t, :], ident[:])
                ins.then_inc(ctx_turned, 1)

            def turn_x(i):
                at_least(pe, x_read, i - 1)
                for t in range(2):
                    for c in range(2):
                        col = (2 * t + c) * P
                        ins = pe.transpose(bank[2 + i % 2][:, col:col + P],
                                           conv[0][:, c, (2 * i + t) * P:(2 * i + t + 1) * P], ident[:])
                ins.then_inc(x_turned, 1)

            pe.wait_ge(tap_done, 12)
            turn_x(0)
            turn_x(1)
            pe.wait_ge(dt_done, 1)
            pe.wait_ge(const_done, 2)
            pe.wait_ge(ctx_read, 2)
            for c in range(2):
                ins = pe.matmul(bank[4][:, c * P:(c + 1) * P], dts[:, 16 * c:16 * c + 16, :].rearrange("p h t -> p (h t)"),
                                neg_tri[:], start=True, stop=True)
            ins.then_inc(cumT_done, 1)
            project(1, 1, 1)
            turn_x(2)
            turn_x(3)
            pe.matmul(bank[7][:, 0:T * NH], neg_tri[:], dts[:].rearrange("p h t -> p (h t)"), start=True, stop=True)
            pe.matmul(bank[7][:, T * NH:2 * T * NH], neg_ones[:], dts[:].rearrange("p h t -> p (h t)"),
                      start=True, stop=True).then_inc(cum_done, 1)
            project(1, 1, 2)
            pe.wait_ge(x_read, 4)
            pe.wait_ge(misc_read, 1)
            pe.wait_ge(wj_done, 1)
            for i in range(2):
                pe.matmul(bank[2 + i][:], wj_rep[:], ctxT[:, HALF * i:HALF * (i + 1)], start=True, stop=True).then_inc(pair_done, 1)
            for t in range(T):
                ins = pe.matmul(bank[6][:, t:t + 1], ctxT[:, t * P:(t + 1) * P], wi_wj[:, 0:1], start=True, stop=True)
            ins.then_inc(pair_done, 1)
            project(1, 1, 3)
            turn_w(2, 1, 0, lambda: pe.wait_ge(pair_read, 3))
            keep_warm(3, uth[:, 0, 0:HALF], 8)
            pe.wait_ge(cpart_done, 1)
            pe.wait_ge(misc_read, 2)
            pe.wait_ge(cum_read, 1)

            def weigh(n, q, u, i):
                a = 4 * (n - 1) + u
                j, h, b = *head_half(n, u), u % 2
                if i == 0:
                    pe.wait_ge(masked, a + 1)
                    if u == 0:
                        pe.wait_ge(xp_done, n)
                        at_least(pe, y_step, 3 * (n - 1) - 1)
                t = 4 * h + i
                c = (2 * t + j) * HD
                ins = pe.matmul(y_bank(n, h)[:, c:c + HD], g[b][:, i * P:(i + 1) * P], xp[q][:, t, j, :],
                                start=True, stop=True)
                if i == 3:
                    ins.then_inc(y_done, 1)

            def new_state(n, q, i):
                if i == 0:
                    pe.wait_ge(b_read, n)
                    pe.wait_ge(xp_done, n)
                ins = pe.matmul(bank[6][:, i * 2 * HD:(i + 1) * 2 * HD], btok[:, i, :], xs[q][:, i, :],
                                start=True, stop=True)
                if i == NSEQ - 1:
                    ins.then_inc(st_done, 1)

            def from_state(n, q, i):
                if i == 0:
                    pe.wait_ge(st_read, 2 * n)
                c = 2 * T * HD + i * 2 * HD
                ins = pe.matmul(y_bank(n, i // 2)[:, c:c + 2 * HD], conv[q][:, 1, (2 * i + 1) * P:(2 * i + 2) * P],
                                state[:, i, :, :].rearrange("p j d -> p (j d)"), start=True, stop=True)
                if i == NSEQ - 1 or (isinstance(n, int) and n == PAIRS and i == NSEQ // 2 - 1):
                    ins.then_inc(inter_done, 1)

            def weigh_before(n, q, u, tiles):
                for i in tiles:
                    if u == 2:
                        weigh(n, q, 1, i)
                    elif not (isinstance(n, int) and n == 1):
                        weigh(n - 1, 1 - q, 3, i)

            def turn_yz(k, half):
                pe.wait_ge(yz_done, 2 * k + half + 1)
                if half and not k:
                    pe.wait_ge(yz_read, 1)
                for t in range(4):
                    ins = pe.transpose(bank[(1, 7 - half)[k]][:, t * P:(t + 1) * P],
                                       y[:, 4 * half + t, k * P:(k + 1) * P], ident[:])
                ins.then_inc(yz_turned, 1)

            def residual(t):
                if t == 2:
                    pe.wait_ge(yz_read, 2)
                pe.matmul(bank[t // 2][:, DM * (t % 2):DM * (t % 2 + 1)], ident[:], xres[:, t, :],
                          start=(t % 2 == 0), stop=False)

            def onto_o(k, t):
                pe.wait_ge(yz_read, 2 * k + t // 4 + 1)
                ins = pe.matmul(bank[t // 2][:, DM * (t % 2):DM * (t % 2 + 1)], yzT[:, k, t * P:(t + 1) * P], woT[:, k, :],
                                start=False, stop=(k == KD - 1 and t % 2 == 1))
                if k == KD - 1 and t % 2:
                    ins.then_inc(o_done, 1)

            def exponents(n, k, q, u):
                j, h, b = *head_half(n, u), u % 2
                if u == 0:
                    pe.wait_ge(cum_in[q], 64 * (k + q))
                at_least(pe, exp_done, 4 * (n - 1) + u - 1)
                pe.matmul(bank[4 + b][:], cl[q][:, j, :], cr[q][:, j, 4 * h:4 * h + 4, :].rearrange("p t k -> p (t k)"),
                          start=True, stop=True).then_inc(expo_done, 1)

            def b_dot_c(n, q, u):
                j, h, b = *head_half(n, u), u % 2
                if j == 0:
                    pe.wait_ge(tap_done, 12 * n + (9, 12)[h])
                at_least(pe, g_done, 4 * (n - 1) + u - 1)
                r = slice(NS * j, NS * (j + 1))
                for i in range(4):
                    s = slice((4 * h + i) * P, (4 * h + i + 1) * P)
                    ins = pe.matmul(bank[2 + b][:, i * P:(i + 1) * P], conv[q][r, 0, s], conv[q][r, 1, s],
                                    start=True, stop=True)
                ins.then_inc(cb_done, 1)

            def turn_b(n, q):
                pe.wait_ge(wtl_done, min(n + 2, PAIRS + 1) if isinstance(n, int) else n + 2)
                for i in range(NSEQ):
                    ins = pe.transpose(bank[6][:, i * P:(i + 1) * P], conv[q][:, 0, 2 * i * P:(2 * i + 1) * P], ident[:])
                ins.then_inc(b_turned, 1)

            def body(n, k, q):
                if isinstance(n, int) and n == PAIRS:
                    last_pair(n, k, q)
                    return
                for u in range(4):
                    exponents(n, k, q, u)
                    if u == 1:
                        project_pass(n + 1, 1 - q, u, 0)
                    b_dot_c(n, q, u)
                    for i in range(3 * KD):
                        if u % 2 == 0 and i == 0:
                            weigh_before(n, q, u, (0, 1))
                        if not (u == 1 and i == 0):
                            project_pass(n + 1, 1 - q, u, i)
                        if u % 2 == 0 and i == 0:
                            weigh_before(n, q, u, (2, 3))
                        if i < 4 and u % 2:
                            weigh(n, q, u - 1, i)
                            if u == 1:
                                new_state(n, q, i)
                            else:
                                from_state(n, q, i)
                    if u == 0:
                        turn_b(n, q)
                    if u == 2:
                        pe.wait_ge(st_read, 2 * n)
                        if not last(n, 2):
                            turn_w(n + 2, k + 1, q, lambda: None)

            def last_pair(n, k, q):
                exponents(n, k, q, 0)
                b_dot_c(n, q, 0)
                weigh_before(n, q, 0, (0, 1))
                residual(0)
                weigh_before(n, q, 0, (2, 3))
                turn_b(n, q)
                exponents(n, k, q, 1)
                b_dot_c(n, q, 1)
                residual(1)
                pe.wait_ge(tap_done, 12 * n + 12)
                turn_yz(0, 0)
                exponents(n, k, q, 2)
                b_dot_c(n, q, 2)
                for i in range(4):
                    weigh(n, q, 0, i)
                    new_state(n, q, i)
                    if i % 2:
                        onto_o(0, i // 2)
                exponents(n, k, q, 3)
                turn_yz(0, 1)
                b_dot_c(n, q, 3)
                for i in range(4):
                    weigh(n, q, 1, i)
                    if i % 2:
                        from_state(n, q, i // 2)
                for t in (2, 3):
                    residual(t)
                for t in (2, 3):
                    onto_o(0, t)
                turn_yz(1, 0)
                for i in range(4):
                    weigh(n, q, 2, i)
                    if i % 2:
                        from_state(n, q, 2 + i // 2)
                residual(4)
                residual(5)
                for t in range(4):
                    onto_o(1, t)
                for i in range(4):
                    weigh(n, q, 3, i)

            over_pairs(pe, body)

            for t in (6, 7):
                residual(t)
            for t in (4, 5, 6, 7):
                onto_o(0, t)
            turn_yz(1, 1)
            for t in (4, 5, 6, 7):
                onto_o(1, t)
            up_weights = ewh[0][:, 0, :, :].rearrange("p k d -> p (k d)")
            pe.wait_ge(ewl_done, 1)
            keep_warm(7, up_weights, 34)
            turn_tokens(4, 4)
            turn_tokens(5, 5)
            keep_warm(7, up_weights, 12)

            def up(e, q, tiles=range(4)):
                pe.wait_ge(ewl_done, 3 * e + 1)
                for v in tiles:
                    n, m = v // 2, v % 2
                    s = slice(HALF * n, HALF * (n + 1))
                    c = slice(P * m, P * (m + 1))
                    at_least(pe, silu2_done, 4 * (e - 1) + v + 1)
                    if isinstance(e, int) and e == 0 and m == 0:
                        pe.wait_ge(utl_done, 6 + 2 * n)
                    three(bank[v][:], lambda k: [(ewh[q][:, 0, k, c], uth[:, k, s]), (ewh[q][:, 0, k, c], utl[:, k, s]),
                                                 (ewl[q][:, 0, k, c], uth[:, k, s])], KD).then_inc(up_done, 1)

            def gate(e, q, tiles=range(4)):
                pe.wait_ge(ewl_done, 3 * e + 2)
                for v in tiles:
                    n, m = v // 2, v % 2
                    c = slice(P * m, P * (m + 1))
                    pe.wait_ge(up_read, 4 * e + v + 1)
                    if m == 0:
                        pe.wait_ge(ul_done, 4 * e + 2 * n + 2)
                    three(bank[v][:], lambda k: [(ewh[q][:, 1, k, c], uh[:, 2 * n + k, :]),
                                                 (ewh[q][:, 1, k, c], ul[:, 2 * n + k, :]),
                                                 (ewl[q][:, 1, k, c], uh[:, 2 * n + k, :])], KD).then_inc(gate2_done, 1)

            def down(e, q):
                pe.wait_ge(ewl_done, 3 * e + 3)
                for t in range(T):
                    n = t // 4
                    if t % 4 == 0 and isinstance(e, int) and e == NE - 1:
                        pe.wait_ge(el_done, 4 * e + n + 1)
                        pe.wait_ge(el_last, n + 1)
                    elif t % 4 == 0:
                        pe.wait_ge(el_done, 4 * e + 2 * n + 2)
                    if t % 2 == 0:
                        if isinstance(e, int) and e == 0:
                            pe.wait_ge(bdn_read, t + 2)
                        at_least(pe, acc_done, T * (e - 1) + t + 2)
                    s = slice((t % 4) * P, (t % 4 + 1) * P)
                    ins = three(bank[4 + t // 2][:, DM * (t % 2):DM * (t % 2 + 1)],
                                lambda k: [(eh[:, 2 * n + k, s], ewh[q][:, 2, k, :]), (eh[:, 2 * n + k, s], ewl[q][:, 2, k, :]),
                                           (el[:, 2 * n + k, s], ewh[q][:, 2, k, :])], KD)
                    if t % 2:
                        ins.then_inc(down_done, 1)

            def logits(i):
                pe.wait_ge(wr_done, 1)
                pe.wait_ge(utl_done, 6 + 2 * i)
                s = slice(HALF * i, HALF * (i + 1))
                three(bank[4 + i][0:NE, :], lambda k: [(wrh[:, k, :], uth[:, k, s]), (wrh[:, k, :], utl[:, k, s]),
                                                       (wrl[:, k, :], uth[:, k, s])], KD).then_inc(lg_done, 1)

            def turn_logits():
                pe.wait_ge(lgT_read, 2)
                for t in range(T):
                    ins = pe.transpose(bank[6][:, t * 8:(t + 1) * 8], lgT[:, t * P:(t + 1) * P], ident[0:NE, 0:NE])
                ins.then_inc(gate_done, 1)

            def turn_prob():
                pe.wait_ge(prob_done, 1)
                for i in range(2):
                    for t in range(4):
                        ins = pe.transpose(bank[4 + i][0:NE, t * P:(t + 1) * P], prob[:, 4 * i + t, :], ident[:])
                    ins.then_inc(prob_turned, 1)

            def down_biases():
                pe.wait_ge(prob_read, 2)
                for i in range(4):
                    for t in range(2):
                        tt = 2 * i + t
                        ins = pe.matmul(bank[4 + i][:, DM * t:DM * (t + 1)], probT[:, tt * P:(tt + 1) * P], bd[:],
                                        start=True, stop=True)
                    ins.then_inc(bdn_done, 1)

            def expert(e, k, q):
                if isinstance(e, int) and e == 0:
                    logits(0)
                    up(0, 0, range(2))
                    turn_tokens(6, 6)
                    turn_tokens(7, 7)
                    keep_warm(5, up_weights, 12)
                    logits(1)
                    turn_logits()
                    up(0, 0, range(2, 4))
                    gate(0, 0, range(2))
                    turn_prob()
                    gate(0, 0, range(2, 4))
                    down_biases()
                else:
                    up(e, q)
                    down(e - 1, 1 - q)
                    gate(e, q)

            over_experts(pe, expert)
            down(NE - 1, 1)


_INS = ['x', 'ctx_512', 'L0_attn_W_in', 'L0_attn_conv_w', 'L0_attn_conv_b', 'L0_attn_D', 'L0_attn_z_bias',
        'L0_attn_W_out', 'L0_xattn_W', 'L0_xattn_b', 'L0_ffn_Wr', 'L0_ffn_br', 'L0_ffn_gate_bias', 'L0_ffn_Wup',
        'L0_ffn_bup', 'L0_ffn_Wgate', 'L0_ffn_bgate', 'L0_ffn_Wdown', 'L0_ffn_bdown', 'L0_ffn_Wsu', 'L0_ffn_bsu',
        'L0_ffn_Wsg', 'L0_ffn_bsg', 'L0_ffn_Wsd', 'L0_ffn_bsd']
_OUTS = [((NSEQ, SEQ, DM), 'float32')]


def kernel(**inputs):
    import numpy as _np
    import concourse.bacc as _bacc
    from concourse import mybir as _mybir
    from concourse.bass_utils import run_bass_kernel_spmd as _run

    nc = _bacc.Bacc("TRN2", target_bir_lowering=False, num_devices=1)
    arrays, args = {}, []
    for name in _INS:
        a = _np.ascontiguousarray(inputs[name])
        arrays[f"in_{name}_dram"] = a
        args.append(nc.dram_tensor(f"in_{name}_dram", a.shape, _mybir.dt.from_np(a.dtype), kind="ExternalInput").ap())
    for i, (shape, dtype) in enumerate(_OUTS):
        dt = _mybir.dt.from_np(_np.dtype(dtype))
        args.append(nc.dram_tensor(f"out_{i}_dram", shape, dt, kind="ExternalOutput").ap())
    decoder_layer(nc, *args)
    r = _run(nc, [arrays], core_ids=[0])
    got = tuple(r.results[0][f"out_{i}_dram"] for i in range(len(_OUTS)))
    return got[0]
```
